# Optimizing a Trainium2 kernel written in Bass

```python
import numpy as np
import jax
import jax.numpy as jnp

def _softmax(x, axis=-1):
    return jax.nn.softmax(x, axis=axis)

def _gelu(x):
    return jax.nn.gelu(x, approximate=True)

def _silu(x):
    return jax.nn.silu(x)

def _sigmoid(x):
    return jax.nn.sigmoid(x)

def _layernorm(x, axis=-1, eps=1e-05):
    m = jnp.mean(x, axis=axis, keepdims=True)
    v = jnp.var(x, axis=axis, keepdims=True)
    return (x - m) / jnp.sqrt(v + eps)

def _scatter_add(tgt, idx, src, axis=0):
    return tgt.at[idx].add(src)

def _segment_sum(src, seg, n):
    return jax.ops.segment_sum(src, seg, n)
kernel_name = 'mk_flamingo_gated_d4_seqx_r4_29f625'

def setup_inputs(seed: int=0):
    np.random.seed(seed)
    _w = jnp.asarray

    def _rec_inputs():
        import jax
        import jax.numpy as jnp
        _rk = jax.random.key(seed)
        x = -0.0002928 + 1 * jax.random.normal(jax.random.fold_in(_rk, 1), (16, 128, 256), jnp.float32)
        _lenS = 128 - jax.random.randint(jax.random.fold_in(_rk, 7), (16,), 0, max(1, 128 // 4) + 1, jnp.int32)
        _lenS2 = 128 - jax.random.randint(jax.random.fold_in(_rk, 8), (16,), 0, max(1, 128 // 4) + 1, jnp.int32)
        _ctx_1024P = jax.random.normal(jax.random.fold_in(_rk, 11), (16, 16, 256), jnp.float32)
        _ctx_1024c = jax.random.dirichlet(jax.random.fold_in(_rk, 511), 0.3 * jnp.ones((16,), jnp.float32), (16, 128))
        _ctx_1024t = jnp.einsum('bsk,bkd->bsd', _ctx_1024c, _ctx_1024P)
        _ctx_1024t = _ctx_1024t * jax.lax.rsqrt(jnp.mean(jnp.square(_ctx_1024t)) + 1e-12) * 0.953939
        ctx_1024 = -1.39393e-06 + 0.999914 * (_ctx_1024t + 0.3 * jax.random.normal(jax.random.fold_in(_rk, 611), (16, 128, 256), jnp.float32))
        _validS = jnp.arange(128)[None, :] < _lenS[:, None]
        _validS2 = jnp.arange(128)[None, :] < _lenS2[:, None]
        _causal = jnp.tril(jnp.ones((128, 128), dtype=bool))
        mask_Bx1xSxS2_ik1 = jnp.where(jnp.broadcast_to(_validS2[:, None, None, :], (16, 1, 128, 128)), 1, 0).astype(jnp.int32)
        _g = jax.random.normal(jax.random.fold_in(_rk, 9001), (2, 4), jnp.float32)
        _g = jnp.sign(_g) * jnp.maximum(jnp.abs(_g), 1.0) + (_g == 0) * 1.0
        g_xattn = _g[0]
        g_ffn = _g[1]
        return (x, ctx_1024, mask_Bx1xSxS2_ik1, g_xattn, g_ffn)
    x, ctx_1024, mask_Bx1xSxS2_ik1, g_xattn, g_ffn = _rec_inputs()

    def _L0_xattn_setup():
        import jax, jax.numpy as jnp
        import numpy as np
        D_MODEL = 256
        NUM_HEADS = 16
        D_K = D_MODEL // NUM_HEADS
        NEG_INF = -1000000000.0

        def _split_heads(x):
            B, S, _ = x.shape
            return x.reshape(B, S, NUM_HEADS, D_K).transpose(0, 2, 1, 3)
        key = jax.random.key(seed)
        ks = jax.random.split(key, 13)
        B, S = (2, 512)
        scale = 1.0 / np.sqrt(D_MODEL)
        inp = {'Query': jax.random.normal(ks[0], (B, S, D_MODEL), jnp.float32), 'Key': jax.random.normal(ks[1], (B, S, D_MODEL), jnp.float32), 'Values': jax.random.normal(ks[2], (B, S, D_MODEL), jnp.float32), 'Mask': jax.random.randint(ks[3], (B, 1, S, S), 0, 2, jnp.int32), 'W_q': jax.random.normal(ks[4], (D_MODEL, D_MODEL), jnp.float32) * scale, 'b_q': jnp.zeros((D_MODEL,), jnp.float32), 'W_k': jax.random.normal(ks[5], (D_MODEL, D_MODEL), jnp.float32) * scale, 'b_k': jnp.zeros((D_MODEL,), jnp.float32), 'W_v': jax.random.normal(ks[6], (D_MODEL, D_MODEL), jnp.float32) * scale, 'b_v': jnp.zeros((D_MODEL,), jnp.float32), 'W_o': jax.random.normal(ks[7], (D_MODEL, D_MODEL), jnp.float32) * scale, 'b_o': jnp.zeros((D_MODEL,), jnp.float32)}
        return inp
    _L0_xattn_all = _L0_xattn_setup()
    _L0_xattn_in = {k: v for k, v in _L0_xattn_all.items() if k in ('W_q', 'b_q', 'W_k', 'b_k', 'W_v', 'b_v', 'W_o', 'b_o')}
    del _L0_xattn_all

    def _L0_ffn_setup():
        import jax, jax.numpy as jnp
        import numpy as np
        N_EXPERTS = 16
        TOP_K = 4
        HIDDEN = 256
        INTER = 128
        B, S = (2, 256)
        key = jax.random.key(seed)
        k1, k2, k3, k4, k5 = jax.random.split(key, 5)
        return {'hidden_states': jax.random.normal(k1, (B, S, HIDDEN), dtype=jnp.float32), 'gate_w': jax.random.normal(k2, (N_EXPERTS, HIDDEN), dtype=jnp.float32) * 0.02, 'w1': jax.random.normal(k3, (N_EXPERTS, HIDDEN, INTER), dtype=jnp.float32) * 0.02, 'w3': jax.random.normal(k4, (N_EXPERTS, HIDDEN, INTER), dtype=jnp.float32) * 0.02, 'w2': jax.random.normal(k5, (N_EXPERTS, INTER, HIDDEN), dtype=jnp.float32) * 0.02}
    _L0_ffn_all = _L0_ffn_setup()
    _L0_ffn_in = {k: v for k, v in _L0_ffn_all.items() if k in ('gate_w', 'w1', 'w3', 'w2')}
    del _L0_ffn_all

    def _L1_xattn_setup():
        import jax, jax.numpy as jnp
        import numpy as np
        B, R, U, D = (16, 512, 512, 256)
        EPS_ATT = 1e-08
        EPS_LN = 1e-06
        key = jax.random.key(seed)
        ks = jax.random.split(key, 6)
        s = 1.0 / np.sqrt(D)
        return {'Q': jax.random.normal(ks[0], (B, R, D), dtype=jnp.float32), 'K': jax.random.normal(ks[1], (B, U, D), dtype=jnp.float32), 'V': jax.random.normal(ks[2], (B, U, D), dtype=jnp.float32), 'W1': jax.random.normal(ks[3], (D, D), dtype=jnp.float32) * s, 'b1': jnp.zeros((D,), dtype=jnp.float32), 'W2': jax.random.normal(ks[4], (D, D), dtype=jnp.float32) * s, 'b2': jnp.zeros((D,), dtype=jnp.float32), 'gamma': jnp.ones((D,), dtype=jnp.float32), 'beta': jnp.zeros((D,), dtype=jnp.float32)}
    _L1_xattn_all = _L1_xattn_setup()
    _L1_xattn_in = {k: v for k, v in _L1_xattn_all.items() if k in ('W1', 'b1', 'W2', 'b2', 'gamma', 'beta')}
    del _L1_xattn_all

    def _L1_ffn_setup():
        import jax, jax.numpy as jnp
        import numpy as np
        DIM = 256
        DEPTH = 2
        HEADS = 8
        DIM_HEAD = 64
        WINDOW = 128
        INNER = HEADS * DIM_HEAD
        HID = int(DIM * 4 * 2 / 3)
        B, N = (2, 2048)
        QK_SCALE = 8.0

        def shift_token(t):
            t1, t2 = jnp.split(t, 2, axis=-1)
            t2 = jnp.pad(t2, ((0, 0), (1, 0), (0, 0)))[:, :-1]
            return jnp.concatenate([t1, t2], axis=-1)

        def l2norm(t):
            return t / jnp.clip(jnp.linalg.norm(t, axis=-1, keepdims=True), 1e-12)

        def rotate_half(x):
            x1, x2 = jnp.split(x, 2, axis=-1)
            return jnp.concatenate([-x2, x1], axis=-1)

        def rotary_xpos(q, k):
            n = q.shape[-2]
            half_idx = jnp.arange(0, DIM_HEAD, 2, dtype=jnp.float32)
            inv_freq = 1.0 / 10000.0 ** (half_idx / DIM_HEAD)
            t = jnp.arange(n, dtype=jnp.float32)
            freqs = t[:, None] * inv_freq[None, :]
            freqs = jnp.concatenate([freqs, freqs], axis=-1)
            base = (half_idx + 0.4 * DIM_HEAD) / (1.4 * DIM_HEAD)
            power = (t - n // 2) / float(WINDOW // 2)
            scale = base[None, :] ** power[:, None]
            scale = jnp.concatenate([scale, scale], axis=-1)
            cos, sin = (jnp.cos(freqs), jnp.sin(freqs))
            q = q * cos * scale + rotate_half(q) * sin * scale
            k = k * cos / scale + rotate_half(k) * sin / scale
            return (q, k)

        def local_attention(q, k, v):
            b, h, n, d = q.shape
            w = n // WINDOW
            bq = q.reshape(b, h, w, WINDOW, d) * QK_SCALE
            bk = k.reshape(b, h, w, WINDOW, d)
            bv = v.reshape(b, h, w, WINDOW, d)

            def look_around(t):
                p = jnp.pad(t, ((0, 0), (0, 0), (1, 0), (0, 0), (0, 0)))
                return jnp.concatenate([p[:, :, :w], p[:, :, 1:]], axis=3)
            bk, bv = (look_around(bk), look_around(bv))
            bt = jnp.arange(n).reshape(w, WINDOW)
            btp = jnp.pad(bt, ((1, 0), (0, 0)), constant_values=-1)
            btk = jnp.concatenate([btp[:w], btp[1:]], axis=1)
            sim = jnp.einsum('bhwid,bhwjd->bhwij', bq, bk)
            i = bt[:, :, None]
            j = btk[:, None, :]
            mask = (i < j) | (i > j + WINDOW) | (j == -1)
            sim = jnp.where(mask, -jnp.finfo(sim.dtype).max, sim)
            attn = jax.nn.softmax(sim, axis=-1)
            out = jnp.einsum('bhwij,bhwjd->bhwid', attn, bv)
            return out.reshape(b, h, n, d)

        def _layer(x, wqkv, qs, ksc, wo, lg, lb, w1, b1, w2, b2):
            b, n, _ = x.shape
            h = shift_token(x)
            qkv = h @ wqkv
            q, k, v = jnp.split(qkv, 3, axis=-1)
            to_heads = lambda t: t.reshape(b, n, HEADS, DIM_HEAD).transpose(0, 2, 1, 3)
            q, k, v = (to_heads(q), to_heads(k), to_heads(v))
            q = l2norm(q) * qs
            k = l2norm(k) * ksc
            q, k = rotary_xpos(q, k)
            o = local_attention(q, k, v)
            o = o.transpose(0, 2, 1, 3).reshape(b, n, INNER)
            x = x + o @ wo
            h = shift_token(x)
            mu = h.mean(-1, keepdims=True)
            var = h.var(-1, keepdims=True)
            h = (h - mu) / jnp.sqrt(var + 1e-05) * lg + lb
            h = h @ w1 + b1
            a, g = jnp.split(h, 2, axis=-1)
            h = a * jax.nn.gelu(g, approximate=False)
            x = x + h @ w2 + b2
            return x
        key = jax.random.key(seed)
        ks = jax.random.split(key, 6)
        return {'x': jax.random.normal(ks[0], (B, N, DIM), jnp.float32), 'wqkv': jax.random.normal(ks[1], (DEPTH, DIM, 3 * INNER), jnp.float32) * 0.02, 'q_scale': jnp.ones((DEPTH, DIM_HEAD), jnp.float32), 'k_scale': jnp.ones((DEPTH, DIM_HEAD), jnp.float32), 'wo': jax.random.normal(ks[2], (DEPTH, INNER, DIM), jnp.float32) * 0.02, 'ln_g': jnp.ones((DEPTH, DIM), jnp.float32), 'ln_b': jnp.zeros((DEPTH, DIM), jnp.float32), 'w1': jax.random.normal(ks[3], (DEPTH, DIM, 2 * HID), jnp.float32) * 0.02, 'b1': jnp.zeros((DEPTH, 2 * HID), jnp.float32), 'w2': jax.random.normal(ks[4], (DEPTH, HID, DIM), jnp.float32) * 0.02, 'b2': jnp.zeros((DEPTH, DIM), jnp.float32)}
    _L1_ffn_all = _L1_ffn_setup()
    _L1_ffn_in = {k: v for k, v in _L1_ffn_all.items() if k in ('wqkv', 'q_scale', 'k_scale', 'wo', 'ln_g', 'ln_b', 'w1', 'b1', 'w2', 'b2')}
    del _L1_ffn_all

    def _L2_xattn_setup():
        import jax, jax.numpy as jnp
        import numpy as np
        DIM = 256
        HEADS = 16
        HEAD_DIM = DIM // HEADS
        SCALE = HEAD_DIM ** (-0.5)
        key = jax.random.key(seed)
        ks = jax.random.split(key, 6)
        B, Nq, Nkv = (2, 256, 512)
        s = DIM ** (-0.5)
        return {'x': jax.random.normal(ks[0], (B, Nq, DIM), jnp.float32), 'mem': jax.random.normal(ks[1], (B, Nkv, DIM), jnp.float32), 'W_kv': jax.random.normal(ks[2], (DIM, 2 * DIM), jnp.float32) * s, 'W_q': jax.random.normal(ks[3], (DIM, DIM), jnp.float32) * s, 'W_proj': jax.random.normal(ks[4], (DIM, DIM), jnp.float32) * s, 'b_proj': jax.random.normal(ks[5], (DIM,), jnp.float32) * 0.01}
    _L2_xattn_all = _L2_xattn_setup()
    _L2_xattn_in = {k: v for k, v in _L2_xattn_all.items() if k in ('W_kv', 'W_q', 'W_proj', 'b_proj')}
    del _L2_xattn_all

    def _L2_ffn_setup():
        import jax, jax.numpy as jnp
        import numpy as np
        TOP_K = 4
        key = jax.random.key(seed)
        ks = jax.random.split(key, 6)
        B, S, H, I, E = (2, 256, 256, 256, 16)
        SD = I * 1
        s = 0.02
        return {'hidden_states': jax.random.normal(ks[0], (B, S, H), jnp.float32), 'gate_w': jax.random.normal(ks[1], (E, H), jnp.float32) * s, 'w1': jax.random.normal(ks[2], (E, I, H), jnp.float32) * s, 'w2': jax.random.normal(ks[3], (E, H, I), jnp.float32) * s, 'shared_gu': jax.random.normal(ks[4], (2 * SD, H), jnp.float32) * s, 'shared_down': jax.random.normal(ks[5], (H, SD), jnp.float32) * s}
    _L2_ffn_all = _L2_ffn_setup()
    _L2_ffn_in = {k: v for k, v in _L2_ffn_all.items() if k in ('gate_w', 'w1', 'w2', 'shared_gu', 'shared_down')}
    del _L2_ffn_all

    def _L3_xattn_setup():
        import jax, jax.numpy as jnp
        import numpy as np
        import math
        D_MODEL = 256
        N_HEADS = 16
        D_K = D_MODEL // N_HEADS

        def _split_heads(x, B):
            return x.reshape(B, -1, N_HEADS, D_K).transpose(0, 2, 1, 3)

        def _phase_sync(x, phase):
            half = D_K // 2
            xr, xi = (x[..., :half], x[..., half:])
            c = jnp.cos(phase)[None]
            s = jnp.sin(phase)[None]
            return jnp.concatenate([xr * c - xi * s, xr * s + xi * c], axis=-1)
        key = jax.random.key(seed)
        ks = jax.random.split(key, 12)
        B, S = (2, 512)
        scale = 1.0 / math.sqrt(D_MODEL)
        inp = {'q': jax.random.normal(ks[0], (B, S, D_MODEL), jnp.float32), 'k': jax.random.normal(ks[1], (B, S, D_MODEL), jnp.float32), 'v': jax.random.normal(ks[2], (B, S, D_MODEL), jnp.float32), 'Wq': jax.random.normal(ks[3], (D_MODEL, D_MODEL), jnp.float32) * scale, 'bq': jnp.zeros((D_MODEL,), jnp.float32), 'Wk': jax.random.normal(ks[4], (D_MODEL, D_MODEL), jnp.float32) * scale, 'bk': jnp.zeros((D_MODEL,), jnp.float32), 'Wv': jax.random.normal(ks[5], (D_MODEL, D_MODEL), jnp.float32) * scale, 'bv': jnp.zeros((D_MODEL,), jnp.float32), 'Wo': jax.random.normal(ks[6], (D_MODEL, D_MODEL), jnp.float32) * scale, 'bo': jnp.zeros((D_MODEL,), jnp.float32), 'phase': jax.random.normal(ks[7], (N_HEADS, 1, 1), jnp.float32)}
        return inp
    _L3_xattn_all = _L3_xattn_setup()
    _L3_xattn_in = {k: v for k, v in _L3_xattn_all.items() if k in ('Wq', 'bq', 'Wk', 'bk', 'Wv', 'bv', 'Wo', 'bo', 'phase')}
    del _L3_xattn_all

    def _L3_ffn_setup():
        import jax, jax.numpy as jnp
        import numpy as np
        B, N, D = (4, 512, 256)
        SPARSITY = 0.01
        key = jax.random.key(seed)
        k1, k2, k3 = jax.random.split(key, 3)
        x = jax.random.normal(k1, (B, N, D), dtype=jnp.float32)
        spatial = jax.random.normal(k2, (D, D), dtype=jnp.float32) * 0.02
        freq = jnp.fft.fft(spatial, axis=-1)
        k = int(D * SPARSITY)
        mag = jnp.abs(freq)
        kth = jax.lax.top_k(mag, k)[0][:, -1:]
        w_sparse = jnp.where(mag >= kth, freq, 0.0 + 0j)
        bias = jax.random.normal(k3, (D,), dtype=jnp.float32) * 0.01
        return {'x': x, 'w_freq_real': jnp.real(w_sparse).astype(jnp.float32), 'w_freq_imag': jnp.imag(w_sparse).astype(jnp.float32), 'bias': bias}
    _L3_ffn_all = _L3_ffn_setup()
    _L3_ffn_in = {k: v for k, v in _L3_ffn_all.items() if k in ('w_freq_real', 'w_freq_imag', 'bias')}
    del _L3_ffn_all
    return {'x': x, 'ctx_1024': ctx_1024, 'mask_Bx1xSxS2_ik1': mask_Bx1xSxS2_ik1, 'g_xattn': g_xattn, 'g_ffn': g_ffn, 'L0_xattn_W_q': _L0_xattn_in['W_q'], 'L0_xattn_b_q': _L0_xattn_in['b_q'], 'L0_xattn_W_k': _L0_xattn_in['W_k'], 'L0_xattn_b_k': _L0_xattn_in['b_k'], 'L0_xattn_W_v': _L0_xattn_in['W_v'], 'L0_xattn_b_v': _L0_xattn_in['b_v'], 'L0_xattn_W_o': _L0_xattn_in['W_o'], 'L0_xattn_b_o': _L0_xattn_in['b_o'], 'L0_ffn_gate_w': _L0_ffn_in['gate_w'], 'L0_ffn_w1': _L0_ffn_in['w1'], 'L0_ffn_w3': _L0_ffn_in['w3'], 'L0_ffn_w2': _L0_ffn_in['w2'], 'L1_xattn_W1': _L1_xattn_in['W1'], 'L1_xattn_b1': _L1_xattn_in['b1'], 'L1_xattn_W2': _L1_xattn_in['W2'], 'L1_xattn_b2': _L1_xattn_in['b2'], 'L1_xattn_gamma': _L1_xattn_in['gamma'], 'L1_xattn_beta': _L1_xattn_in['beta'], 'L1_ffn_wqkv': _L1_ffn_in['wqkv'], 'L1_ffn_q_scale': _L1_ffn_in['q_scale'], 'L1_ffn_k_scale': _L1_ffn_in['k_scale'], 'L1_ffn_wo': _L1_ffn_in['wo'], 'L1_ffn_ln_g': _L1_ffn_in['ln_g'], 'L1_ffn_ln_b': _L1_ffn_in['ln_b'], 'L1_ffn_w1': _L1_ffn_in['w1'], 'L1_ffn_b1': _L1_ffn_in['b1'], 'L1_ffn_w2': _L1_ffn_in['w2'], 'L1_ffn_b2': _L1_ffn_in['b2'], 'L2_xattn_W_kv': _L2_xattn_in['W_kv'], 'L2_xattn_W_q': _L2_xattn_in['W_q'], 'L2_xattn_W_proj': _L2_xattn_in['W_proj'], 'L2_xattn_b_proj': _L2_xattn_in['b_proj'], 'L2_ffn_gate_w': _L2_ffn_in['gate_w'], 'L2_ffn_w1': _L2_ffn_in['w1'], 'L2_ffn_w2': _L2_ffn_in['w2'], 'L2_ffn_shared_gu': _L2_ffn_in['shared_gu'], 'L2_ffn_shared_down': _L2_ffn_in['shared_down'], 'L3_xattn_Wq': _L3_xattn_in['Wq'], 'L3_xattn_bq': _L3_xattn_in['bq'], 'L3_xattn_Wk': _L3_xattn_in['Wk'], 'L3_xattn_bk': _L3_xattn_in['bk'], 'L3_xattn_Wv': _L3_xattn_in['Wv'], 'L3_xattn_bv': _L3_xattn_in['bv'], 'L3_xattn_Wo': _L3_xattn_in['Wo'], 'L3_xattn_bo': _L3_xattn_in['bo'], 'L3_xattn_phase': _L3_xattn_in['phase'], 'L3_ffn_w_freq_real': _L3_ffn_in['w_freq_real'], 'L3_ffn_w_freq_imag': _L3_ffn_in['w_freq_imag'], 'L3_ffn_bias': _L3_ffn_in['bias']}

def reference(x, ctx_1024, mask_Bx1xSxS2_ik1, g_xattn, g_ffn, L0_xattn_W_q, L0_xattn_b_q, L0_xattn_W_k, L0_xattn_b_k, L0_xattn_W_v, L0_xattn_b_v, L0_xattn_W_o, L0_xattn_b_o, L0_ffn_gate_w, L0_ffn_w1, L0_ffn_w3, L0_ffn_w2, L1_xattn_W1, L1_xattn_b1, L1_xattn_W2, L1_xattn_b2, L1_xattn_gamma, L1_xattn_beta, L1_ffn_wqkv, L1_ffn_q_scale, L1_ffn_k_scale, L1_ffn_wo, L1_ffn_ln_g, L1_ffn_ln_b, L1_ffn_w1, L1_ffn_b1, L1_ffn_w2, L1_ffn_b2, L2_xattn_W_kv, L2_xattn_W_q, L2_xattn_W_proj, L2_xattn_b_proj, L2_ffn_gate_w, L2_ffn_w1, L2_ffn_w2, L2_ffn_shared_gu, L2_ffn_shared_down, L3_xattn_Wq, L3_xattn_bq, L3_xattn_Wk, L3_xattn_bk, L3_xattn_Wv, L3_xattn_bv, L3_xattn_Wo, L3_xattn_bo, L3_xattn_phase, L3_ffn_w_freq_real, L3_ffn_w_freq_imag, L3_ffn_bias):
    import jax
    import jax.numpy as jnp

    def _L0_xattn_ref(Query, Key, Values, Mask, W_q, b_q, W_k, b_k, W_v, b_v, W_o, b_o):
        import jax, jax.numpy as jnp
        import numpy as np
        D_MODEL = 256
        NUM_HEADS = 16
        D_K = D_MODEL // NUM_HEADS
        NEG_INF = -1000000000.0

        def _split_heads(x):
            B, S, _ = x.shape
            return x.reshape(B, S, NUM_HEADS, D_K).transpose(0, 2, 1, 3)
        q = _split_heads(Query @ W_q.T + b_q)
        k = _split_heads(Key @ W_k.T + b_k)
        v = _split_heads(Values @ W_v.T + b_v)
        scores = jnp.einsum('bhqd,bhkd->bhqk', q, k) / jnp.sqrt(jnp.float32(D_K))
        scores = jnp.where(Mask == 0, jnp.float32(NEG_INF), scores)
        attn = jax.nn.softmax(scores, axis=-1)
        out = jnp.einsum('bhqk,bhkd->bhqd', attn, v)
        B, H, S, Dk = out.shape
        out = out.transpose(0, 2, 1, 3).reshape(B, S, H * Dk)
        return out @ W_o.T + b_o

    def _L0_ffn_ref(hidden_states, gate_w, w1, w3, w2):
        import jax, jax.numpy as jnp
        import numpy as np
        N_EXPERTS = 16
        TOP_K = 4
        HIDDEN = 256
        INTER = 128
        B, S = (2, 256)
        'DeepseekV3 MoE adapter forward: router -> sparse scores -> expert GLU MLP -> combine.'
        b, s, h = hidden_states.shape
        x = hidden_states.reshape(-1, h)
        logits = jnp.einsum('th,eh->te', x, gate_w)
        probs = jax.nn.softmax(logits, axis=-1)
        topk_w, topk_idx = jax.lax.top_k(probs, TOP_K)
        topk_w = topk_w / jnp.sum(topk_w, axis=-1, keepdims=True)
        one_hot = (topk_idx[..., None] == jnp.arange(N_EXPERTS)).astype(topk_w.dtype)
        scores = jnp.einsum('tk,tke->te', topk_w, one_hot)
        g = jnp.einsum('th,ehi->tei', x, w1)
        u = jnp.einsum('th,ehi->tei', x, w3)
        act = jax.nn.silu(g) * u
        expert_out = jnp.einsum('tei,eih->teh', act, w2)
        out = jnp.einsum('teh,te->th', expert_out, scores)
        return out.reshape(b, s, h)

    def _L1_xattn_ref(Q, K, V, W1, b1, W2, b2, gamma, beta):
        import jax, jax.numpy as jnp
        import numpy as np
        B, R, U, D = (16, 512, 512, 256)
        EPS_ATT = 1e-08
        EPS_LN = 1e-06
        d_model = Q.shape[-1]
        scale = jnp.sqrt(jnp.asarray(d_model, jnp.float32) + EPS_ATT)
        scores = jnp.einsum('brd,bud->bru', Q, K) / scale
        att = jax.nn.softmax(scores, axis=-1)
        V_att = jnp.einsum('bru,bud->brd', att, V)

        def layer_norm(x):
            mu = jnp.mean(x, axis=-1, keepdims=True)
            var = jnp.mean(jnp.square(x - mu), axis=-1, keepdims=True)
            return gamma * (x - mu) / jnp.sqrt(var + EPS_LN) + beta
        X = layer_norm(Q + V_att)
        ffn = jnp.maximum(X @ W1 + b1, 0.0) @ W2 + b2
        return layer_norm(ffn + X)

    def _L1_ffn_ref(x, wqkv, q_scale, k_scale, wo, ln_g, ln_b, w1, b1, w2, b2):
        import jax, jax.numpy as jnp
        import numpy as np
        DIM = 256
        DEPTH = 2
        HEADS = 8
        DIM_HEAD = 64
        WINDOW = 128
        INNER = HEADS * DIM_HEAD
        HID = int(DIM * 4 * 2 / 3)
        B, N = (2, 2048)
        QK_SCALE = 8.0

        def shift_token(t):
            t1, t2 = jnp.split(t, 2, axis=-1)
            t2 = jnp.pad(t2, ((0, 0), (1, 0), (0, 0)))[:, :-1]
            return jnp.concatenate([t1, t2], axis=-1)

        def l2norm(t):
            return t / jnp.clip(jnp.linalg.norm(t, axis=-1, keepdims=True), 1e-12)

        def rotate_half(x):
            x1, x2 = jnp.split(x, 2, axis=-1)
            return jnp.concatenate([-x2, x1], axis=-1)

        def rotary_xpos(q, k):
            n = q.shape[-2]
            half_idx = jnp.arange(0, DIM_HEAD, 2, dtype=jnp.float32)
            inv_freq = 1.0 / 10000.0 ** (half_idx / DIM_HEAD)
            t = jnp.arange(n, dtype=jnp.float32)
            freqs = t[:, None] * inv_freq[None, :]
            freqs = jnp.concatenate([freqs, freqs], axis=-1)
            base = (half_idx + 0.4 * DIM_HEAD) / (1.4 * DIM_HEAD)
            power = (t - n // 2) / float(WINDOW // 2)
            scale = base[None, :] ** power[:, None]
            scale = jnp.concatenate([scale, scale], axis=-1)
            cos, sin = (jnp.cos(freqs), jnp.sin(freqs))
            q = q * cos * scale + rotate_half(q) * sin * scale
            k = k * cos / scale + rotate_half(k) * sin / scale
            return (q, k)

        def local_attention(q, k, v):
            b, h, n, d = q.shape
            w = n // WINDOW
            bq = q.reshape(b, h, w, WINDOW, d) * QK_SCALE
            bk = k.reshape(b, h, w, WINDOW, d)
            bv = v.reshape(b, h, w, WINDOW, d)

            def look_around(t):
                p = jnp.pad(t, ((0, 0), (0, 0), (1, 0), (0, 0), (0, 0)))
                return jnp.concatenate([p[:, :, :w], p[:, :, 1:]], axis=3)
            bk, bv = (look_around(bk), look_around(bv))
            bt = jnp.arange(n).reshape(w, WINDOW)
            btp = jnp.pad(bt, ((1, 0), (0, 0)), constant_values=-1)
            btk = jnp.concatenate([btp[:w], btp[1:]], axis=1)
            sim = jnp.einsum('bhwid,bhwjd->bhwij', bq, bk)
            i = bt[:, :, None]
            j = btk[:, None, :]
            mask = (i < j) | (i > j + WINDOW) | (j == -1)
            sim = jnp.where(mask, -jnp.finfo(sim.dtype).max, sim)
            attn = jax.nn.softmax(sim, axis=-1)
            out = jnp.einsum('bhwij,bhwjd->bhwid', attn, bv)
            return out.reshape(b, h, n, d)

        def _layer(x, wqkv, qs, ksc, wo, lg, lb, w1, b1, w2, b2):
            b, n, _ = x.shape
            h = shift_token(x)
            qkv = h @ wqkv
            q, k, v = jnp.split(qkv, 3, axis=-1)
            to_heads = lambda t: t.reshape(b, n, HEADS, DIM_HEAD).transpose(0, 2, 1, 3)
            q, k, v = (to_heads(q), to_heads(k), to_heads(v))
            q = l2norm(q) * qs
            k = l2norm(k) * ksc
            q, k = rotary_xpos(q, k)
            o = local_attention(q, k, v)
            o = o.transpose(0, 2, 1, 3).reshape(b, n, INNER)
            x = x + o @ wo
            h = shift_token(x)
            mu = h.mean(-1, keepdims=True)
            var = h.var(-1, keepdims=True)
            h = (h - mu) / jnp.sqrt(var + 1e-05) * lg + lb
            h = h @ w1 + b1
            a, g = jnp.split(h, 2, axis=-1)
            h = a * jax.nn.gelu(g, approximate=False)
            x = x + h @ w2 + b2
            return x
        for l in range(DEPTH):
            x = _layer(x, wqkv[l], q_scale[l], k_scale[l], wo[l], ln_g[l], ln_b[l], w1[l], b1[l], w2[l], b2[l])
        return x

    def _L2_xattn_ref(x, mem, W_kv, W_q, W_proj, b_proj):
        import jax, jax.numpy as jnp
        import numpy as np
        DIM = 256
        HEADS = 16
        HEAD_DIM = DIM // HEADS
        SCALE = HEAD_DIM ** (-0.5)
        B, Nkv, C = mem.shape
        Nq = x.shape[1]
        kv = (mem @ W_kv).reshape(B, Nkv, 2, HEADS, HEAD_DIM)
        k = kv[:, :, 0].transpose(0, 2, 1, 3)
        v = kv[:, :, 1].transpose(0, 2, 1, 3)
        q = (x @ W_q).reshape(B, Nq, HEADS, HEAD_DIM).transpose(0, 2, 1, 3)
        attn = jnp.einsum('bhqd,bhkd->bhqk', q, k) * SCALE
        attn = jax.nn.softmax(attn, axis=-1)
        out = jnp.einsum('bhqk,bhkd->bhqd', attn, v)
        out = out.transpose(0, 2, 1, 3).reshape(B, Nq, C)
        return out @ W_proj + b_proj

    def _L2_ffn_ref(hidden_states, gate_w, w1, w2, shared_gu, shared_down):
        import jax, jax.numpy as jnp
        import numpy as np
        TOP_K = 4
        orig_shape = hidden_states.shape
        H = orig_shape[-1]
        x = hidden_states.reshape(-1, H)
        T = x.shape[0]
        E = gate_w.shape[0]
        logits = x @ gate_w.T
        probs = jax.nn.softmax(logits, axis=-1)
        topv, topi = jax.lax.top_k(probs, TOP_K)
        topv = topv / jnp.sum(topv, axis=-1, keepdims=True)
        W = jnp.zeros((T, E), x.dtype).at[jnp.arange(T)[:, None], topi].set(topv)
        h = jax.nn.silu(jnp.einsum('th,eih->tei', x, w1))
        routed = jnp.einsum('tei,ehi,te->th', h, w2, W)
        gu = x @ shared_gu.T
        gate, up = jnp.split(gu, 2, axis=-1)
        shared = jax.nn.silu(gate) * up @ shared_down.T
        return (routed + shared).reshape(orig_shape)

    def _L3_xattn_ref(q, k, v, Wq, bq, Wk, bk, Wv, bv, Wo, bo, phase):
        import jax, jax.numpy as jnp
        import numpy as np
        import math
        D_MODEL = 256
        N_HEADS = 16
        D_K = D_MODEL // N_HEADS

        def _split_heads(x, B):
            return x.reshape(B, -1, N_HEADS, D_K).transpose(0, 2, 1, 3)

        def _phase_sync(x, phase):
            half = D_K // 2
            xr, xi = (x[..., :half], x[..., half:])
            c = jnp.cos(phase)[None]
            s = jnp.sin(phase)[None]
            return jnp.concatenate([xr * c - xi * s, xr * s + xi * c], axis=-1)
        B = q.shape[0]
        qh = _split_heads(q @ Wq.T + bq, B)
        kh = _split_heads(k @ Wk.T + bk, B)
        vh = _split_heads(v @ Wv.T + bv, B)
        qh = _phase_sync(qh, phase)
        kh = _phase_sync(kh, phase)
        scores = jnp.einsum('bhqd,bhkd->bhqk', qh, kh) / math.sqrt(D_K)
        attn = jax.nn.softmax(scores, axis=-1)
        out = jnp.einsum('bhqk,bhkd->bhqd', attn, vh)
        out = out.transpose(0, 2, 1, 3).reshape(B, -1, D_MODEL)
        return out @ Wo.T + bo

    def _L3_ffn_ref(x, w_freq_real, w_freq_imag, bias):
        import jax, jax.numpy as jnp
        import numpy as np
        B, N, D = (4, 512, 256)
        SPARSITY = 0.01
        w = jax.lax.complex(w_freq_real, w_freq_imag)
        x_freq = jnp.fft.fft(x, axis=-1)
        y_freq = jnp.einsum('bnd,do->bno', x_freq, w)
        y = jnp.real(jnp.fft.ifft(y_freq, axis=-1))
        return y + bias
    x = x + jnp.tanh(g_xattn[0]) * _L0_xattn_ref(_layernorm(x, axis=-1), ctx_1024, ctx_1024, mask_Bx1xSxS2_ik1, L0_xattn_W_q, L0_xattn_b_q, L0_xattn_W_k, L0_xattn_b_k, L0_xattn_W_v, L0_xattn_b_v, L0_xattn_W_o, L0_xattn_b_o)
    x = x + jnp.tanh(g_ffn[0]) * _L0_ffn_ref(_layernorm(x, axis=-1), L0_ffn_gate_w, L0_ffn_w1, L0_ffn_w3, L0_ffn_w2)
    x = x + jnp.tanh(g_xattn[1]) * _L1_xattn_ref(_layernorm(x, axis=-1), ctx_1024, ctx_1024, L1_xattn_W1, L1_xattn_b1, L1_xattn_W2, L1_xattn_b2, L1_xattn_gamma, L1_xattn_beta)
    x = x + jnp.tanh(g_ffn[1]) * _L1_ffn_ref(_layernorm(x, axis=-1), L1_ffn_wqkv, L1_ffn_q_scale, L1_ffn_k_scale, L1_ffn_wo, L1_ffn_ln_g, L1_ffn_ln_b, L1_ffn_w1, L1_ffn_b1, L1_ffn_w2, L1_ffn_b2)
    x = x + jnp.tanh(g_xattn[2]) * _L2_xattn_ref(_layernorm(x, axis=-1), ctx_1024, L2_xattn_W_kv, L2_xattn_W_q, L2_xattn_W_proj, L2_xattn_b_proj)
    x = x + jnp.tanh(g_ffn[2]) * _L2_ffn_ref(_layernorm(x, axis=-1), L2_ffn_gate_w, L2_ffn_w1, L2_ffn_w2, L2_ffn_shared_gu, L2_ffn_shared_down)
    x = x + jnp.tanh(g_xattn[3]) * _L3_xattn_ref(_layernorm(x, axis=-1), ctx_1024, ctx_1024, L3_xattn_Wq, L3_xattn_bq, L3_xattn_Wk, L3_xattn_bk, L3_xattn_Wv, L3_xattn_bv, L3_xattn_Wo, L3_xattn_bo, L3_xattn_phase)
    x = x + jnp.tanh(g_ffn[3]) * _L3_ffn_ref(_layernorm(x, axis=-1), L3_ffn_w_freq_real, L3_ffn_w_freq_imag, L3_ffn_bias)
    return x

_drawn_inputs = setup_inputs


def setup_inputs(seed=0):
    import zlib

    import numpy as np

    out = dict(_drawn_inputs(seed))
    spreads = {'L0_xattn_b_q': (0.0, 0.632),
     'L0_xattn_b_k': (0.0, 2.0),
     'L0_xattn_b_v': (0.0, 0.1),
     'L0_xattn_b_o': (0.0, 0.1),
     'L1_xattn_b1': (0.0, 0.345),
     'L1_xattn_b2': (0.0, 0.329),
     'L1_xattn_gamma': (1.0, 0.2),
     'L1_xattn_beta': (0.0, 0.1),
     'L1_ffn_q_scale': (1.0, 0.6),
     'L1_ffn_k_scale': (1.0, 0.6),
     'L1_ffn_ln_g': (1.0, 0.6),
     'L1_ffn_ln_b': (0.0, 0.8),
     'L1_ffn_b1': (0.0, 0.786),
     'L1_ffn_b2': (0.0, 0.1),
     'L3_xattn_bq': (0.0, 2.0),
     'L3_xattn_bk': (0.0, 2.0),
     'L3_xattn_bv': (0.0, 0.8),
     'L3_xattn_bo': (0.0, 0.8)}
    factors = {'L0_ffn_gate_w': 8.0,
     'L0_ffn_w1': 8.0,
     'L0_ffn_w3': 8.0,
     'L0_ffn_w2': 8.0,
     'L2_xattn_b_proj': 24.957,
     'L2_ffn_gate_w': 5.938,
     'L2_ffn_w1': 5.248,
     'L2_ffn_w2': 5.179,
     'L2_ffn_shared_gu': 8.0,
     'L2_ffn_shared_down': 8.0,
     'L3_xattn_phase': 200.0,
     'L3_ffn_bias': 64.0,
     'g_ffn': 8.0,
     'L3_xattn_Wq': 3.379,
     'L3_xattn_Wk': 2.79}
    for name, (base, spread) in spreads.items():
        noise = np.random.default_rng([zlib.crc32(name.encode()), seed]).standard_normal(out[name].shape)
        drawn = base * np.exp(spread * noise) if base else spread * noise
        out[name] = jnp.asarray(drawn.astype(out[name].dtype))
    for name, factor in factors.items():
        out[name] = (out[name] * factor).astype(out[name].dtype)
    return out
```

```python
from contextlib import ExitStack

import numpy as np
import concourse.bass as bass
from concourse import mybir

P = 128
NB, S, D = 16, 128, 256
KC = D // P
E, TOPK = 16, 4
GT = 512
NG = NB * S // GT
TPG = GT // P
H16, DH = 16, 16
LH, LD = 8, 64
INNER = LH * LD
HID = int(D * 4 * 2 / 3)

F32 = mybir.dt.float32
BF16 = mybir.dt.bfloat16
I32 = mybir.dt.int32
ALU = mybir.AluOpType
ACT = mybir.ActivationFunctionType
AXX = mybir.AxisListType.X

UNIT_GLU, UNIT_ONE = 3 * D, 2 * D
L0F = E * UNIT_GLU
UNITS1 = -(-HID // P)
WQKV, WO1 = KC * 3 * INNER, INNER // P * D
L1F = WQKV + WO1 + UNITS1 * UNIT_GLU
L2F = 2 * UNIT_GLU + 2 * E * UNIT_ONE
MLP1 = 2 * KC * D
ARENA = 2 * L1F + MLP1
MLP1_AT = 2 * L1F
assert L2F <= ARENA and L0F <= MLP1_AT
HEADS_W = 4 * KC * D
SLOT = HEADS_W + 6 + D
C_IDENT, C_PARITY, C_SHIFT, C_CAUSAL, C_ROPE = 0, P, 3 * P, 4 * P, 5 * P
CONSTS = C_ROPE + 4 * LD
COLS1X, ROWS1X = KC, 3 * D
COLS1F, ROWS1F = 2 * KC + 2 * UNITS1, D + 2 * LD


class Step:

    def __init__(self, n, parity, half):
        self.n, self.p, self.h = n, parity, half


def run_pipeline(eng, pieces, count=NB):
    def step(t, parity, half, peeled):
        for fn, off in pieces:
            if peeled and not 0 <= t + off < count:
                continue
            fn(Step(t + off, (parity + off) % 2, half + (parity + off) // 2))
    for t in (-1, 0):
        step(t, t % 2, t // 2, True)
    with eng.Fori(0, (count - 2) // 2) as i:
        step(i * 2 + 1, 1, i, False)
        step(i * 2 + 2, 0, i + 1, False)
    for t in (count - 1, count):
        step(t, t % 2, t // 2, True)


def after(eng, sem, value, s=None, first=0):
    if s is not None and isinstance(s.n, int) and s.n < first:
        return
    if isinstance(value, int) and value <= 0:
        return
    eng.wait_ge(sem, value)


def last(s):
    return isinstance(s.n, int) and s.n == NB - 1


def seq(t, s):
    if isinstance(s.n, int):
        return t[:, s.n, :]
    return t[:, bass.ds(s.n, 1), :].rearrange("p a d -> p (a d)")


class Phase:

    def __init__(self, nc, name):
        self.nc, self.name, self.sems = nc, name, []
        self.ctx, self.work = ExitStack(), ExitStack()

    def __enter__(self):
        return self

    def sb(self, name, shape, dt=F32):
        return self.ctx.enter_context(self.nc.sbuf_tensor(f"{self.name}_{name}", shape, dt))

    def ps(self, name, shape, dt=F32):
        return self.ctx.enter_context(self.nc.psum_tensor(f"{self.name}_{name}", shape, dt))

    def sem(self, name):
        s = self.ctx.enter_context(self.nc.semaphore(f"{self.name}_{name}"))
        self.sems.append(s)
        return s

    def semaphores(self, names):
        return [self.sem(n) for n in names.split()]

    def block(self):
        return self.work.enter_context(self.nc.Block())

    def __exit__(self, kind, *rest):
        if kind is None:
            self.work.close()
            for s in self.sems:
                self.nc.gpsimd.sem_clear(s)
            self.nc.all_engine_barrier()
            self.ctx.close()


class Core:

    def __init__(self, nc, ctx, dram):
        self.nc, self.dram = nc, dram

        def sb(name, shape, dt=F32):
            return ctx.enter_context(nc.sbuf_tensor(name, shape, dt))
        self.X = sb("X", [P, NB, D])
        self.slot = sb("slot", [P, SLOT])
        self.arena = sb("arena", [P, ARENA])
        self.consts = sb("consts", [P, CONSTS])
        self.gates = sb("gates", [P, 8])
        self.stats = sb("stats", [P, NB, 12])
        self.mean, self.rstd, self.var, self.tmp = (sb(n, [P, NB]) for n in ("mean", "rstd", "var", "tmp"))
        self.dev = sb("dev", [P, NB, 4])
        self.causal = sb("causal", [P, 4, P], BF16)
        self.ident16 = sb("ident16", [P, P], BF16)
        self.gatew = sb("gatew", [P, 2, KC, E])
        self.vec1x = sb("vec1x", [P, COLS1X + ROWS1X])
        self.vec1f = sb("vec1f", [P, 2, COLS1F + ROWS1F])
        self.ident = self.consts[:, C_IDENT:C_IDENT + P]
        self.parity = self.consts[:, C_PARITY:C_SHIFT].rearrange("p (e t) -> p e t", e=2)
        self.shift = self.consts[:, C_SHIFT:C_SHIFT + P]
        self.rope = self.consts[:, C_ROPE:C_ROPE + 4 * LD]
        names = ["const", "L0x", "L0f", "L1x", "L1f0", "L1f1", "L2x", "L2f", "L3x", "L3f"]
        self.loaded = {n: ctx.enter_context(nc.semaphore(f"loaded_{n}")) for n in names}
        self.s_gate = ctx.enter_context(nc.semaphore("gates_ready"))

    def dma(self, eng, name, dst, src):
        eng.dma_start(dst, src).then_inc(self.loaded[name], 16)

    def load(self, eng, name):
        d = self.dram
        if name in ("L0x", "L2x", "L3x"):
            self.dma(eng, name, self.slot[:, 0:HEADS_W + 6], d[f"w_{name}"])
            self.dma(eng, name, self.slot[:, HEADS_W + 6:SLOT], d[f"row_{name}"].partition_broadcast(P))
        elif name in ("L0f", "L2f"):
            n = L0F if name == "L0f" else L2F
            for a in range(0, n, n // 4):
                self.dma(eng, name, self.arena[:, a:a + n // 4], d[f"w_{name}"][:, a:a + n // 4])
        elif name == "L1x":
            self.dma(eng, name, self.arena[:, MLP1_AT:MLP1_AT + MLP1], d["w_L1x"])
            self.dma(eng, name, self.vec1x[:, 0:COLS1X], d["col_L1x"])
            self.dma(eng, name, self.vec1x[:, COLS1X:], d["row_L1x"].partition_broadcast(P))
        elif name == "L3f":
            self.dma(eng, name, self.arena[:, 0:3 * KC * D], d["dft"])
            self.dma(eng, name, self.arena[:, 3 * KC * D:5 * KC * D], d["w_L3f"])
            self.dma(eng, name, self.arena[:, 5 * KC * D:5 * KC * D + D], d["row_L3f"].partition_broadcast(P))
        else:
            i = int(name[-1])
            self.dma(eng, name, self.arena[:, i * L1F:(i + 1) * L1F], d[f"w_{name}"])
            self.dma(eng, name, self.vec1f[:, i, 0:COLS1F], d[f"col_{name}"])
            self.dma(eng, name, self.vec1f[:, i, COLS1F:], d[f"row_{name}"].partition_broadcast(P))

    def wait(self, eng, name):
        n = {"L0x": 2, "L2x": 2, "L3x": 2, "L0f": 4, "L2f": 4, "const": 4}.get(name, 3)
        eng.wait_ge(self.loaded[name], 16 * n)


class Chain:

    def __init__(self, eng, sem, base=0):
        self.eng, self.sem, self.base, self.n = eng, sem, base, 0

    def __call__(self, ins, wait=True):
        ins.then_inc(self.sem, 1)
        self.n += 1
        if wait:
            self.eng.wait_ge(self.sem, self.base + self.n)


MAGIC = float(0x5F3759DF)


def guess_rsqrt(vec, y, v):
    return vec.tensor_scalar(y.bitcast(I32), v.bitcast(I32), -0.5, MAGIC, ALU.mult, ALU.add)


def rsqrt(vec, link, y, v, t):
    link(guess_rsqrt(vec, y, v))
    for _ in range(3):
        link(vec.tensor_tensor(t, y, y, ALU.mult))
        link(vec.tensor_tensor(t, t, v, ALU.mult))
        link(vec.tensor_scalar(t, t, -0.5, 1.5, ALU.mult, ALU.add))
        link(vec.tensor_tensor(y, y, t, ALU.mult))


NEWTON_STEPS = 13


def newton_rsqrt(pool, link, y, v, t, half, three_halves):
    link(pool.tensor_tensor(v, v, half, ALU.mult))
    for _ in range(3):
        link(pool.tensor_tensor(t, y, y, ALU.mult))
        link(pool.tensor_tensor(t, t, v, ALU.mult))
        link(pool.tensor_tensor(t, t, three_halves, ALU.add))
        link(pool.tensor_tensor(y, y, t, ALU.mult))


def finish_stats(nc, link, c, groups, eps):
    v = nc.vector
    parts = c.stats[:, :, 0:3 * groups].rearrange("p b (g s) -> p b g s", s=3)
    means, m2 = parts[:, :, :, 1], parts[:, :, :, 2]
    dev, var, t = c.dev[:, :, 0:groups], c.var[:, :], c.tmp[:, :]
    link(v.tensor_reduce(c.mean[:, :], means, AXX, ALU.add))
    link(v.tensor_scalar(c.mean[:, :], c.mean[:, :], 1.0 / groups, None, ALU.mult))
    link(v.tensor_tensor(dev, means, c.mean[:, :].unsqueeze(2).broadcast_to([P, NB, groups]), ALU.subtract))
    link(v.tensor_tensor(dev, dev, dev, ALU.mult))
    link(v.tensor_reduce(t, dev, AXX, ALU.add))
    link(v.tensor_reduce(var, m2, AXX, ALU.add))
    link(v.tensor_scalar(var, var, 1.0 / D, eps, ALU.mult, ALU.add))
    link(v.scalar_tensor_tensor(var, t, 1.0 / groups, var, ALU.mult, ALU.add))
    rsqrt(v, link, c.rstd[:, :], var, t)


def normalize(nc, c, dst, src, s):
    return nc.vector.tensor_scalar(dst, src, per_seq(c.mean, s), per_seq(c.rstd, s), ALU.subtract, ALU.mult)


def dram_seq(t, s, form):
    return t[s.n] if isinstance(s.n, int) else t[bass.ds(s.n, 1)].rearrange(form)


def per_seq(t, s):
    return t[:, s.n:s.n + 1] if isinstance(s.n, int) else t[:, bass.ds(s.n, 1)]



def heads_attention(nc, c, name, gate, mask=None, loads=()):
    with Phase(nc, name) as ph:
        W = c.slot[:, 0:HEADS_W].rearrange("p (m k n) -> p m k n", m=4, k=KC)
        wq, wk, wv, wo = W[:, 0], W[:, 1], W[:, 2], W[:, 3]
        cols = c.slot[:, HEADS_W:HEADS_W + 6]
        bq, bk, bv, bo = cols[:, 0:2], cols[:, 2:4], cols[:, 4:6], c.slot[:, HEADS_W + 6:SLOT]

        hn = ph.sb("hn", [P, 2, D])
        hT, cT, qT, kc = (ph.sb(n, [P, 2, KC, P]) for n in ("hT", "cT", "qT", "kc"))
        kEO = ph.sb("kEO", [P, 2, KC, 2, P])
        vx = ph.sb("vx", [P, 2, H16, DH + 1])
        pr = ph.sb("pr", [P, 2, 4, 512])
        nmx = ph.sb("nmx", [P, 2, H16])
        pT = ph.sb("pT", [P, 2, 512])
        rs = ph.sb("rs", [P, H16])
        on = ph.sb("on", [P, D])
        oT = ph.sb("oT", [P, KC, P])
        gbo = ph.sb("gbo", [P, D])
        bq4 = ph.sb("bq4", [P, KC])
        if mask is not None:
            mi = ph.sb("mi", [P, NB, P], I32)
            cap = ph.sb("cap", [P, NB, P])
            sm = ph.sb("sm", [P, 2, 4, 512])
        psS = ph.ps("psS", [P, 4, 512])
        psP = ph.ps("psP", [P, 2, 512])
        psO = ph.ps("psO", [P, 512])
        psQ = ph.ps("psQ", [P, 512])

        s_ctx = [ph.sem("ctx0"), ph.sem("ctx1")]
        (s_one, s_fin, s_mi, s_cap, s_bias, s_ln, s_T, s_hT, s_K, s_kc, s_k, s_Q, s_q, s_V, s_vx, s_S, s_min, s_mx,
         s_exp, s_pt, s_pT0, s_pT1, s_pv, s_on, s_ot, s_oT, s_out, s_xb, s_x) = ph.semaphores(
            "ones fin mask cap bias ln T hT K kc k Q q V vx S min mx exp pt pT0 pT1 pv on ot oT out xb x")
        block = ph.block()

        @block.sync
        def _(sp):
            if mask is not None:
                sp.dma_start(mi[:, :, :], mask.rearrange("b q k -> q b k")).then_inc(s_mi, 16)
            for load in loads:
                load(sp)

            def context_in(s):
                after(sp, s_V, s.n - 1, s, 2)
                after(sp, s_K, s.n - 1, s, 2)
                sp.dma_start(cT[:, s.p], dram_seq(c.dram["ctxT"], s, "b p k t -> (b p) k t")).then_inc(s_ctx[s.p], 16)
            run_pipeline(sp, [(context_in, 1)])

        @block.gpsimd
        def _(pool):
            nc.gpsimd.memset(vx[:, :, :, DH:DH + 1], 1.0).then_inc(s_one, 1)
            c.wait(pool, name)
            pool.wait_ge(c.s_gate, 1)
            nc.gpsimd.tensor_scalar(gbo[:, :], bo, c.gates[:, gate:gate + 1], None, ALU.mult).then_inc(s_bias, 1)
            pool.wait_ge(s_bias, 1)

            def keys(s):
                pool.wait_ge(s_kc, s.n + 1)
                after(pool, s_S, (s.n - 1) * 4, s, 2)
                for eo in range(2):
                    nc.gpsimd.tensor_tensor(kEO[:, s.p, :, eo], kc[:, s.p], c.parity[:, eo, :].unsqueeze(1).broadcast_to([P, KC, P]),
                                            ALU.mult).then_inc(s_k, 1)

            def output_bias(s):
                pool.wait_ge(s_ln, s.n + 1)
                nc.gpsimd.tensor_tensor(seq(c.X, s), seq(c.X, s), gbo[:, :], ALU.add).then_inc(s_xb, 1)
            run_pipeline(pool, [(output_bias, 0), (keys, 1)])

        @block.tensor
        def _(pe):
            c.wait(pe, name)
            c.wait(pe, "const")

            def scores(s):
                pe.wait_ge(s_k, s.n * 2 + 2)
                pe.wait_ge(s_q, s.n + 1)
                for g in range(4):
                    r = slice(32 * g, 32 * g + 32)
                    after(pe, s_exp if mask is None else s_min, s.n * 4 - (3 - g), s, 1)
                    for k in range(KC):
                        mm = nc.tensor.matmul(psS[:, g, k * 256:(k + 1) * 256], qT[r, s.p, k], kEO[r, s.p, k],
                                              start=True, stop=True)
                    mm.then_inc(s_S, 1)

            def turn_out(s):
                pe.wait_ge(s_on, s.n * 2 + 2)
                for k in range(KC):
                    mm = nc.tensor.transpose(psO[:, k * P:(k + 1) * P], on[:, k * P:(k + 1) * P], c.ident)
                mm.then_inc(s_ot, 1)

            def turn_in(s):
                pe.wait_ge(s_ln, s.n + 1)
                after(pe, s_q, s.n, s, 1)
                for k in range(KC):
                    mm = nc.tensor.transpose(psQ[:, k * P:(k + 1) * P], hn[:, s.p, k * P:(k + 1) * P], c.ident)
                mm.then_inc(s_T, 1)

            def values_in(s):
                pe.wait_ge(s_ctx[s.p], s.h * 16 + 16)
                after(pe, s_pT1, s.n * 2 - 2, s, 2)
                for k in range(KC):
                    mm = nc.tensor.matmul(psP[:, 1, 0:D], cT[:, s.p, k], wv[:, k], start=(k == 0), stop=(k == KC - 1))
                mm.then_inc(s_V, 1)

            def output(s):
                pe.wait_ge(s_oT, s.n * 2 + 2)
                for k in range(KC):
                    mm = nc.tensor.matmul(psO[:, 0:D], oT[:, k], wo[:, k], start=(k == 0), stop=(k == KC - 1))
                mm.then_inc(s_out, 1)

            def project(w, rhs, base, s, done):
                for o in range(KC):
                    for k in range(KC):
                        mm = nc.tensor.matmul(psQ[:, base + o * P:base + (o + 1) * P], w[:, k, o * P:(o + 1) * P],
                                              rhs[:, s.p, k], start=(k == 0), stop=(k == KC - 1))
                mm.then_inc(done, 1)

            def keys(s):
                pe.wait_ge(s_hT, s.n + 1)
                project(wk, cT, D, s, s_K)

            def queries(s):
                pe.wait_ge(s_kc, s.n + 1)
                project(wq, hT, 0, s, s_Q)

            def turn(s, g):
                pe.wait_ge(s_exp, s.n * 4 + g + 1)
                if g == 1:
                    pe.wait_ge(s_vx, s.n + (1 if last(s) else 2))
                if g == 0:
                    after(pe, s_pT0, s.n * 2, s, 1)
                if g > 1:
                    pe.wait_ge(s_pT1 if g % 2 else s_pT0, s.n * 2 + 1)
                for j in range(4):
                    mm = nc.tensor.transpose(psP[:, g % 2, j * P:(j + 1) * P], pr[:, s.p, g, j * P:(j + 1) * P], c.ident)
                mm.then_inc(s_pt, 1)

            def weigh(s, g):
                pe.wait_ge(s_pT1 if g % 2 else s_pT0, s.n * 2 + g // 2 + 1)
                if g == 0:
                    after(pe, s_x, s.n, s, 1)
                for j in range(4):
                    head = 8 * (j // 2) + 2 * g + j % 2
                    mm = nc.tensor.matmul(psO[:, head * 17:head * 17 + 17], pT[:, g % 2, j * P:(j + 1) * P],
                                          vx[:, s.p, head, :], start=True, stop=True)
                mm.then_inc(s_pv, 1)

            def turn01(s):
                turn(s, 0)
                turn(s, 1)

            def rest(s):
                weigh(s, 0)
                turn(s, 2)
                weigh(s, 1)
                turn(s, 3)
                weigh(s, 2)
                weigh(s, 3)
            run_pipeline(pe, [(scores, 0), (turn_out, -1), (turn_in, 1), (values_in, 1), (output, -1), (keys, 1),
                              (turn01, 0), (queries, 1), (rest, 0)])

        @block.scalar
        def _(act):
            c.wait(act, name)
            c.wait(act, "const")
            act.wait_ge(s_one, 1)
            nc.scalar.activation(bq4[:, :], bq, ACT.Copy, scale=0.25).then_inc(s_bias, 1)
            act.wait_ge(s_bias, 2)

            def exps(s, groups):
                for g in groups:
                    act.wait_ge(s_mx, s.n * 4 + g + 1)
                    if g == 0:
                        after(act, s_pt, s.n * 4 - 4, s, 2)
                    src = psS[:, g] if mask is None else sm[:, s.p, g]
                    for j in range(4):
                        ins = nc.scalar.activation(pr[:, s.p, g, j * P:(j + 1) * P], src[:, j * P:(j + 1) * P], ACT.Exp,
                                                   bias=nmx[:, s.p, 4 * g + j:4 * g + j + 1])
                    ins.then_inc(s_exp, 1)

            def output(s):
                act.wait_ge(s_ot, s.n + 1)
                after(act, s_out, s.n, s, 1)
                for k in range(KC):
                    nc.scalar.activation(oT[:, k], psO[:, k * P:(k + 1) * P], ACT.Identity,
                                         bias=bv[:, k:k + 1]).then_inc(s_oT, 1)

            def rows(s):
                act.wait_ge(s_T, s.n + 1)
                after(act, s_Q, s.n - 1, s, 2)
                nc.scalar.activation(hT[:, s.p].rearrange("p k t -> p (k t)"), psQ[:, 0:D], ACT.Copy).then_inc(s_hT, 1)

            def values_in(s):
                act.wait_ge(s_V, s.n + 1)
                after(act, s_pv, s.n * 4 - 4, s, 2)
                nc.scalar.activation(vx[:, s.p, :, 0:DH], psP[:, 1, 0:D].rearrange("p (h d) -> p h d", h=H16), ACT.Copy).then_inc(s_vx, 1)

            def keys(s):
                act.wait_ge(s_K, s.n + 1)
                after(act, s_k, s.n * 2 - 2, s, 2)
                for k in range(KC):
                    ins = nc.scalar.activation(kc[:, s.p, k], psQ[:, D + k * P:D + (k + 1) * P], ACT.Identity, bias=bk[:, k:k + 1])
                ins.then_inc(s_kc, 1)

            def queries(s):
                act.wait_ge(s_Q, s.n + 1)
                after(act, s_S, s.n * 4 - 4, s, 2)
                for k in range(KC):
                    ins = nc.scalar.activation(qT[:, s.p, k], psQ[:, k * P:(k + 1) * P], ACT.Identity, scale=DH ** -0.5,
                                               bias=bq4[:, k:k + 1])
                ins.then_inc(s_q, 1)

            def turned(s, g):
                act.wait_ge(s_pt, s.n * 4 + g + 1)
                if g == 1:
                    after(act, s_pv, s.n * 4, s, 1)
                else:
                    act.wait_ge(s_pv, s.n * 4 + 2)
                nc.scalar.activation(pT[:, 1], psP[:, 1], ACT.Copy).then_inc(s_pT1, 1)
            run_pipeline(act, [(lambda s: exps(s, (0, 1)), 0), (output, -1), (rows, 1), (values_in, 1), (lambda s: exps(s, (2, 3)), 0),
                               (keys, 1), (lambda s: turned(s, 1), 0), (queries, 1), (lambda s: turned(s, 3), 0)])

        @block.vector
        def _(dve):
            c.wait(dve, name)
            c.wait(dve, "const")
            dve.wait_ge(c.s_gate, 1)
            finish_stats(nc, Chain(dve, s_fin), c, 2, 1e-5)
            if mask is not None:
                dve.wait_ge(s_mi, 16)
                huge = sm[:, 0].rearrange("p g (h k) -> p (g h) k", k=P)
                link = Chain(dve, s_cap)
                link(nc.vector.tensor_scalar(huge, mi[:, :, :], 0.0, 3e38, ALU.not_equal, ALU.mult), wait=False)
                link(nc.vector.tensor_scalar(cap[:, :, :], mi[:, :, :], 0.0, -1e9, ALU.is_equal, ALU.mult))
                link(nc.vector.tensor_tensor(cap[:, :, :], cap[:, :, :], huge, ALU.add))

            def heads4(t):
                return t.rearrange("p (h k) -> p h k", h=4)

            def rows(s):
                after(dve, s_T, s.n - 1, s, 2)
                normalize(nc, c, hn[:, s.p], seq(c.X, s), s).then_inc(s_ln, 1)

            def tops(s):
                after(dve, s_exp, s.n * 4 - 4, s, 2)
                for g in range(4):
                    dve.wait_ge(s_S, s.n * 4 + g + 1)
                    src = psS[:, g]
                    if mask is not None:
                        src = sm[:, s.p, g]
                        nc.vector.tensor_tensor(heads4(src), heads4(psS[:, g]),
                                                seq(cap, s).unsqueeze(1).broadcast_to([P, 4, P]), ALU.min).then_inc(s_min, 1)
                        dve.wait_ge(s_min, s.n * 4 + g + 1)
                    nc.vector.tensor_reduce(nmx[:, s.p, 4 * g:4 * g + 4], heads4(src), AXX, ALU.max, negate=True).then_inc(s_mx, 1)

            def output(s):
                dve.wait_ge(s_out, s.n + 1)
                dve.wait_ge(s_xb, s.n + 1)
                nc.vector.scalar_tensor_tensor(seq(c.X, s), psO[:, 0:D], c.gates[:, gate:gate + 1], seq(c.X, s),
                                               ALU.mult, ALU.add).then_inc(s_x, 1)
                dve.wait_ge(s_x, s.n + 1)
                nc.vector.bn_stats(seq(c.stats, s)[:, 0:6], seq(c.X, s))

            def values(s):
                for g in (0, 2):
                    dve.wait_ge(s_pt, s.n * 4 + g + 1)
                    if g:
                        dve.wait_ge(s_pv, s.n * 4 + 1)
                    else:
                        after(dve, s_pv, s.n * 4 - 1, s, 1)
                    nc.vector.tensor_copy(pT[:, 0], psP[:, 0]).then_inc(s_pT0, 1)
                dve.wait_ge(s_pv, s.n * 4 + 4)
                o = psO[:, 0:H16 * 17].rearrange("p (h d) -> p h d", h=H16)
                nc.vector.reciprocal(rs[:, :], o[:, :, DH]).then_inc(s_on, 1)
                dve.wait_ge(s_on, s.n * 2 + 1)
                after(dve, s_ot, s.n, s, 1)
                nc.vector.tensor_tensor(on[:, :].rearrange("p (h d) -> p h d", h=H16), o[:, :, 0:DH],
                                        rs[:, :].unsqueeze(2).broadcast_to([P, H16, DH]), ALU.mult).then_inc(s_on, 1)
            run_pipeline(dve, [(rows, 1), (tops, 0), (output, -1), (values, 0)])



def tokens_in(nc, c, name, xT, src, affine=None, gate_w=None, wts=None, scores_dram=None, shift=False, loads=()):
    with Phase(nc, name) as ph:
        hn = ph.sb("hn", [P, 2, D])
        psT = ph.ps("psT", [P, 2, 512])
        psL = ph.ps("psL", [P, 2, 512])
        psW = ph.ps("psW", [P, 4, 512])
        s_fin, s_sh, s_sum, s_ln, s_T, s_in, s_lg, s_lgo, s_r, s_e, s_wT, s_wo, s_sc, s_st, s_one = ph.semaphores(
            "fin shifted summed ln T in logits logits_out routing exp wT wT_out stored st static")
        routed = gate_w is not None
        if routed:
            hs = ph.sb("hs", [P, 2, KC, P])
            lg, sel, eq, run, run2 = (ph.sb(n, [P, NB, E]) for n in ("logits", "sel", "eq", "run", "run2"))
            top = ph.sb("top", [P, NB, 8])
            red = ph.sb("red", [P, NB])
            wT = ph.sb("wT", [E, NB, P])
        block = ph.block()

        @block.sync
        def _(sp):
            for load in loads:
                load(sp)
            if routed:
                sp.wait_ge(s_wo, 4)
                sp.dma_start(scores_dram, wT[:, :, :].rearrange("e b t -> e (b t)")).then_inc(s_sc, 16)
                sp.wait_ge(s_sc, 16)

        if routed:
            @block.gpsimd
            def _(pool):
                def keep(s):
                    pool.wait_ge(s_in, s.n + 1)
                    nc.gpsimd.tensor_copy(xT[:, :, bass.ds(s.n * P, P)], hs[:, s.p]).then_inc(s_st, 1)
                run_pipeline(pool, [(keep, 1)])

        @block.tensor
        def _(pe):
            c.wait(pe, "const")
            if affine is not None:
                c.wait(pe, affine[2])

            if shift:
                def shift_in(s):
                    after(pe, s_sh, s.n - 1, s, 2)
                    nc.tensor.matmul(psL[:, s.p, 0:P], c.shift, seq(src, s)[:, P:D], start=True, stop=True).then_inc(s_lg, 1)
                run_pipeline(pe, [(shift_in, 1)])

                def shift_again(s):
                    if isinstance(s.n, int) and s.n < 2:
                        pe.wait_ge(s_sh, NB)
                    else:
                        pe.wait_ge(s_ln, s.n * 2 - 2)
                    nc.tensor.matmul(psL[:, s.p, 0:P], c.shift, seq(src, s)[:, P:D], start=True, stop=True).then_inc(s_lg, 1)

            def turn(s):
                pe.wait_ge(s_ln, s.n * 2 + 2 if shift else s.n + 1)
                after(pe, s_in, s.n - 1, s, 2)
                for k in range(KC):
                    mm = nc.tensor.transpose(psT[:, s.p, k * P:(k + 1) * P], hn[:, s.p, k * P:(k + 1) * P], c.ident)
                mm.then_inc(s_T, 1)

            def logits(s):
                pe.wait_ge(s_in, s.n + 1)
                after(pe, s_lgo, s.n - 1, s, 2)
                for k in range(KC):
                    mm = nc.tensor.matmul(psL[:, s.p, 0:E], hs[:, s.p, k], gate_w[:, k], start=(k == 0), stop=(k == KC - 1))
                mm.then_inc(s_lg, 1)
            if shift:
                run_pipeline(pe, [(turn, 0), (shift_again, 1)])
            else:
                run_pipeline(pe, [(turn, 1)] + [(logits, 0)] * routed)
            if routed:
                pe.wait_ge(s_r, ROUTING_STEPS)
                for b in range(NB):
                    mm = nc.tensor.transpose(psW[0:E, b // 4, b % 4 * P:(b % 4 + 1) * P], sel[:, b], c.ident)
                    if b % 4 == 3:
                        mm.then_inc(s_wT, 1)

        @block.scalar
        def _(act):
            c.wait(act, "const")

            def copy_in(s):
                act.wait_ge(s_T, s.n + 1)
                if routed:
                    after(act, s_lg, s.n - 1, s, 2)
                    after(act, s_st, s.n - 1, s, 2)
                    nc.scalar.activation(hs[:, s.p].rearrange("p k t -> p (k t)"), psT[:, s.p, 0:D], ACT.Copy).then_inc(s_in, 1)
                else:
                    for k in range(KC):
                        ins = nc.scalar.activation(xT[:, k, bass.ds(s.n * P, P)], psT[:, s.p, k * P:(k + 1) * P], ACT.Identity,
                                                   scale=affine[0][:, k:k + 1], bias=affine[1][:, k:k + 1])
                    ins.then_inc(s_in, 1)
            if affine is not None:
                c.wait(act, affine[2])
            run_pipeline(act, [(copy_in, 1)])
            if routed:
                act.wait_ge(s_r, 2)
                nc.scalar.activation(lg[:, :, :], lg[:, :, :], ACT.Exp).then_inc(s_e, 1)
                for q in range(4):
                    act.wait_ge(s_wT, q + 1)
                    nc.scalar.activation(wT[:, 4 * q:4 * q + 4, :].rearrange("e b t -> e (b t)"), psW[0:E, q], ACT.Copy).then_inc(s_wo, 1)

        @block.vector
        def _(dve):
            c.wait(dve, "const")
            if shift:
                def stats(s):
                    nc.vector.bn_stats(seq(c.stats, s)[:, 0:6], seq(src, s)[:, 0:P])
                    dve.wait_ge(s_lg, s.n + 1)
                    nc.vector.bn_stats(seq(c.stats, s)[:, 6:12], psL[:, s.p, 0:P]).then_inc(s_sh, 1)
                run_pipeline(dve, [(stats, 1)])
                dve.wait_ge(s_sh, NB)
            finish_stats(nc, Chain(dve, s_fin), c, 4 if shift else 2, 1e-5)

            def rows(s):
                after(dve, s_T, s.n - 1, s, 2)
                if not shift:
                    normalize(nc, c, hn[:, s.p], seq(src, s), s).then_inc(s_ln, 1)
                    return
                normalize(nc, c, hn[:, s.p, 0:P], seq(src, s)[:, 0:P], s).then_inc(s_ln, 1)
                dve.wait_ge(s_lg, s.n + (NB + 1))
                normalize(nc, c, hn[:, s.p, P:D], psL[:, s.p, 0:P], s).then_inc(s_ln, 1)

            def logits(s):
                dve.wait_ge(s_lg, s.n + 1)
                nc.vector.tensor_copy(seq(lg, s), psL[:, s.p, 0:E]).then_inc(s_lgo, 1)
            run_pipeline(dve, [(rows, 1)] + [(logits, 0)] * routed)
            if routed:
                dve.wait_ge(s_lgo, NB)
                routing(nc, dve, Chain(dve, s_r), s_e, lg, sel, eq, run, run2, top, red)


def routing(nc, dve, link, s_e, lg, sel, eq, run, run2, top, red):
    v = nc.vector

    def per_token(t):
        return t.unsqueeze(2).broadcast_to([P, NB, E])
    link(v.tensor_reduce(red[:, :], lg[:, :, :], AXX, ALU.max))
    link(v.tensor_tensor(lg[:, :, :], lg[:, :, :], per_token(red[:, :]), ALU.subtract))
    dve.wait_ge(s_e, 1)
    link(v.tensor_reduce(red[:, :], lg[:, :, :], AXX, ALU.add))
    link(v.reciprocal(red[:, :], red[:, :]))
    link(v.tensor_tensor(lg[:, :, :], lg[:, :, :], per_token(red[:, :]), ALU.mult))
    for b in range(NB):
        link(v.max(top[:, b], lg[:, b]), wait=(b == NB - 1))
    fourth = top[:, :, TOPK - 1:TOPK].broadcast_to([P, NB, E])
    link(v.tensor_tensor(sel[:, :, :], lg[:, :, :], fourth, ALU.is_gt), wait=False)
    link(v.tensor_tensor(eq[:, :, :], lg[:, :, :], fourth, ALU.is_equal))
    link(v.tensor_reduce(red[:, :], sel[:, :, :], AXX, ALU.add), wait=False)
    a, b = eq, run
    for d in (1, 2, 4, 8):
        link(v.tensor_copy(b[:, :, 0:d], a[:, :, 0:d]), wait=False)
        link(v.tensor_tensor(b[:, :, d:E], a[:, :, d:E], a[:, :, 0:E - d], ALU.add))
        a, b = b, (run2 if b is run else run)
    link(v.tensor_tensor(b[:, :, :], a[:, :, :], per_token(red[:, :]), ALU.add))
    link(v.tensor_scalar(b[:, :, :], b[:, :, :], float(TOPK) + 0.5, None, ALU.is_lt))
    link(v.tensor_tensor(eq[:, :, :], eq[:, :, :], b[:, :, :], ALU.mult))
    link(v.tensor_tensor(sel[:, :, :], sel[:, :, :], eq[:, :, :], ALU.add))
    link(v.tensor_tensor(sel[:, :, :], sel[:, :, :], lg[:, :, :], ALU.mult))
    link(v.tensor_reduce(red[:, :], sel[:, :, :], AXX, ALU.add))
    link(v.reciprocal(red[:, :], red[:, :]))
    link(v.tensor_tensor(sel[:, :, :], sel[:, :, :], per_token(red[:, :]), ALU.mult))
    assert link.n == ROUTING_STEPS


ROUTING_STEPS = 5 + NB + 3 + 8 + 8



def units(nc, c, name, weights, xT, plan, func, gate, scores_dram=None, bias=None, row=None, state=None,
          into_x=True, loads=()):
    U = len(plan)
    assert U % 2 == 0
    scored = [u for u, (_, _, e) in enumerate(plan) if e is not None]
    last_use = {plan[u][2]: u for u in scored}
    with Phase(nc, name) as ph:
        RING = 4
        sc = ph.sb("sc", [P, RING, GT]) if scored else None
        sg = ph.sb("sg", [P, 2, GT])
        up = ph.sb("up", [P, 2, GT]) if scored and any(p[1] and p[2] is not None for p in plan) else None
        act_ = ph.sb("act", [P, 2, GT])
        yt = ph.sb("yt", [P, 2, D])
        psG, psU, psO = ph.ps("psG", [P, 2, 512]), ph.ps("psU", [P, 2, 512]), ph.ps("psO", [P, 2, 512])
        s_gu, s_sg, s_act, s_down, s_up, s_y, s_x = ph.semaphores("hidden func act down up y x")
        s_sc = [ph.sem(f"sc{r}") for r in range(RING)] if scored else []
        block = ph.block()

        def groups(eng, body):
            body(0)
            with eng.Fori(1, NG) as n:
                body(n)

        def ready(eng, sem, n, u, back):
            if isinstance(n, int):
                if n * U + u - back + 1 > 0:
                    eng.wait_ge(sem, n * U + u - back + 1)
            else:
                eng.wait_ge(sem, n * U + (u - back + 1))

        def wide(ap, n):
            return ap[:, n * GT:(n + 1) * GT] if isinstance(n, int) else ap[:, bass.ds(n * GT, GT)]

        @block.sync
        def _(sp):
            for load in loads:
                load(sp)
            if not scored:
                return

            def scores_in(n):
                for e in range(E):
                    if e >= RING:
                        ready(sp, s_act, n, last_use[e - RING], 0)
                    else:
                        ready(sp, s_act, n, last_use[e - RING + E] - U, 0)
                    sp.dma_start(sc[:, e % RING], wide(scores_dram[e:e + 1], n).rearrange("a t -> (a t)").partition_broadcast(P)) \
                      .then_inc(s_sc[e % RING], 16)
            groups(sp, scores_in)

        @block.tensor
        def _(pe):
            c.wait(pe, weights)

            def group(n):
                for u in range(U + 1):
                    if u < U:
                        at, has_up, _ = plan[u]
                        ready(pe, s_act, n, u, 2)
                        w = c.arena[:, at:at + 2 * KC * P].rearrange("p (m k i) -> p m k i", m=2, k=KC)
                        for m, ps in ((0, psG), (1, psU))[:1 + has_up]:
                            for k in range(KC):
                                mm = nc.tensor.matmul(ps[:, u % 2], w[:, m, k], wide(xT[:, k], n), start=(k == 0), stop=(k == KC - 1))
                        mm.then_inc(s_gu, 1)
                    if u:
                        at, has_up, _ = plan[u - 1]
                        down = c.arena[:, at + (1 + has_up) * D:at + (2 + has_up) * D]
                        ready(pe, s_act, n, u, 1)
                        if u == 1 and not (isinstance(n, int) and n == 0):
                            pe.wait_ge(s_x, n * TPG)
                        for j in range(TPG):
                            mm = nc.tensor.matmul(psO[:, j // 2, j % 2 * D:(j % 2 + 1) * D], act_[:, (u - 1) % 2, j * P:(j + 1) * P],
                                                  down, start=(u == 1 and j % 2 == 0), stop=(u == U), skip_group_check=True)
                        mm.then_inc(s_down, 1)
            groups(pe, group)

        @block.scalar
        def _(act):
            c.wait(act, weights)

            def group(n):
                for u in range(U):
                    ready(act, s_gu, n, u, 0)
                    ready(act, s_act, n, u, 2)
                    b = {} if bias is None else {"bias": bias[0][:, u:u + 1]}
                    nc.scalar.activation(sg[:, u % 2], psG[:, u % 2], func, **b).then_inc(s_sg, 1)
            groups(act, group)

        @block.vector
        def _(dve):
            c.wait(dve, weights)
            per = 2 if into_x else 1
            n_up = sum(1 for _, has_up, e in plan if has_up and e is not None)

            def group(n):
                ups = 0
                for u, (_, has_up, e) in enumerate(plan):
                    hidden, score = act_[:, u % 2], None
                    if e is not None:
                        score = sc[:, e % RING]
                        dve.wait_ge(s_sc[e % RING], n * (16 * E // RING) + 16 * (e // RING + 1))
                    ready(dve, s_down, n, u, 2)
                    if has_up and e is not None:
                        ready(dve, s_gu, n, u, 0)
                        nc.vector.tensor_tensor(up[:, u % 2], psU[:, u % 2], score, ALU.mult).then_inc(s_up, 1)
                        ups += 1
                        dve.wait_ge(s_up, n * n_up + ups)
                    ready(dve, s_sg, n, u, 0)
                    if has_up and bias is not None:
                        ins = nc.vector.scalar_tensor_tensor(hidden, psU[:, u % 2], bias[1][:, u:u + 1], sg[:, u % 2], ALU.add, ALU.mult)
                    elif has_up and e is None:
                        ins = nc.vector.tensor_tensor(hidden, psU[:, u % 2], sg[:, u % 2], ALU.mult)
                    elif has_up:
                        ins = nc.vector.tensor_tensor(hidden, up[:, u % 2], sg[:, u % 2], ALU.mult)
                    else:
                        ins = nc.vector.tensor_tensor(hidden, sg[:, u % 2], score, ALU.mult)
                    ins.then_inc(s_act, 1)
                ready(dve, s_down, n, U - 1, 0)
                for j in range(TPG):
                    s = Step(n * TPG + j, j % 2, None)
                    o = psO[:, j // 2, j % 2 * D:(j % 2 + 1) * D]
                    if state is None:
                        nc.vector.scalar_tensor_tensor(seq(c.X, s), o, c.gates[:, gate:gate + 1], seq(c.X, s),
                                                       ALU.mult, ALU.add).then_inc(s_x, 1)
                    else:
                        link = Chain(dve, s_y, n * (per * TPG) + per * j)
                        y = yt[:, j % 2]
                        if into_x:
                            link(nc.vector.tensor_tensor(y, o, seq(state, s), ALU.add))
                            link(nc.vector.tensor_tensor(y, y, row, ALU.add))
                            nc.vector.scalar_tensor_tensor(seq(c.X, s), y, c.gates[:, gate:gate + 1], seq(c.X, s),
                                                           ALU.mult, ALU.add).then_inc(s_x, 1)
                        else:
                            link(nc.vector.tensor_tensor(y, o, row, ALU.add))
                            nc.vector.tensor_tensor(seq(state, s), y, seq(state, s), ALU.add).then_inc(s_x, 1)
                    if into_x:
                        dve.wait_ge(s_x, n * TPG + (j + 1))
                        nc.vector.bn_stats(seq(c.stats, s)[:, 0:6], seq(c.X, s))
            groups(dve, group)



def single_attention(nc, c, Y, gate, loads=()):
    W = c.arena[:, MLP1_AT:MLP1_AT + MLP1].rearrange("p (m k n) -> p m k n", m=2, k=KC)
    b1 = c.vec1x[:, 0:COLS1X]
    gamma, beta, b2 = (c.vec1x[:, COLS1X + i * D:COLS1X + (i + 1) * D] for i in range(3))
    with Phase(nc, "L1x_attend") as ph:
        hn = ph.sb("hn", [P, 2, D])
        hT, cT = ph.sb("hT", [P, 2, KC, P]), ph.sb("cT", [P, 2, KC, P])
        cN = ph.sb("cN", [P, 2, D])
        pr, pT = ph.sb("pr", [P, 2, P]), ph.sb("pT", [P, 2, P])
        mx, sm, rs = ph.sb("mx", [P, 2]), ph.sb("sm", [P, 2]), ph.sb("rs", [P, 2])
        psT, psS, psP, psV = (ph.ps(n, [P, 2, 512]) for n in ("psT", "psS", "psP", "psV"))
        s_fin, s_ln, s_T, s_hT, s_S, s_mx, s_sub, s_exp, s_pt, s_pT, s_v, s_rs, s_y = ph.semaphores(
            "fin ln T hT S mx sub exp pt pT v rs y")
        s_ctx = [ph.sem("ctx0"), ph.sem("ctx1")]
        block = ph.block()

        @block.sync
        def _(sp):
            for load in loads:
                load(sp)

            def context_in(s):
                after(sp, s_v, s.n - 1, s, 2)
                sp.dma_start(cT[:, s.p], dram_seq(c.dram["ctxT"], s, "b p k t -> (b p) k t")).then_inc(s_ctx[s.p], 16)
                sp.dma_start(cN[:, s.p], dram_seq(c.dram["ctx"], s, "b t d -> (b t) d")).then_inc(s_ctx[s.p], 16)
            run_pipeline(sp, [(context_in, 1)])

        @block.tensor
        def _(pe):
            def scores(s):
                pe.wait_ge(s_ln, s.n + 1)
                after(pe, s_hT, s.n - 1, s, 2)
                for k in range(KC):
                    mm = nc.tensor.transpose(psT[:, s.p, k * P:(k + 1) * P], hn[:, s.p, k * P:(k + 1) * P], c.ident)
                mm.then_inc(s_T, 1)
                pe.wait_ge(s_hT, s.n + 1)
                pe.wait_ge(s_ctx[s.p], s.h * 32 + 32)
                after(pe, s_sub, s.n - 1, s, 2)
                for k in range(KC):
                    mm = nc.tensor.matmul(psS[:, s.p, 0:P], hT[:, s.p, k], cT[:, s.p, k], start=(k == 0), stop=(k == KC - 1))
                mm.then_inc(s_S, 1)

            def values(s):
                pe.wait_ge(s_exp, s.n + 1)
                after(pe, s_pT, s.n - 1, s, 2)
                nc.tensor.transpose(psP[:, s.p, 0:P], pr[:, s.p], c.ident).then_inc(s_pt, 1)
                pe.wait_ge(s_pT, s.n + 1)
                after(pe, s_y, s.n - 1, s, 2)
                nc.tensor.matmul(psV[:, s.p, 0:D], pT[:, s.p], cN[:, s.p], start=True, stop=True).then_inc(s_v, 1)
            run_pipeline(pe, [(scores, 1), (values, 0)])

        @block.scalar
        def _(act):
            def turned(s):
                act.wait_ge(s_T, s.n + 1)
                after(act, s_S, s.n - 1, s, 2)
                nc.scalar.activation(hT[:, s.p].rearrange("p k t -> p (k t)"), psT[:, s.p, 0:D], ACT.Copy).then_inc(s_hT, 1)

            def softmax(s):
                act.wait_ge(s_sub, s.n + 1)
                after(act, s_rs, s.n - 1, s, 2)
                nc.scalar.activation(pr[:, s.p], pr[:, s.p], ACT.Exp, scale=1.0 / 16, accum_out=sm[:, s.p:s.p + 1]).then_inc(s_exp, 1)
                act.wait_ge(s_pt, s.n + 1)
                after(act, s_v, s.n - 1, s, 2)
                nc.scalar.activation(pT[:, s.p], psP[:, s.p, 0:P], ACT.Copy).then_inc(s_pT, 1)
            run_pipeline(act, [(turned, 1), (softmax, 0)])

        @block.vector
        def _(dve):
            finish_stats(nc, Chain(dve, s_fin), c, 2, 1e-5)

            def rows(s):
                after(dve, s_T, s.n - 1, s, 2)
                after(dve, s_y, s.n - 1, s, 2)
                normalize(nc, c, hn[:, s.p], seq(c.X, s), s).then_inc(s_ln, 1)

            def softmax(s):
                dve.wait_ge(s_S, s.n + 1)
                after(dve, s_sub, s.n - 1, s, 2)
                nc.vector.tensor_reduce(mx[:, s.p:s.p + 1], psS[:, s.p, 0:P], AXX, ALU.max).then_inc(s_mx, 1)
                dve.wait_ge(s_mx, s.n + 1)
                after(dve, s_pt, s.n - 1, s, 2)
                nc.vector.tensor_scalar(pr[:, s.p], psS[:, s.p, 0:P], mx[:, s.p:s.p + 1], None, ALU.subtract).then_inc(s_sub, 1)

            def add(s):
                dve.wait_ge(s_v, s.n + 1)
                nc.vector.reciprocal(rs[:, s.p:s.p + 1], sm[:, s.p:s.p + 1]).then_inc(s_rs, 1)
                dve.wait_ge(s_rs, s.n + 1)
                nc.vector.scalar_tensor_tensor(seq(Y, s), psV[:, s.p, 0:D], rs[:, s.p:s.p + 1], hn[:, s.p], ALU.mult, ALU.add).then_inc(s_y, 1)
                dve.wait_ge(s_y, s.n + 1)
                nc.vector.bn_stats(seq(c.stats, s)[:, 0:6], seq(Y, s))
            run_pipeline(dve, [(add, -1), (rows, 1), (softmax, 0)])

    with Phase(nc, "L1x_mlp") as ph:
        xn, xb = ph.sb("xn", [P, 2, D]), ph.sb("xb", [P, 2, D])
        x1 = ph.sb("x1", [P, 2, D])
        x1T, h1T = ph.sb("x1T", [P, 2, KC, P]), ph.sb("h1T", [P, 2, KC, P])
        psT, psH, psO = (ph.ps(n, [P, 2, 512]) for n in ("psT", "psH", "psO"))
        s_fin, s_ln, s_g, s_x1, s_T, s_x1T, s_H, s_h1, s_o, s_y, s_st = ph.semaphores("fin ln g x1 T x1T H h1 o y st")
        block = ph.block()

        @block.gpsimd
        def _(pool):
            c.wait(pool, "L1x")

            def affine(s):
                pool.wait_ge(s_ln, s.n + 1)
                after(pool, s_T, s.n - 1, s, 2)
                nc.gpsimd.tensor_tensor(xn[:, s.p], xn[:, s.p], gamma, ALU.mult).then_inc(s_g, 1)
                pool.wait_ge(s_g, s.n + 1)
                nc.gpsimd.tensor_tensor(x1[:, s.p], xn[:, s.p], beta, ALU.add).then_inc(s_x1, 1)
                pool.wait_ge(s_x1, s.n * 2 + 1)
                after(pool, s_y, s.n - 1, s, 2)
                nc.gpsimd.tensor_tensor(xb[:, s.p], x1[:, s.p], b2, ALU.add).then_inc(s_x1, 1)
            run_pipeline(pool, [(affine, 1)])

        @block.tensor
        def _(pe):
            c.wait(pe, "L1x")

            def hidden(s):
                pe.wait_ge(s_x1, s.n * 2 + 1)
                after(pe, s_x1T, s.n - 1, s, 2)
                for k in range(KC):
                    mm = nc.tensor.transpose(psT[:, s.p, k * P:(k + 1) * P], x1[:, s.p, k * P:(k + 1) * P], c.ident)
                mm.then_inc(s_T, 1)
                pe.wait_ge(s_x1T, s.n + 1)
                after(pe, s_h1, (s.n - 1) * 2, s, 2)
                for o in range(KC):
                    for k in range(KC):
                        mm = nc.tensor.matmul(psH[:, s.p, o * P:(o + 1) * P], W[:, 0, k, o * P:(o + 1) * P], x1T[:, s.p, k],
                                              start=(k == 0), stop=(k == KC - 1))
                mm.then_inc(s_H, 1)

            def output(s):
                pe.wait_ge(s_h1, s.n * 2 + 2)
                after(pe, s_y, s.n - 1, s, 2)
                for k in range(KC):
                    mm = nc.tensor.matmul(psO[:, s.p, 0:D], h1T[:, s.p, k], W[:, 1, k], start=(k == 0), stop=(k == KC - 1))
                mm.then_inc(s_o, 1)
            run_pipeline(pe, [(hidden, 1), (output, 0)])

        @block.scalar
        def _(act):
            c.wait(act, "L1x")

            def turned(s):
                act.wait_ge(s_T, s.n + 1)
                after(act, s_H, s.n - 1, s, 2)
                nc.scalar.activation(x1T[:, s.p].rearrange("p k t -> p (k t)"), psT[:, s.p, 0:D], ACT.Copy).then_inc(s_x1T, 1)
                act.wait_ge(s_H, s.n + 1)
                after(act, s_o, s.n - 1, s, 2)
                for k in range(KC):
                    nc.scalar.activation(h1T[:, s.p, k], psH[:, s.p, k * P:(k + 1) * P], ACT.Relu, bias=b1[:, k:k + 1]).then_inc(s_h1, 1)
            run_pipeline(act, [(turned, 1)])

        @block.vector
        def _(dve):
            c.wait(dve, "L1x")
            finish_stats(nc, Chain(dve, s_fin), c, 2, 1e-6)

            def rows(s):
                after(dve, s_x1, s.n * 2 - 2, s, 2)
                normalize(nc, c, xn[:, s.p], seq(Y, s), s).then_inc(s_ln, 1)

            def add(s):
                dve.wait_ge(s_o, s.n + 1)
                dve.wait_ge(s_x1, s.n * 2 + 2)
                nc.vector.tensor_tensor(seq(Y, s), psO[:, s.p, 0:D], xb[:, s.p], ALU.add).then_inc(s_y, 1)
                dve.wait_ge(s_y, s.n + 1)
                nc.vector.bn_stats(seq(c.stats, s)[:, 0:6], seq(Y, s))
            run_pipeline(dve, [(rows, 1), (add, 0)])

    with Phase(nc, "L1x_last") as ph:
        xn = ph.sb("xn", [P, 2, D])
        x2, x3 = ph.sb("x2", [P, 2, D]), ph.sb("x3", [P, 2, D])
        s_fin, s_ln, s_g, s_b, s_x = ph.semaphores("fin ln g b x")
        block = ph.block()

        @block.gpsimd
        def _(pool):
            def affine(s):
                pool.wait_ge(s_ln, s.n + 1)
                after(pool, s_b, s.n - 1, s, 2)
                nc.gpsimd.tensor_tensor(x2[:, s.p], xn[:, s.p], gamma, ALU.mult).then_inc(s_g, 1)
                pool.wait_ge(s_g, s.n + 1)
                after(pool, s_x, s.n - 1, s, 2)
                nc.gpsimd.tensor_tensor(x3[:, s.p], x2[:, s.p], beta, ALU.add).then_inc(s_b, 1)
            run_pipeline(pool, [(affine, 1)])

        @block.vector
        def _(dve):
            finish_stats(nc, Chain(dve, s_fin), c, 2, 1e-6)

            def rows(s):
                after(dve, s_g, s.n - 1, s, 2)
                normalize(nc, c, xn[:, s.p], seq(Y, s), s).then_inc(s_ln, 1)

            def add(s):
                dve.wait_ge(s_b, s.n + 1)
                nc.vector.scalar_tensor_tensor(seq(c.X, s), x3[:, s.p], c.gates[:, gate:gate + 1], seq(c.X, s),
                                               ALU.mult, ALU.add).then_inc(s_x, 1)
                dve.wait_ge(s_x, s.n + 1)
                nc.vector.bn_stats(seq(c.stats, s)[:, 0:6], seq(c.X, s))
            run_pipeline(dve, [(rows, 1), (add, 0)])



def window_attention(nc, c, Y, layer, loads=()):
    name = f"L1f{layer}"
    base = layer * L1F
    wqkv = c.arena[:, base:base + WQKV].rearrange("p (k n) -> p k n", k=KC)
    wo = c.arena[:, base + WQKV:base + WQKV + WO1].rearrange("p (k n) -> p k n", k=INNER // P)
    scales = c.vec1f[:, layer, COLS1F + D:COLS1F + D + 2 * LD].rearrange("p (w d) -> p w d", w=2)
    HALF = LD // 2
    with Phase(nc, name + "_attend") as ph:
        hn = ph.sb("hn", [P, 2, D])
        hT = ph.sb("hT", [P, 2, KC, P])
        sq = ph.sb("sq", [P, 2 * INNER])
        ss, rn, tt = ph.sb("ss", [P, 2, 2 * LH]), ph.sb("rn", [P, 2, 2 * LH]), ph.sb("tt", [P, 2 * LH])
        root_c = ph.sb("root_c", [P, 2, 2 * LH])
        qn = ph.sb("qn", [P, 2, LH, LD])
        rot, cosd = ph.sb("rot", [P, 2, LH, LD]), ph.sb("cosd", [P, 2, LH, LD])
        qr = ph.sb("qr", [P, 2, LH, LD])
        cosT, sinT = ph.sb("cosT", [P, 2, LD]), ph.sb("sinT", [P, 2, LD])
        qT, kT = ph.sb("qT", [P, 2, 4, P]), ph.sb("kT", [P, 2, 4, P])
        vx = ph.sb("vx", [P, 2, LH, LD + 1])
        pr = ph.sb("pr", [P, 2, 2, 512])
        mx = ph.sb("mx", [P, 2, 2, 4])
        pT = ph.sb("pT", [P, 2, 512])
        rs = ph.sb("rs", [P, 2, 4])
        on, oT = ph.sb("on", [P, INNER]), ph.sb("oT", [P, 4, P])
        psQ = ph.ps("psQ", [P, 2, 512])
        psB = ph.ps("psB", [P, 2, 512])
        psS = ph.ps("psS", [P, 2, 512])
        psP = ph.ps("psP", [P, 2, 512])
        (s_fin, s_one, s_tab, s_ln, s_y, s_T, s_hT, s_qk, s_v, s_sq, s_ss, s_rn, s_qn, s_cos, s_rot, s_qr,
         s_qkT, s_qT, s_kT, s_vx, s_S, s_mx, s_sub, s_exp, s_pt, s_ptA, s_ptV, s_pv, s_rs, s_on, s_ot, s_oT,
         s_out, s_x) = ph.semaphores(
            "fin ones tab ln y T hT qk v sq ss rn qn cos rot qr qkT qT kT vx S mx sub exp pt ptA ptV pv rs on ot oT out x")
        def halves(t):
            return t[:, :, :, :].rearrange("p w h (i d) -> p w i h d", i=2)

        block = ph.block()

        @block.sync
        def _(sp):
            for load in loads:
                load(sp)

        @block.gpsimd
        def _(pool):
            nc.gpsimd.memset(vx[:, :, :, LD:LD + 1], 1.0).then_inc(s_one, 1)
            nc.gpsimd.memset(hT[:, :, 1, 0:1], 0.0).then_inc(s_one, 1)
            for i, value in enumerate((-0.5, 1.5)):
                nc.gpsimd.memset(root_c[:, i], value).then_inc(s_one, 1)
            pool.wait_ge(s_one, 4)

            def rows(s):
                if layer == 0:
                    pool.wait_ge(s_ln, s.n + 1)
                    nc.gpsimd.tensor_copy(seq(Y, s), hn[:, s.p]).then_inc(s_y, 1)
                else:
                    after(pool, s_T, s.n - 1, s, 2)
                    nc.gpsimd.tensor_copy(hn[:, s.p], seq(Y, s)).then_inc(s_y, 1)

            def roots(s):
                pool.wait_ge(s_ss, s.n * 3 + 3)
                after(pool, s_qn, s.n * 2 - 2, s, 2)
                newton_rsqrt(nc.gpsimd, Chain(pool, s_rn, s.n * NEWTON_STEPS), rn[:, s.p], ss[:, s.p], tt[:, :],
                             root_c[:, 0], root_c[:, 1])

            def rotate(s):
                pool.wait_ge(s_qn, s.n * 2 + 2)
                pool.wait_ge(s_tab, TABLE_STEPS)
                after(pool, s_qr, s.n, s, 1)
                for i, o in ((0, 1), (1, 0)):
                    nc.gpsimd.tensor_tensor(halves(rot)[:, :, i], halves(qn)[:, :, o],
                                            sinT[:, :, i * HALF:(i + 1) * HALF].unsqueeze(2).broadcast_to([P, 2, LH, HALF]),
                                            ALU.mult).then_inc(s_rot, 1)
            run_pipeline(pool, [(rows, 1), (roots, 1), (rotate, 1)])

        @block.tensor
        def _(pe):
            c.wait(pe, name)
            pe.wait_ge(s_one, 2)

            def project(s):
                pe.wait_ge(s_ln if layer == 0 else s_y, s.n + 1)
                after(pe, s_x, s.n - 1, s, 2)
                for k in range(KC):
                    mm = nc.tensor.transpose(psB[:, 1, k * P:(k + 1) * P], hn[:, s.p, k * P:(k + 1) * P], c.ident)
                mm.then_inc(s_T, 1)
                pe.wait_ge(s_hT, s.n + 1)
                after(pe, s_qn, s.n * 2, s, 1)
                for j in range(3):
                    out = psQ[:, j] if j < 2 else psB[:, 0]
                    for k in range(KC):
                        mm = nc.tensor.matmul(out, hT[:, s.p, k], wqkv[:, k, j * INNER:(j + 1) * INNER],
                                              start=(k == 0), stop=(k == KC - 1))
                    mm.then_inc(s_qk if j < 2 else s_v, 1)

            def turn(s):
                pe.wait_ge(s_qr, s.n + 1)
                after(pe, s_ptA, s.n, s, 1)
                after(pe, s_ptV, s.n, s, 1)
                for w in range(2):
                    for k in range(4):
                        mm = nc.tensor.transpose(psP[:, w, k * P:(k + 1) * P],
                                                 qr[:, w].rearrange("p h d -> p (h d)")[:, k * P:(k + 1) * P], c.ident)
                    mm.then_inc(s_qkT, 1)

            def scores(s):
                pe.wait_ge(s_qT, s.n + 1)
                pe.wait_ge(s_kT, s.n + 1)
                after(pe, s_sub, s.n * 2, s, 1)
                for r in range(2):
                    nc.tensor.matmul(psS[:, r], c.ident16[:, :], c.causal[:, :, :].rearrange("p a k -> p (a k)"),
                                     start=True, stop=False, skip_group_check=True)
                for k in range(4):
                    for r in range(2):
                        rows = slice(64 * r, 64 * r + 64)
                        mm = nc.tensor.matmul(psS[:, r, k * P:(k + 1) * P], qT[rows, s.p, k], kT[rows, s.p, k],
                                              start=False, stop=True, skip_group_check=True)
                        if k == 3:
                            mm.then_inc(s_S, 1)

            def values(s):
                for r in range(2):
                    pe.wait_ge(s_exp, s.n * 2 + r + 1)
                    if r == 0:
                        pe.wait_ge(s_kT, s.n + 1)
                    for k in range(4):
                        mm = nc.tensor.transpose(psP[:, r, k * P:(k + 1) * P], pr[:, s.p, r, k * P:(k + 1) * P], c.ident)
                    mm.then_inc(s_pt, 1)
                last = isinstance(s.n, int) and s.n == NB - 1
                for r in range(2):
                    pe.wait_ge(s_ptV if r else s_ptA, s.n + 1)
                    if r == 0:
                        pe.wait_ge(s_vx, s.n + (1 if last else 2))
                        after(pe, s_x, s.n, s, 1)
                    elif not last:
                        pe.wait_ge(s_hT, s.n + 2)
                    for k in range(4):
                        mm = nc.tensor.matmul(psB[:, r, k * 65:k * 65 + 65], pT[:, r, k * P:(k + 1) * P], vx[:, s.p, 2 * k + r],
                                              start=True, stop=True)
                    mm.then_inc(s_pv, 1)

            def output(s):
                pe.wait_ge(s_on, s.n * 2 + 2)
                for k in range(4):
                    mm = nc.tensor.transpose(psB[:, 1, k * P:(k + 1) * P], on[:, k * P:(k + 1) * P], c.ident)
                mm.then_inc(s_ot, 1)
                pe.wait_ge(s_oT, s.n + 1)
                for k in range(4):
                    mm = nc.tensor.matmul(psB[:, 0, 0:D], oT[:, k], wo[:, k], start=(k == 0), stop=(k == 3))
                mm.then_inc(s_out, 1)
            run_pipeline(pe, [(scores, 0), (output, -1), (project, 1), (values, 0), (turn, 1)])

        @block.scalar
        def _(act):
            act.wait_ge(s_one, 2)

            def project(s):
                act.wait_ge(s_T, s.n + 1)
                after(act, s_v, s.n - 1, s, 2)
                nc.scalar.activation(hT[:, s.p, 0], psB[:, 1, 0:P], ACT.Copy)
                nc.scalar.activation(hT[:, s.p, 1, 1:P], psB[:, 1, P:2 * P - 1], ACT.Copy).then_inc(s_hT, 1)
                for w in range(2):
                    act.wait_ge(s_qk, s.n * 2 + w + 1)
                    after(act, s_ss, s.n * 3, s, 1)
                    nc.scalar.activation(sq[:, w * INNER:(w + 1) * INNER], psQ[:, w], ACT.Square).then_inc(s_sq, 1)
                act.wait_ge(s_v, s.n + 1)
                after(act, s_pv, s.n * 2 - 2, s, 2)
                nc.scalar.activation(vx[:, s.p, :, 0:LD], psB[:, 0].rearrange("p (h d) -> p h d", h=LH), ACT.Copy).then_inc(s_vx, 1)

            def turn(s):
                act.wait_ge(s_qkT, s.n * 2 + 1)
                after(act, s_S, s.n * 2 - 2, s, 2)
                nc.scalar.activation(qT[:, s.p].rearrange("p k t -> p (k t)"), psP[:, 0], ACT.Copy).then_inc(s_qT, 1)

            def softmax(s):
                for r in range(2):
                    act.wait_ge(s_sub, s.n * 2 + r + 1)
                    nc.scalar.activation(pr[:, s.p, r], pr[:, s.p, r], ACT.Exp, scale=8.0).then_inc(s_exp, 1)

            def values(s):
                act.wait_ge(s_pt, s.n * 2 + 1)
                after(act, s_pv, s.n * 2 - 1, s, 1)
                nc.scalar.activation(pT[:, 0], psP[:, 0], ACT.Copy).then_inc(s_ptA, 1)

            def output(s):
                act.wait_ge(s_ot, s.n + 1)
                after(act, s_out, s.n, s, 1)
                nc.scalar.activation(oT[:, :, :].rearrange("p k t -> p (k t)"), psB[:, 1], ACT.Copy).then_inc(s_oT, 1)
            run_pipeline(act, [(softmax, 0), (output, -1), (project, 1), (values, 0), (turn, 1)])

        @block.vector
        def _(dve):
            c.wait(dve, name)
            v = nc.vector
            link = Chain(dve, s_tab)
            rope = c.rope.rearrange("p (t w d) -> p t w d", t=2, w=2)
            link(v.tensor_tensor(cosT[:, :, :], rope[:, 0], scales, ALU.mult), wait=False)
            for i, o in ((0, 1), (1, 0)):
                link(v.tensor_tensor(sinT[:, :, i * HALF:(i + 1) * HALF], rope[:, 1, :, i * HALF:(i + 1) * HALF],
                                     scales[:, :, o * HALF:(o + 1) * HALF], ALU.mult), wait=(i == 1))
            if layer == 0:
                finish_stats(nc, Chain(dve, s_fin), c, 2, 1e-5)

            def rows(s):
                if layer == 0:
                    after(dve, s_T, s.n - 1, s, 2)
                    after(dve, s_y, s.n - 1, s, 2)
                    normalize(nc, c, hn[:, s.p], seq(c.X, s), s).then_inc(s_ln, 1)

            def project(s):
                dve.wait_ge(s_sq, s.n * 2 + 2)
                after(dve, s_rn, (s.n - 1) * NEWTON_STEPS, s, 2)
                nc.vector.tensor_reduce(ss[:, s.p], sq[:, :].rearrange("p (h d) -> p h d", d=LD), AXX, ALU.add).then_inc(s_ss, 1)
                dve.wait_ge(s_ss, s.n * 3 + 1)
                nc.vector.tensor_scalar(ss[:, s.p], ss[:, s.p], 1e-24, None, ALU.max).then_inc(s_ss, 1)
                dve.wait_ge(s_ss, s.n * 3 + 2)
                after(dve, s_qn, s.n * 2 - 2, s, 2)
                guess_rsqrt(nc.vector, rn[:, s.p], ss[:, s.p]).then_inc(s_ss, 1)
                dve.wait_ge(s_rn, (s.n + 1) * NEWTON_STEPS)
                after(dve, s_rot, s.n * 2, s, 1)
                after(dve, s_qr, s.n, s, 1)
                for w in range(2):
                    nc.vector.tensor_tensor(qn[:, w], psQ[:, w].rearrange("p (h d) -> p h d", h=LH),
                                            rn[:, s.p, w * LH:(w + 1) * LH].unsqueeze(2).broadcast_to([P, LH, LD]), ALU.mult).then_inc(s_qn, 1)
                dve.wait_ge(s_qn, s.n * 2 + 2)
                nc.vector.tensor_tensor(cosd[:, :, :, :], qn[:, :, :, :], cosT[:, :, :].unsqueeze(2).broadcast_to([P, 2, LH, LD]), ALU.mult).then_inc(s_cos, 1)
                dve.wait_ge(s_rot, s.n * 2 + 2)
                dve.wait_ge(s_cos, s.n + 1)
                after(dve, s_qkT, s.n * 2, s, 1)
                nc.vector.tensor_tensor(qr[:, :, :, :], cosd[:, :, :, :], rot[:, :, :, :], ALU.add).then_inc(s_qr, 1)

            def turn(s):
                dve.wait_ge(s_qkT, s.n * 2 + 2)
                after(dve, s_S, s.n * 2 - 2, s, 2)
                nc.vector.tensor_copy(kT[:, s.p].rearrange("p k t -> p (k t)"), psP[:, 1]).then_inc(s_kT, 1)

            def softmax(s):
                after(dve, s_pt, s.n * 2 - 2, s, 2)

                def heads4(t):
                    return t.rearrange("p (h k) -> p h k", h=4)
                for r in range(2):
                    dve.wait_ge(s_S, s.n * 2 + r + 1)
                    nc.vector.tensor_reduce(mx[:, s.p, r], heads4(psS[:, r]), AXX, ALU.max).then_inc(s_mx, 1)
                for r in range(2):
                    dve.wait_ge(s_mx, s.n * 2 + r + 1)
                    nc.vector.tensor_tensor(heads4(pr[:, s.p, r]), heads4(psS[:, r]),
                                            mx[:, s.p, r].unsqueeze(2).broadcast_to([P, 4, P]), ALU.subtract).then_inc(s_sub, 1)

            def values(s):
                dve.wait_ge(s_pt, s.n * 2 + 2)
                after(dve, s_pv, s.n * 2, s, 1)
                nc.vector.tensor_copy(pT[:, 1], psP[:, 1]).then_inc(s_ptV, 1)
                dve.wait_ge(s_pv, s.n * 2 + 2)
                after(dve, s_on, s.n * 2, s, 1)
                for r in range(2):
                    o = psB[:, r, 0:260].rearrange("p (h d) -> p h d", h=4)
                    nc.vector.reciprocal(rs[:, r], o[:, :, LD]).then_inc(s_rs, 1)
                after(dve, s_ot, s.n, s, 1)
                for r in range(2):
                    o = psB[:, r, 0:260].rearrange("p (h d) -> p h d", h=4)
                    dve.wait_ge(s_rs, s.n * 2 + r + 1)
                    nc.vector.tensor_tensor(on[:, :].rearrange("p (h r d) -> p r h d", r=2, d=LD)[:, r], o[:, :, 0:LD],
                                            rs[:, r].unsqueeze(2).broadcast_to([P, 4, LD]), ALU.mult).then_inc(s_on, 1)

            def output(s):
                dve.wait_ge(s_out, s.n + 1)
                if layer == 0:
                    dve.wait_ge(s_y, s.n + 1)
                nc.vector.tensor_tensor(seq(Y, s), psB[:, 0, 0:D], seq(Y, s), ALU.add).then_inc(s_x, 1)
            run_pipeline(dve, [(softmax, 0), (output, -1), (rows, 1), (project, 1), (values, 0), (turn, 1)])


TABLE_STEPS = 3



def turn_by_phase(nc, c):
    W = c.slot[:, 0:HEADS_W].rearrange("p (m k n) -> p m k n", m=4, k=KC)
    with Phase(nc, "L3x_turn") as ph:
        ang = ph.sb("ang", [P, 8, H16])
        rows = ph.sb("rows", [P, 2, D])
        t = [ph.sb(f"t{i}", [P, KC, H16, DH // 2]) for i in range(2)]
        psT = ph.ps("psT", [P, 4, P])
        s_in, s_r, s_sin, s_T = ph.semaphores("in r sin T")
        block = ph.block()

        @block.sync
        def _(sp):
            sp.dma_start(ang[:, 0, :], c.dram["phase"].partition_broadcast(P)).then_inc(s_in, 16)
            sp.dma_start(rows[:, :, :].rearrange("p m d -> p (m d)"), c.dram["bias_L3x"].partition_broadcast(P)).then_inc(s_in, 16)

        @block.scalar
        def _(act):
            act.wait_ge(s_r, 10)
            nc.scalar.activation(ang[:, 4, :], ang[:, 2, :], ACT.Sin)
            nc.scalar.activation(ang[:, 5, :], ang[:, 3, :], ACT.Sin).then_inc(s_sin, 1)

        @block.vector
        def _(dve):
            v = nc.vector
            c.wait(dve, "L3x")
            dve.wait_ge(s_in, 32)
            link = Chain(dve, s_r)
            rounder = float(3 << 22)
            two_pi = 2 * np.pi
            p1 = 6.28125
            p2 = round((two_pi - p1) * 2 ** 21) / 2 ** 21
            p3 = two_pi - p1 - p2
            a = [ang[:, i, :] for i in range(8)]
            link(v.tensor_scalar(a[1], a[0], 1 / two_pi, rounder, ALU.mult, ALU.add))
            link(v.tensor_scalar(a[1], a[1], -rounder, None, ALU.add))
            link(v.scalar_tensor_tensor(a[2], a[1], -p1, a[0], ALU.mult, ALU.add))
            link(v.scalar_tensor_tensor(a[2], a[1], -p2, a[2], ALU.mult, ALU.add))
            link(v.scalar_tensor_tensor(a[2], a[1], -p3, a[2], ALU.mult, ALU.add))
            link(v.tensor_scalar(a[2], a[2], 3.1415925, -3.1415925, ALU.min, ALU.max))
            link(v.tensor_scalar(a[6], a[2], -1.0, None, ALU.mult))
            link(v.tensor_tensor(a[6], a[6], a[2], ALU.max))
            link(v.tensor_scalar(a[3], a[6], -1.0, np.pi / 2, ALU.mult, ALU.add))
            link(v.tensor_copy(a[7], a[3]))
            dve.wait_ge(s_sin, 1)
            sin, cos = a[4], a[5]
            for m in range(3):
                w = (W[:, m] if m < 2 else rows[:, :, :]).rearrange("p k (h i d) -> p k h i d", h=H16, i=2)
                for k in range(KC):
                    re, im = w[:, k, :, 0], w[:, k, :, 1]
                    cb, sb = (x.unsqueeze(2).broadcast_to([P, H16, DH // 2]) for x in (cos, sin))
                    link(v.tensor_tensor(t[0][:, 0], re, sb, ALU.mult), wait=False)
                    link(v.tensor_tensor(t[0][:, 1], im, sb, ALU.mult), wait=False)
                    link(v.tensor_tensor(t[1][:, 0], re, cb, ALU.mult), wait=False)
                    link(v.tensor_tensor(t[1][:, 1], im, cb, ALU.mult))
                    link(v.tensor_tensor(re, t[1][:, 0], t[0][:, 1], ALU.subtract), wait=False)
                    link(v.tensor_tensor(im, t[1][:, 1], t[0][:, 0], ALU.add))
            dve.wait_ge(s_T, 1)
            v.tensor_copy(c.slot[:, HEADS_W:HEADS_W + 4], psT[:, :, 0])

        @block.tensor
        def _(pe):
            pe.wait_ge(s_r, 10 + 36)
            for m in range(2):
                for k in range(KC):
                    mm = nc.tensor.transpose(psT[:, 2 * m + k], rows[:, m, k * P:(k + 1) * P], c.ident)
            mm.then_inc(s_T, 1)


def fourier_filter(nc, c, gate):
    with Phase(nc, "L3f") as ph:
        base = 3 * KC * D
        dft = c.arena[:, 0:base].rearrange("p (m k n) -> p m k n", m=3, k=KC)
        w = c.arena[:, base:base + 2 * KC * D].rearrange("p (m k n) -> p m k n", m=2, k=KC)
        bias = c.arena[:, base + 2 * KC * D:base + 2 * KC * D + D]
        aT = ph.sb("aT", [P, 2, KC, D])
        M = ph.sb("M", [P, KC, D])
        hn, hT = ph.sb("hn", [P, 2, D]), ph.sb("hT", [P, 2, KC, P])
        yo = ph.sb("yo", [P, 2, D])
        psA, psT, psY = ph.ps("psA", [P, 4, 512]), ph.ps("psT", [P, 2, 512]), ph.ps("psY", [P, 2, 512])
        s_fin, s_A, s_a, s_M, s_m, s_ln, s_T, s_hT, s_y, s_yo, s_x = ph.semaphores("fin A a M m ln T hT y yo x")
        block = ph.block()

        @block.tensor
        def _(pe):
            c.wait(pe, "L3f")
            for part, pairs in enumerate((((0, 0), (1, 1)), ((1, 0), (0, 2)))):
                for o in range(KC):
                    n = 0
                    for m, f in pairs:
                        for k in range(KC):
                            mm = nc.tensor.matmul(psA[:, 2 * part + o, 0:D], w[:, m, k, o * P:(o + 1) * P], dft[:, f, k],
                                                  start=(n == 0), stop=(n == 3))
                            n += 1
            mm.then_inc(s_A, 1)
            pe.wait_ge(s_a, 4)
            for o in range(KC):
                n = 0
                for part, f in ((0, 0), (1, 2)):
                    for k in range(KC):
                        mm = nc.tensor.matmul(psY[:, o, 0:D], aT[:, part, k, o * P:(o + 1) * P], dft[:, f, k],
                                              start=(n == 0), stop=(n == 3))
                        n += 1
            mm.then_inc(s_M, 1)
            pe.wait_ge(s_m, 2)

            def turn(s):
                pe.wait_ge(s_ln, s.n + 1)
                after(pe, s_hT, s.n - 1, s, 2)
                for k in range(KC):
                    mm = nc.tensor.transpose(psT[:, s.p, k * P:(k + 1) * P], hn[:, s.p, k * P:(k + 1) * P], c.ident)
                mm.then_inc(s_T, 1)

            def filtered(s):
                pe.wait_ge(s_hT, s.n + 1)
                after(pe, s_yo, s.n - 1, s, 2)
                for k in range(KC):
                    mm = nc.tensor.matmul(psY[:, s.p, 0:D], hT[:, s.p, k], M[:, k], start=(k == 0), stop=(k == KC - 1))
                mm.then_inc(s_y, 1)
            run_pipeline(pe, [(turn, 1), (filtered, 0)])

        @block.scalar
        def _(act):
            act.wait_ge(s_A, 1)
            for i in range(4):
                nc.scalar.activation(aT[:, i // 2, i % 2], psA[:, i, 0:D], ACT.Copy, scale=1.0 / D).then_inc(s_a, 1)
            act.wait_ge(s_M, 1)
            for o in range(KC):
                nc.scalar.activation(M[:, o], psY[:, o, 0:D], ACT.Copy).then_inc(s_m, 1)

            def turned(s):
                act.wait_ge(s_T, s.n + 1)
                after(act, s_y, s.n - 1, s, 2)
                nc.scalar.activation(hT[:, s.p].rearrange("p k t -> p (k t)"), psT[:, s.p, 0:D], ACT.Copy).then_inc(s_hT, 1)
            run_pipeline(act, [(turned, 1)])

        @block.vector
        def _(dve):
            c.wait(dve, "L3f")
            finish_stats(nc, Chain(dve, s_fin), c, 2, 1e-5)

            def rows(s):
                after(dve, s_T, s.n - 1, s, 2)
                normalize(nc, c, hn[:, s.p], seq(c.X, s), s).then_inc(s_ln, 1)

            def add(s):
                dve.wait_ge(s_y, s.n + 1)
                after(dve, s_x, s.n - 1, s, 2)
                nc.vector.tensor_tensor(yo[:, s.p], psY[:, s.p, 0:D], bias, ALU.add).then_inc(s_yo, 1)
                dve.wait_ge(s_yo, s.n + 1)
                nc.vector.scalar_tensor_tensor(seq(c.X, s), yo[:, s.p], c.gates[:, gate:gate + 1], seq(c.X, s),
                                               ALU.mult, ALU.add).then_inc(s_x, 1)
            run_pipeline(dve, [(rows, 1), (add, 0)])



def prepare(nc, c, d):
    with Phase(nc, "start") as ph:
        block = ph.block()

        @block.sync
        def _(sp):
            c.dma(sp, "const", c.consts[:, :], d["consts"])
            c.dma(sp, "const", c.gates[:, :], d["gates"].partition_broadcast(P))
            c.dma(sp, "const", c.gatew[:, :].rearrange("p l k e -> p (l k e)"), d["gatew"])
            c.dma(sp, "const", c.X[:, :, :], d["x"].rearrange("b p d -> p b d"))
            for n in ("L0x", "L0f", "L1x"):
                c.load(sp, n)

        @block.scalar
        def _(act):
            c.wait(act, "const")
            nc.scalar.activation(c.gates[:, :], c.gates[:, :], ACT.Tanh).then_inc(c.s_gate, 1)

        @block.vector
        def _(dve):
            c.wait(dve, "const")
            for b in range(NB):
                nc.vector.bn_stats(c.stats[:, b, 0:6], c.X[:, b, :])
            nc.vector.tensor_copy(c.ident16[:, :], c.ident)
            nc.vector.tensor_copy(c.causal[:, :], c.consts[:, C_CAUSAL:C_CAUSAL + P].unsqueeze(1).broadcast_to([P, 4, P]))


def store(nc, c, out):
    with Phase(nc, "end") as ph:
        s_out = ph.sem("stored")
        block = ph.block()

        @block.sync
        def _(sp):
            sp.dma_start(out.rearrange("b p d -> p b d"), c.X[:, :, :]).then_inc(s_out, 16)
            sp.wait_ge(s_out, 16)


def window_layers(nc, c, Y, gate):
    for layer in range(2):
        name = f"L1f{layer}"
        window_attention(nc, c, Y, layer)
        cols = c.vec1f[:, layer, 0:COLS1F]
        start = layer * L1F + WQKV + WO1
        with nc.sbuf_tensor(f"xT_{name}", [P, KC, NB * S], F32) as xT:
            tokens_in(nc, c, name + "_in", xT, Y, affine=(cols[:, 0:2], cols[:, 2:4], name), shift=True)
            units(nc, c, name + "_units", name, xT, [(start + u * UNIT_GLU, True, None) for u in range(UNITS1)], ACT.Gelu, gate,
                  bias=(cols[:, 4:4 + UNITS1], cols[:, 4 + UNITS1:]), row=c.vec1f[:, layer, COLS1F:COLS1F + D],
                  state=Y, into_x=(layer == 1))


def expert_layer(nc, c, name, gate, plan, which, loads=()):
    scores = nc.dram_tensor(f"scores_{name}", (E, NB * S), F32).ap()
    with nc.sbuf_tensor(f"xT_{name}", [P, KC, NB * S], F32) as xT:
        tokens_in(nc, c, name + "_in", xT, c.X, gate_w=c.gatew[:, which], scores_dram=scores, loads=loads)
        units(nc, c, name + "_units", name, xT, plan, ACT.Silu, gate, scores_dram=scores)


def flamingo_stack(nc, dram, out):
    with ExitStack() as ctx:
        c = Core(nc, ctx, dram)
        c.ctxT = dram["ctxT"]
        prepare(nc, c, dram)
        def loads(*names):
            return [lambda sp, n=n: c.load(sp, n) for n in names]
        heads_attention(nc, c, "L0x", 0, mask=dram["mask"])
        expert_layer(nc, c, "L0f", 1, [(e * UNIT_GLU, True, e) for e in range(E)], 0, loads("L2x"))
        with nc.sbuf_tensor("Y", [P, NB, D], F32) as Y:
            single_attention(nc, c, Y, 2, loads("L1f0", "L1f1"))
            window_layers(nc, c, Y, 3)
        heads_attention(nc, c, "L2x", 4, loads=loads("L2f"))
        shared = [(i * UNIT_GLU, True, None) for i in range(2)]
        routed = [(2 * UNIT_GLU + i * UNIT_ONE, False, i // 2) for i in range(2 * E)]
        expert_layer(nc, c, "L2f", 5, shared + routed, 1, loads("L3x"))
        turn_by_phase(nc, c)
        heads_attention(nc, c, "L3x", 6, loads=loads("L3f"))
        fourier_filter(nc, c, 7)
        store(nc, c, out)



def chunks(w):
    w = np.asarray(w)
    k = w.shape[0] // P
    return w.reshape(k, P, -1).transpose(1, 0, 2).reshape(P, -1)


def columns(v):
    return np.asarray(v).reshape(-1, P).T


def glu_unit(gate, up, down):
    m = P - gate.shape[1]
    return np.concatenate([chunks(np.pad(gate, ((0, 0), (0, m)))), chunks(np.pad(up, ((0, 0), (0, m)))),
                           np.pad(down, ((0, m), (0, 0)))], axis=1)


def constants():
    parity = (np.arange(P)[:, None] // DH % 2 == np.repeat(np.arange(2), P)[None, :])
    shift = np.eye(P, k=1)
    causal = np.where(np.arange(P)[None, :] > np.arange(P)[:, None], -1e30, 0.0)
    half = np.arange(0, LD, 2, dtype=np.float32)
    inv_freq = np.float32(1) / np.float32(10000) ** (half / np.float32(LD))
    t = np.arange(S, dtype=np.float32)
    freqs = t[:, None] * inv_freq[None, :]
    base = (half + np.float32(0.4 * LD)) / np.float32(1.4 * LD)
    scale = base[None, :] ** ((t - S // 2) / np.float32(64))[:, None]
    cos, sin = np.cos(freqs), np.sin(freqs)

    def both(a):
        return np.concatenate([a, a], axis=1)

    def signed(a):
        return np.concatenate([-a, a], axis=1)
    return np.concatenate([np.eye(P), parity, shift, causal, both(cos * scale), both(cos / scale),
                           signed(sin * scale), signed(sin / scale)], axis=1).astype(np.float32)


def layout(i):
    f = {k: np.asarray(v) for k, v in i.items()}
    zero = np.zeros(D, np.float32)

    def heads(q, k, v, o, bq, bk, bv):
        return np.concatenate([chunks(q), chunks(k), chunks(v), chunks(o), columns(bq), columns(bk), columns(bv)], axis=1)
    d = {
        "consts": constants(),
        "x": f["x"],
        "ctxT": f["ctx_1024"].transpose(0, 2, 1).reshape(NB, KC, P, S).transpose(0, 2, 1, 3),
        "ctx": f["ctx_1024"],
        "mask": f["mask_Bx1xSxS2_ik1"][:, 0],
        "gates": np.stack([f["g_xattn"], f["g_ffn"]], axis=1).reshape(8),
        "gatew": np.concatenate([chunks(f["L0_ffn_gate_w"].T), chunks(f["L2_ffn_gate_w"].T)], axis=1),
        "w_L0x": heads(f["L0_xattn_W_q"].T, f["L0_xattn_W_k"].T, f["L0_xattn_W_v"].T, f["L0_xattn_W_o"].T,
                       f["L0_xattn_b_q"], f["L0_xattn_b_k"], f["L0_xattn_b_v"]),
        "row_L0x": f["L0_xattn_b_o"],
        "w_L2x": heads(f["L2_xattn_W_q"], f["L2_xattn_W_kv"][:, :D], f["L2_xattn_W_kv"][:, D:], f["L2_xattn_W_proj"],
                       zero, zero, zero),
        "row_L2x": f["L2_xattn_b_proj"],
        "w_L3x": heads(f["L3_xattn_Wq"].T, f["L3_xattn_Wk"].T, f["L3_xattn_Wv"].T, f["L3_xattn_Wo"].T,
                       f["L3_xattn_bq"], f["L3_xattn_bk"], f["L3_xattn_bv"]),
        "row_L3x": f["L3_xattn_bo"],
        "phase": f["L3_xattn_phase"].reshape(-1),
        "bias_L3x": np.concatenate([f["L3_xattn_bq"], f["L3_xattn_bk"]]),
        "w_L0f": np.concatenate([glu_unit(f["L0_ffn_w1"][e], f["L0_ffn_w3"][e], f["L0_ffn_w2"][e]) for e in range(E)], axis=1),
        "w_L1x": np.concatenate([chunks(f["L1_xattn_W1"]), chunks(f["L1_xattn_W2"])], axis=1),
        "col_L1x": columns(f["L1_xattn_b1"]),
        "row_L1x": np.concatenate([f["L1_xattn_gamma"], f["L1_xattn_beta"], f["L1_xattn_b2"]]),
    }
    for n in range(2):
        w1, b1, w2 = f["L1_ffn_w1"][n], f["L1_ffn_b1"][n], f["L1_ffn_w2"][n]
        cuts = [(a, min(a + P, HID)) for a in range(0, HID, P)]
        pad = UNITS1 * P - HID
        d[f"w_L1f{n}"] = np.concatenate(
            [chunks(f["L1_ffn_wqkv"][n]), chunks(f["L1_ffn_wo"][n])]
            + [glu_unit(w1[:, HID + a:HID + b], w1[:, a:b], w2[a:b]) for a, b in cuts], axis=1)
        d[f"col_L1f{n}"] = np.concatenate([columns(f["L1_ffn_ln_g"][n]), columns(f["L1_ffn_ln_b"][n]),
                                           columns(np.pad(b1[HID:], (0, pad))), columns(np.pad(b1[:HID], (0, pad)))], axis=1)
        d[f"row_L1f{n}"] = np.concatenate([f["L1_ffn_b2"][n], f["L1_ffn_q_scale"][n], f["L1_ffn_k_scale"][n]])
    gu, down = f["L2_ffn_shared_gu"].T, f["L2_ffn_shared_down"].T
    units = [glu_unit(gu[:, a:a + P], gu[:, D + a:D + a + P], down[a:a + P]) for a in range(0, D, P)]
    for e in range(E):
        up, down = f["L2_ffn_w1"][e].T, f["L2_ffn_w2"][e].T
        units += [np.concatenate([chunks(up[:, a:a + P]), down[a:a + P]], axis=1) for a in range(0, D, P)]
    d["w_L2f"] = np.concatenate(units, axis=1)
    angle = 2 * np.pi * (np.outer(np.arange(D), np.arange(D)) % D) / D
    cos, sin = np.cos(angle).astype(np.float32), np.sin(angle).astype(np.float32)
    d["dft"] = np.concatenate([chunks(cos), chunks(sin), chunks(-sin)], axis=1)
    d["w_L3f"] = np.concatenate([chunks(f["L3_ffn_w_freq_real"]), chunks(f["L3_ffn_w_freq_imag"])], axis=1)
    d["row_L3f"] = f["L3_ffn_bias"]
    return {k: np.ascontiguousarray(v) for k, v in d.items()}


def kernel(**inputs):
    import concourse.bacc as bacc
    from concourse.bass_utils import run_bass_kernel_spmd

    nc = bacc.Bacc("TRN2", target_bir_lowering=False, num_devices=1)
    arrays = layout(inputs)
    dram = {k: nc.dram_tensor(f"in_{k}", v.shape, mybir.dt.from_np(v.dtype), kind="ExternalInput").ap()
            for k, v in arrays.items()}
    out = nc.dram_tensor("out_x", (NB, S, D), F32, kind="ExternalOutput").ap()
    flamingo_stack(nc, dram, out)
    r = run_bass_kernel_spmd(nc, [{f"in_{k}": v for k, v in arrays.items()}], core_ids=[0])
    return r.results[0]["out_x"]
```

```python
from contextlib import ExitStack

import numpy as np
import concourse.bass as bass
from concourse import mybir

P = 128
NB, S, D = 16, 128, 256
KC = D // P
E, TOPK = 16, 4
GT = 512
NG = NB * S // GT
TPG = GT // P
H16, DH = 16, 16
LH, LD = 8, 64
INNER = LH * LD
HID = int(D * 4 * 2 / 3)

F32 = mybir.dt.float32
BF16 = mybir.dt.bfloat16
I32 = mybir.dt.int32
ALU = mybir.AluOpType
ACT = mybir.ActivationFunctionType
AXX = mybir.AxisListType.X

UNIT_GLU, UNIT_ONE = 3 * D, 2 * D
L0F = E * UNIT_GLU
UNITS1 = -(-HID // P)
WQKV, WO1 = KC * 3 * INNER, INNER // P * D
L1F = WQKV + WO1 + UNITS1 * UNIT_GLU
L2F = 2 * UNIT_GLU + 2 * E * UNIT_ONE
MLP1 = 2 * KC * D
ARENA = 2 * L1F + MLP1
MLP1_AT = 2 * L1F
assert L2F <= ARENA and L0F <= MLP1_AT
HEADS_W = 4 * KC * D
SLOT = HEADS_W + 6 + D
C_IDENT, C_PARITY, C_SHIFT, C_CAUSAL, C_ROPE = 0, P, 3 * P, 4 * P, 5 * P
CONSTS = C_ROPE + 4 * LD
COLS1X, ROWS1X = 3 * KC, 3 * D
COLS1F, ROWS1F = 2 * KC + 2 * UNITS1, D + 2 * LD


class Step:

    def __init__(self, n, parity, half):
        self.n, self.p, self.h = n, parity, half


def run_pipeline(eng, pieces, count=NB):
    low, high = min(off for _, off in pieces), max(off for _, off in pieces)

    def step(t, i=None):
        for fn, off in pieces:
            n = t + off
            if i is not None:
                fn(Step(i * 2 + n, n % 2, i + n // 2))
            elif 0 <= n < count:
                fn(Step(n, n % 2, n // 2))
    first = 2 - low
    rounds = (count - high - first) // 2
    for t in range(-high, first):
        step(t)
    with eng.Fori(0, rounds) as i:
        step(first, i)
        step(first + 1, i)
    for t in range(first + 2 * rounds, count - low):
        step(t)


def seq_chunk(t, s, k):
    if isinstance(s.n, int):
        return t[:, s.n, k, :]
    return t[:, bass.ds(s.n, 1), k, :].rearrange("p a d -> p (a d)")


def at(fn, g):
    return lambda s: fn(s, g)


def after(eng, sem, value, s=None, first=0):
    if s is not None and isinstance(s.n, int) and s.n < first:
        return
    if isinstance(value, int) and value <= 0:
        return
    eng.wait_ge(sem, value)


def last(s):
    return isinstance(s.n, int) and s.n == NB - 1


def seq(t, s):
    if isinstance(s.n, int):
        return t[:, s.n, :]
    return t[:, bass.ds(s.n, 1), :].rearrange("p a d -> p (a d)")


class Phase:

    def __init__(self, nc, name):
        self.nc, self.name, self.sems = nc, name, []
        self.ctx, self.work = ExitStack(), ExitStack()

    def __enter__(self):
        return self

    def sb(self, name, shape, dt=F32):
        return self.ctx.enter_context(self.nc.sbuf_tensor(f"{self.name}_{name}", shape, dt))

    def ps(self, name, shape, dt=F32):
        return self.ctx.enter_context(self.nc.psum_tensor(f"{self.name}_{name}", shape, dt))

    def sem(self, name):
        s = self.ctx.enter_context(self.nc.semaphore(f"{self.name}_{name}"))
        self.sems.append(s)
        return s

    def semaphores(self, names):
        return [self.sem(n) for n in names.split()]

    def block(self):
        return self.work.enter_context(self.nc.Block())

    def __exit__(self, kind, *rest):
        if kind is None:
            self.work.close()
            for s in self.sems:
                self.nc.gpsimd.sem_clear(s)
            self.nc.all_engine_barrier()
            self.ctx.close()


class Core:

    def __init__(self, nc, ctx, dram):
        self.nc, self.dram = nc, dram

        def sb(name, shape, dt=F32):
            return ctx.enter_context(nc.sbuf_tensor(name, shape, dt))
        self.X = sb("X", [P, NB, D])
        self.slot = sb("slot", [P, SLOT])
        self.arena = sb("arena", [P, ARENA])
        self.consts = sb("consts", [P, CONSTS])
        self.gates = sb("gates", [P, 8])
        self.stats = sb("stats", [P, NB, 12])
        self.mean, self.rstd, self.var, self.tmp = (sb(n, [P, NB]) for n in ("mean", "rstd", "var", "tmp"))
        self.dev = sb("dev", [P, NB, 4])
        self.causal = sb("causal", [P, 4, P], BF16)
        self.ident16 = sb("ident16", [P, P], BF16)
        self.gatew = sb("gatew", [P, 2, KC, E])
        self.vec1x = sb("vec1x", [P, COLS1X + ROWS1X])
        self.vec1f = sb("vec1f", [P, 2, COLS1F + ROWS1F])
        self.ident = self.consts[:, C_IDENT:C_IDENT + P]
        self.parity = self.consts[:, C_PARITY:C_SHIFT].rearrange("p (e t) -> p e t", e=2)
        self.shift = self.consts[:, C_SHIFT:C_SHIFT + P]
        self.rope = self.consts[:, C_ROPE:C_ROPE + 4 * LD]
        names = ["const", "L0x", "L0f", "L1x", "L1f0", "L1f1", "L2x", "L2f", "L3x", "L3f", "ctx"]
        self.loaded = {n: ctx.enter_context(nc.semaphore(f"loaded_{n}")) for n in names}
        self.s_gate = ctx.enter_context(nc.semaphore("gates_ready"))

    def dma(self, eng, name, dst, src):
        eng.dma_start(dst, src).then_inc(self.loaded[name], 16)

    def load(self, eng, name):
        d = self.dram
        if name in ("L0x", "L2x", "L3x"):
            self.dma(eng, name, self.slot[:, 0:HEADS_W + 6], d[f"w_{name}"])
            self.dma(eng, name, self.slot[:, HEADS_W + 6:SLOT], d[f"row_{name}"].partition_broadcast(P))
        elif name in ("L0f", "L2f"):
            n = L0F if name == "L0f" else L2F
            for a in range(0, n, n // 4):
                self.dma(eng, name, self.arena[:, a:a + n // 4], d[f"w_{name}"][:, a:a + n // 4])
        elif name == "L1x":
            self.dma(eng, name, self.arena[:, MLP1_AT:MLP1_AT + MLP1], d["w_L1x"])
            self.dma(eng, name, self.vec1x[:, 0:COLS1X], d["col_L1x"])
            self.dma(eng, name, self.vec1x[:, COLS1X:], d["row_L1x"].partition_broadcast(P))
        elif name == "ctx":
            for b in range(0, NB, NB // 4):
                some = slice(b, b + NB // 4)
                self.dma(eng, name, self.ctxT[:, some], d["ctxT"][some].rearrange("b p k t -> p b k t"))
                self.dma(eng, name, self.ctx[:, some], d["ctx"][some].rearrange("b t d -> t b d"))
        elif name == "L3f":
            self.dma(eng, name, self.arena[:, 0:3 * KC * D], d["dft"])
            self.dma(eng, name, self.arena[:, 3 * KC * D:5 * KC * D], d["w_L3f"])
            self.dma(eng, name, self.arena[:, 5 * KC * D:5 * KC * D + D], d["row_L3f"].partition_broadcast(P))
        else:
            i = int(name[-1])
            self.dma(eng, name, self.arena[:, i * L1F:(i + 1) * L1F], d[f"w_{name}"])
            self.dma(eng, name, self.vec1f[:, i, 0:COLS1F], d[f"col_{name}"])
            self.dma(eng, name, self.vec1f[:, i, COLS1F:], d[f"row_{name}"].partition_broadcast(P))

    def wait(self, eng, name):
        n = {"L0x": 2, "L2x": 2, "L3x": 2, "L0f": 4, "L2f": 4, "const": 4, "ctx": 8}.get(name, 3)
        eng.wait_ge(self.loaded[name], 16 * n)


class Chain:

    def __init__(self, eng, sem, base=0):
        self.eng, self.sem, self.base, self.n = eng, sem, base, 0

    def __call__(self, ins, wait=True):
        ins.then_inc(self.sem, 1)
        self.n += 1
        if wait:
            self.eng.wait_ge(self.sem, self.base + self.n)


MAGIC = float(0x5F3759DF)


def guess_rsqrt(vec, y, v):
    return vec.tensor_scalar(y.bitcast(I32), v.bitcast(I32), -0.5, MAGIC, ALU.mult, ALU.add)


def rsqrt(vec, link, y, v, t):
    link(guess_rsqrt(vec, y, v))
    for _ in range(3):
        link(vec.tensor_tensor(t, y, y, ALU.mult))
        link(vec.tensor_tensor(t, t, v, ALU.mult))
        link(vec.tensor_scalar(t, t, -0.5, 1.5, ALU.mult, ALU.add))
        link(vec.tensor_tensor(y, y, t, ALU.mult))


NEWTON_STEPS = 13


def newton_rsqrt(pool, link, y, v, t, half, three_halves):
    link(pool.tensor_tensor(v, v, half, ALU.mult))
    for _ in range(3):
        link(pool.tensor_tensor(t, y, y, ALU.mult))
        link(pool.tensor_tensor(t, t, v, ALU.mult))
        link(pool.tensor_tensor(t, t, three_halves, ALU.add))
        link(pool.tensor_tensor(y, y, t, ALU.mult))


def finish_stats(nc, link, c, groups, eps):
    v = nc.vector
    parts = c.stats[:, :, 0:3 * groups].rearrange("p b (g s) -> p b g s", s=3)
    means, m2 = parts[:, :, :, 1], parts[:, :, :, 2]
    dev, var, t = c.dev[:, :, 0:groups], c.var[:, :], c.tmp[:, :]
    link(v.tensor_reduce(c.mean[:, :], means, AXX, ALU.add))
    link(v.tensor_scalar(c.mean[:, :], c.mean[:, :], 1.0 / groups, None, ALU.mult))
    link(v.tensor_tensor(dev, means, c.mean[:, :].unsqueeze(2).broadcast_to([P, NB, groups]), ALU.subtract))
    link(v.tensor_tensor(dev, dev, dev, ALU.mult))
    link(v.tensor_reduce(t, dev, AXX, ALU.add))
    link(v.tensor_reduce(var, m2, AXX, ALU.add))
    link(v.tensor_scalar(var, var, 1.0 / D, eps, ALU.mult, ALU.add))
    link(v.scalar_tensor_tensor(var, t, 1.0 / groups, var, ALU.mult, ALU.add))
    rsqrt(v, link, c.rstd[:, :], var, t)


def normalize(nc, c, dst, src, s):
    return nc.vector.tensor_scalar(dst, src, per_seq(c.mean, s), per_seq(c.rstd, s), ALU.subtract, ALU.mult)


def dram_seq(t, s, form):
    return t[s.n] if isinstance(s.n, int) else t[bass.ds(s.n, 1)].rearrange(form)


def per_seq(t, s):
    return t[:, s.n:s.n + 1] if isinstance(s.n, int) else t[:, bass.ds(s.n, 1)]



def heads_attention(nc, c, name, gate, mask=None, loads=()):
    with Phase(nc, name) as ph:
        W = c.slot[:, 0:HEADS_W].rearrange("p (m k n) -> p m k n", m=4, k=KC)
        wq, wk, wv, wo = W[:, 0], W[:, 1], W[:, 2], W[:, 3]
        cols = c.slot[:, HEADS_W:HEADS_W + 6]
        bq, bk, bv, bo = cols[:, 0:2], cols[:, 2:4], cols[:, 4:6], c.slot[:, HEADS_W + 6:SLOT]

        hn = ph.sb("hn", [P, 2, D])
        hT, cT, qT, kc = (ph.sb(n, [P, 2, KC, P]) for n in ("hT", "cT", "qT", "kc"))
        kEO = ph.sb("kEO", [P, 2, KC, 2, P])
        vx = ph.sb("vx", [P, 2, KC, 8 * (P + DH)])
        pr = ph.sb("pr", [P, 2, 4, 512])
        nmx = ph.sb("nmx", [P, 2, H16])
        pT = ph.sb("pT", [P, 2, 512])
        sums, rs = ph.sb("sums", [P, 2, H16]), ph.sb("rs", [P, 2, H16])
        oT = ph.sb("oT", [P, KC, P])
        gbo = ph.sb("gbo", [P, D])
        bq4 = ph.sb("bq4", [P, KC])
        if mask is not None:
            mi = ph.sb("mi", [P, NB, P], I32)
            cap = ph.sb("cap", [P, NB, P])
            sm = ph.sb("sm", [P, 2, 4, 512])
        psS = ph.ps("psS", [P, 4, 512])
        psP = ph.ps("psP", [P, 2, 512])
        psO = ph.ps("psO", [P, 512])
        psQ = ph.ps("psQ", [P, 512])

        s_ctx = [ph.sem("ctx0"), ph.sem("ctx1")]
        (s_zero, s_fin, s_mi, s_cap, s_bias, s_ln, s_T, s_hT, s_K, s_kc, s_k, s_Q, s_q, s_V, s_vx, s_S, s_min, s_mx,
         s_exp, s_rs, s_pr, s_pt, s_pT0, s_pT1, s_pv, s_oT, s_out, s_xb, s_x) = ph.semaphores(
            "zero fin mask cap bias ln T hT K kc k Q q V vx S min mx exp rs pr pt pT0 pT1 pv oT out xb x")
        block = ph.block()

        @block.sync
        def _(sp):
            if mask is not None:
                sp.dma_start(mi[:, :, :], mask.rearrange("b q k -> q b k")).then_inc(s_mi, 16)
            for load in loads:
                load(sp)

            def context_in(s):
                after(sp, s_V, s.n - 1, s, 2)
                after(sp, s_K, s.n - 1, s, 2)
                sp.dma_start(cT[:, s.p], dram_seq(c.dram["ctxT"], s, "b p k t -> (b p) k t")).then_inc(s_ctx[s.p], 16)
            run_pipeline(sp, [(context_in, 1)])

        @block.gpsimd
        def _(pool):
            nc.gpsimd.memset(vx[:, :, :, :], 0.0).then_inc(s_zero, 1)
            c.wait(pool, name)
            pool.wait_ge(c.s_gate, 1)
            nc.gpsimd.tensor_scalar(gbo[:, :], bo, c.gates[:, gate:gate + 1], None, ALU.mult).then_inc(s_bias, 1)
            pool.wait_ge(s_bias, 1)

            def keys(s):
                pool.wait_ge(s_kc, s.n + 1)
                after(pool, s_S, (s.n - 1) * 4, s, 2)
                for eo in range(2):
                    nc.gpsimd.tensor_tensor(kEO[:, s.p, :, eo], kc[:, s.p], c.parity[:, eo, :].unsqueeze(1).broadcast_to([P, KC, P]),
                                            ALU.mult).then_inc(s_k, 1)

            def output_bias(s):
                pool.wait_ge(s_ln, s.n + 1)
                nc.gpsimd.tensor_tensor(seq(c.X, s), seq(c.X, s), gbo[:, :], ALU.add).then_inc(s_xb, 1)

            def divide(s, g):
                pool.wait_ge(s_rs, s.n * 2 + g // 2 + 1)
                heads = pr[:, s.p, g].rearrange("p (h k) -> p h k", h=4)
                nc.gpsimd.tensor_tensor(heads, heads, rs[:, s.p, 4 * g:4 * g + 4].unsqueeze(2).broadcast_to([P, 4, P]),
                                        ALU.mult).then_inc(s_pr, 1)
            run_pipeline(pool, [(output_bias, 0), (at(divide, 0), 0), (at(divide, 1), 0), (at(divide, 2), 0), (keys, 1),
                                (at(divide, 3), 0)])

        @block.tensor
        def _(pe):
            c.wait(pe, name)
            c.wait(pe, "const")

            def scores(s, g):
                if g == 0:
                    pe.wait_ge(s_k, s.n * 2 + 2)
                    pe.wait_ge(s_q, s.n + 1)
                r = slice(32 * g, 32 * g + 32)
                after(pe, s_exp if mask is None else s_min, s.n * 4 - (3 - g), s, 1)
                for k in range(KC):
                    mm = nc.tensor.matmul(psS[:, g, k * 256:(k + 1) * 256], qT[r, s.p, k], kEO[r, s.p, k],
                                          start=True, stop=True)
                mm.then_inc(s_S, 1)

            def turn_in(s):
                pe.wait_ge(s_ln, s.n + 1)
                after(pe, s_q, s.n, s, 1)
                for k in range(KC):
                    mm = nc.tensor.transpose(psQ[:, k * P:(k + 1) * P], hn[:, s.p, k * P:(k + 1) * P], c.ident)
                mm.then_inc(s_T, 1)

            def values_in(s):
                after(pe, s_pT1, s.n * 2 - 2, s, 2)
                for k in range(KC):
                    mm = nc.tensor.matmul(psP[:, 1, 0:D], cT[:, s.p, k], wv[:, k], start=(k == 0), stop=(k == KC - 1))
                mm.then_inc(s_V, 1)

            def output(s):
                pe.wait_ge(s_oT, s.n * 2 + 2)
                for k in range(KC):
                    mm = nc.tensor.matmul(psO[:, 0:D], oT[:, k], wo[:, k], start=(k == 0), stop=(k == KC - 1))
                mm.then_inc(s_out, 1)

            def project(w, rhs, base, s, done):
                for o in range(KC):
                    for k in range(KC):
                        mm = nc.tensor.matmul(psQ[:, base + o * P:base + (o + 1) * P], w[:, k, o * P:(o + 1) * P],
                                              rhs[:, s.p, k], start=(k == 0), stop=(k == KC - 1))
                mm.then_inc(done, 1)

            def keys(s):
                pe.wait_ge(s_ctx[s.p], s.h * 16 + 16)
                pe.wait_ge(s_hT, s.n + 1)
                project(wk, cT, D, s, s_K)

            def queries(s):
                pe.wait_ge(s_kc, s.n + 1)
                project(wq, hT, 0, s, s_Q)

            def turn(s, g):
                pe.wait_ge(s_pr, s.n * 4 + g + 1)
                if g == 1:
                    pe.wait_ge(s_vx, s.n + (1 if last(s) else 2))
                if g == 0:
                    after(pe, s_pT0, s.n * 2, s, 1)
                if g > 1:
                    pe.wait_ge(s_pT1 if g % 2 else s_pT0, s.n * 2 + 1)
                for j in range(4):
                    mm = nc.tensor.transpose(psP[:, g % 2, j * P:(j + 1) * P], pr[:, s.p, g, j * P:(j + 1) * P], c.ident)
                mm.then_inc(s_pt, 1)

            def weigh(s, g):
                pe.wait_ge(s_pT1 if g % 2 else s_pT0, s.n * 2 + g // 2 + 1)
                if g == 0:
                    after(pe, s_x, s.n, s, 1)
                for j in range(4):
                    k, h = j // 2, 2 * g + j % 2
                    mm = nc.tensor.matmul(psO[:, k * P:(k + 1) * P], vx[:, s.p, k, h * P:(h + 1) * P],
                                          pT[:, g % 2, j * P:(j + 1) * P], start=(g == 0 and j == 0), stop=(g == 3),
                                          skip_group_check=True)
                mm.then_inc(s_pv, 1)

            run_pipeline(pe, [(at(scores, 0), 0), (at(turn, 0), -1), (at(scores, 1), 0), (at(turn, 1), -1), (at(weigh, 0), -1),
                              (at(scores, 2), 0), (at(turn, 2), -1), (at(weigh, 1), -1), (at(scores, 3), 0), (turn_in, 1),
                              (at(turn, 3), -1), (at(weigh, 2), -1), (keys, 1), (at(weigh, 3), -1), (queries, 1),
                              (values_in, 1), (output, -1)])

        @block.scalar
        def _(act):
            c.wait(act, name)
            c.wait(act, "const")
            act.wait_ge(s_zero, 1)
            nc.scalar.activation(bq4[:, :], bq, ACT.Copy, scale=0.25).then_inc(s_bias, 1)
            act.wait_ge(s_bias, 2)

            def exps(s, g):
                act.wait_ge(s_mx, s.n * 4 + g + 1)
                if g == 0:
                    after(act, s_pt, s.n * 4 - 4, s, 2)
                    after(act, s_rs, s.n * 2 - 2, s, 2)
                src = psS[:, g] if mask is None else sm[:, s.p, g]
                for j in range(4):
                    ins = nc.scalar.activation(pr[:, s.p, g, j * P:(j + 1) * P], src[:, j * P:(j + 1) * P], ACT.Exp,
                                               bias=nmx[:, s.p, 4 * g + j:4 * g + j + 1],
                                               accum_out=sums[:, s.p, 4 * g + j:4 * g + j + 1])
                ins.then_inc(s_exp, 1)

            def output(s):
                act.wait_ge(s_pv, s.n * 4 + 4)
                after(act, s_out, s.n, s, 1)
                for k in range(KC):
                    nc.scalar.activation(oT[:, k], psO[:, k * P:(k + 1) * P], ACT.Identity,
                                         bias=bv[:, k:k + 1]).then_inc(s_oT, 1)

            def rows(s):
                act.wait_ge(s_T, s.n + 1)
                after(act, s_Q, s.n - 1, s, 2)
                nc.scalar.activation(hT[:, s.p].rearrange("p k t -> p (k t)"), psQ[:, 0:D], ACT.Copy).then_inc(s_hT, 1)

            def values_in(s):
                act.wait_ge(s_V, s.n + 1)
                after(act, s_pv, s.n * 4 - 4, s, 2)
                nc.scalar.activation(vx[:, s.p].rearrange("p k (h e) -> p k h e", h=8)[:, :, :, 0:DH],
                                     psP[:, 1, 0:D].rearrange("p (k h d) -> p k h d", k=KC, h=8), ACT.Copy).then_inc(s_vx, 1)

            def keys(s):
                act.wait_ge(s_K, s.n + 1)
                after(act, s_k, s.n * 2 - 2, s, 2)
                for k in range(KC):
                    ins = nc.scalar.activation(kc[:, s.p, k], psQ[:, D + k * P:D + (k + 1) * P], ACT.Identity, bias=bk[:, k:k + 1])
                ins.then_inc(s_kc, 1)

            def queries(s):
                act.wait_ge(s_Q, s.n + 1)
                after(act, s_S, s.n * 4 - 4, s, 2)
                for k in range(KC):
                    ins = nc.scalar.activation(qT[:, s.p, k], psQ[:, k * P:(k + 1) * P], ACT.Identity, scale=DH ** -0.5,
                                               bias=bq4[:, k:k + 1])
                ins.then_inc(s_q, 1)

            def turned(s, g):
                act.wait_ge(s_pt, s.n * 4 + g + 1)
                if g == 1:
                    after(act, s_pv, s.n * 4, s, 1)
                else:
                    act.wait_ge(s_pv, s.n * 4 + 2)
                nc.scalar.activation(pT[:, 1], psP[:, 1], ACT.Copy).then_inc(s_pT1, 1)

            run_pipeline(act, [(at(exps, 0), 0), (at(turned, 1), -1), (at(exps, 1), 0), (at(exps, 2), 0), (rows, 1),
                               (at(turned, 3), -1), (at(exps, 3), 0), (keys, 1), (output, -1), (queries, 1), (values_in, 1)])

        @block.vector
        def _(dve):
            c.wait(dve, name)
            c.wait(dve, "const")
            dve.wait_ge(c.s_gate, 1)
            finish_stats(nc, Chain(dve, s_fin), c, 2, 1e-5)
            if mask is not None:
                dve.wait_ge(s_mi, 16)
                huge = sm[:, 0].rearrange("p g (h k) -> p (g h) k", k=P)
                link = Chain(dve, s_cap)
                link(nc.vector.tensor_scalar(huge, mi[:, :, :], 0.0, 3e38, ALU.not_equal, ALU.mult), wait=False)
                link(nc.vector.tensor_scalar(cap[:, :, :], mi[:, :, :], 0.0, -1e9, ALU.is_equal, ALU.mult))
                link(nc.vector.tensor_tensor(cap[:, :, :], cap[:, :, :], huge, ALU.add))

            def heads4(t):
                return t.rearrange("p (h k) -> p h k", h=4)

            def rows(s):
                after(dve, s_T, s.n - 1, s, 2)
                normalize(nc, c, hn[:, s.p], seq(c.X, s), s).then_inc(s_ln, 1)

            def tops(s, g):
                if g == 0:
                    after(dve, s_exp, s.n * 4 - 4, s, 2)
                dve.wait_ge(s_S, s.n * 4 + g + 1)
                src = psS[:, g]
                if mask is not None:
                    src = sm[:, s.p, g]
                    nc.vector.tensor_tensor(heads4(src), heads4(psS[:, g]),
                                            seq(cap, s).unsqueeze(1).broadcast_to([P, 4, P]), ALU.min).then_inc(s_min, 1)
                    dve.wait_ge(s_min, s.n * 4 + g + 1)
                nc.vector.tensor_reduce(nmx[:, s.p, 4 * g:4 * g + 4], heads4(src), AXX, ALU.max, negate=True).then_inc(s_mx, 1)

            def output(s):
                dve.wait_ge(s_out, s.n + 1)
                dve.wait_ge(s_xb, s.n + 1)
                nc.vector.scalar_tensor_tensor(seq(c.X, s), psO[:, 0:D], c.gates[:, gate:gate + 1], seq(c.X, s),
                                               ALU.mult, ALU.add).then_inc(s_x, 1)
                dve.wait_ge(s_x, s.n + 1)
                nc.vector.bn_stats(seq(c.stats, s)[:, 0:6], seq(c.X, s))

            def turned(s, g):
                dve.wait_ge(s_pt, s.n * 4 + g + 1)
                if g:
                    dve.wait_ge(s_pv, s.n * 4 + 1)
                else:
                    after(dve, s_pv, s.n * 4 - 1, s, 1)
                nc.vector.tensor_copy(pT[:, 0], psP[:, 0]).then_inc(s_pT0, 1)

            def sums_of(s, half):
                dve.wait_ge(s_exp, s.n * 4 + 2 * half + 2)
                after(dve, s_pr, s.n * 4 - 4, s, 2)
                heads = slice(8 * half, 8 * half + 8)
                nc.vector.reciprocal(rs[:, s.p, heads], sums[:, s.p, heads]).then_inc(s_rs, 1)
            run_pipeline(dve, [(at(tops, 0), 0), (at(turned, 0), -1), (at(tops, 1), 0), (at(tops, 2), 0), (at(sums_of, 0), 0),
                               (at(turned, 2), -1), (rows, 1), (at(tops, 3), 0), (at(sums_of, 1), 0), (output, -1)])



def tokens_in(nc, c, name, xT, src, affine=None, gate_w=None, scores_dram=None, shift=False, loads=()):
    with Phase(nc, name) as ph:
        hn = ph.sb("hn", [P, 2, D])
        psT = ph.ps("psT", [P, 2, 512])
        psL = ph.ps("psL", [P, 2, 512])
        psW = ph.ps("psW", [P, 4, 512])
        s_fin, s_sh, s_ln, s_T, s_in, s_lg, s_lgo, s_r, s_e, s_wT, s_wo, s_sc, s_hs = ph.semaphores(
            "fin shifted ln T in logits logits_out routing exp wT wT_out stored hs")
        routed = gate_w is not None
        if routed:
            hs = ph.sb("hs", [P, 2, KC, P])
            lg, sel, eq, run, run2 = (ph.sb(n, [P, NB, E]) for n in ("logits", "sel", "eq", "run", "run2"))
            top = ph.sb("top", [P, NB, 8])
            red = ph.sb("red", [P, NB])
            wT = ph.sb("wT", [E, NB, P])
        block = ph.block()

        @block.sync
        def _(sp):
            for load in loads:
                load(sp)
            if routed:
                sp.wait_ge(s_wo, 4)
                sp.dma_start(scores_dram, wT[:, :, :].rearrange("e b t -> e (b t)")).then_inc(s_sc, 16)
                sp.wait_ge(s_sc, 16)

        @block.tensor
        def _(pe):
            c.wait(pe, "const")
            if affine is not None:
                c.wait(pe, affine[2])

            if shift:
                second = c.stats[:, :, 6:12]
                nc.tensor.matmul(psL[:, 0, 0:NB * 6], c.shift, second, start=True, stop=True).then_inc(s_lg, 1)

                def shift_in(s):
                    if isinstance(s.n, int) and s.n < 2:
                        pe.wait_ge(s_sh, 1)
                    else:
                        pe.wait_ge(s_ln, s.n * 2 - 2)
                    nc.tensor.matmul(psL[:, s.p, 0:P], c.shift, seq(src, s)[:, P:D], start=True, stop=True).then_inc(s_lg, 1)

            def turn(s):
                pe.wait_ge(s_ln, s.n * 2 + 2 if shift else s.n + 1)
                after(pe, s_in, s.n - 1, s, 2)
                for k in range(KC):
                    mm = nc.tensor.transpose(psT[:, s.p, k * P:(k + 1) * P], hn[:, s.p, k * P:(k + 1) * P], c.ident)
                mm.then_inc(s_T, 1)

            def logits(s):
                pe.wait_ge(s_hs, s.n + 1)
                after(pe, s_lgo, s.n - 1, s, 2)
                for k in range(KC):
                    mm = nc.tensor.matmul(psL[:, s.p, 0:E], hs[:, s.p, k], gate_w[:, k], start=(k == 0), stop=(k == KC - 1))
                mm.then_inc(s_lg, 1)
            if shift:
                run_pipeline(pe, [(turn, 0), (shift_in, 1)])
            else:
                run_pipeline(pe, [(turn, 1)] + [(logits, 0)] * routed)
            if routed:
                pe.wait_ge(s_r, ROUTING_STEPS)
                for b in range(NB):
                    mm = nc.tensor.transpose(psW[0:E, b // 4, b % 4 * P:(b % 4 + 1) * P], sel[:, b], c.ident)
                    if b % 4 == 3:
                        mm.then_inc(s_wT, 1)

        @block.scalar
        def _(act):
            c.wait(act, "const")

            def copy_in(s):
                act.wait_ge(s_T, s.n + 1)
                if routed:
                    after(act, s_lg, s.n - 1, s, 2)
                    nc.scalar.activation(hs[:, s.p].rearrange("p k t -> p (k t)"), psT[:, s.p, 0:D], ACT.Copy).then_inc(s_hs, 1)
                    nc.scalar.activation(xT[:, :, bass.ds(s.n * P, P)], psT[:, s.p, 0:D].rearrange("p (k t) -> p k t", k=KC),
                                         ACT.Copy).then_inc(s_in, 1)
                else:
                    for k in range(KC):
                        ins = nc.scalar.activation(xT[:, k, bass.ds(s.n * P, P)], psT[:, s.p, k * P:(k + 1) * P], ACT.Identity,
                                                   scale=affine[0][:, k:k + 1], bias=affine[1][:, k:k + 1])
                    ins.then_inc(s_in, 1)
            if affine is not None:
                c.wait(act, affine[2])
            run_pipeline(act, [(copy_in, 1)])
            if routed:
                act.wait_ge(s_r, 2)
                nc.scalar.activation(lg[:, :, :], lg[:, :, :], ACT.Exp).then_inc(s_e, 1)
                for q in range(4):
                    act.wait_ge(s_wT, q + 1)
                    nc.scalar.activation(wT[:, 4 * q:4 * q + 4, :].rearrange("e b t -> e (b t)"), psW[0:E, q], ACT.Copy).then_inc(s_wo, 1)

        @block.vector
        def _(dve):
            c.wait(dve, "const")
            if shift:
                dve.wait_ge(s_lg, 1)
                nc.vector.tensor_copy(c.stats[:, :, 6:12], psL[:, 0, 0:NB * 6].rearrange("p (b s) -> p b s", b=NB)).then_inc(s_sh, 1)
                dve.wait_ge(s_sh, 1)
            finish_stats(nc, Chain(dve, s_fin), c, 4 if shift else 2, 1e-5)

            def rows(s):
                after(dve, s_T, s.n - 1, s, 2)
                if not shift:
                    normalize(nc, c, hn[:, s.p], seq(src, s), s).then_inc(s_ln, 1)
                    return
                normalize(nc, c, hn[:, s.p, 0:P], seq(src, s)[:, 0:P], s).then_inc(s_ln, 1)
                dve.wait_ge(s_lg, s.n + 2)
                normalize(nc, c, hn[:, s.p, P:D], psL[:, s.p, 0:P], s).then_inc(s_ln, 1)

            def logits(s):
                dve.wait_ge(s_lg, s.n + 1)
                nc.vector.tensor_copy(seq(lg, s), psL[:, s.p, 0:E]).then_inc(s_lgo, 1)
            run_pipeline(dve, [(rows, 1)] + [(logits, -1)] * routed)
            if routed:
                dve.wait_ge(s_lgo, NB)
                routing(nc, dve, Chain(dve, s_r), s_e, lg, sel, eq, run, run2, top, red)


def routing(nc, dve, link, s_e, lg, sel, eq, run, run2, top, red):
    v = nc.vector

    def per_token(t):
        return t.unsqueeze(2).broadcast_to([P, NB, E])
    link(v.tensor_reduce(red[:, :], lg[:, :, :], AXX, ALU.max))
    link(v.tensor_tensor(lg[:, :, :], lg[:, :, :], per_token(red[:, :]), ALU.subtract))
    dve.wait_ge(s_e, 1)
    link(v.tensor_reduce(red[:, :], lg[:, :, :], AXX, ALU.add))
    link(v.reciprocal(red[:, :], red[:, :]))
    link(v.tensor_tensor(lg[:, :, :], lg[:, :, :], per_token(red[:, :]), ALU.mult))
    for b in range(NB):
        link(v.max(top[:, b], lg[:, b]), wait=(b == NB - 1))
    fourth = top[:, :, TOPK - 1:TOPK].broadcast_to([P, NB, E])
    link(v.tensor_tensor(sel[:, :, :], lg[:, :, :], fourth, ALU.is_gt), wait=False)
    link(v.tensor_tensor(eq[:, :, :], lg[:, :, :], fourth, ALU.is_equal))
    link(v.tensor_reduce(red[:, :], sel[:, :, :], AXX, ALU.add), wait=False)
    a, b = eq, run
    for d in (1, 2, 4, 8):
        link(v.tensor_copy(b[:, :, 0:d], a[:, :, 0:d]), wait=False)
        link(v.tensor_tensor(b[:, :, d:E], a[:, :, d:E], a[:, :, 0:E - d], ALU.add))
        a, b = b, (run2 if b is run else run)
    link(v.tensor_tensor(b[:, :, :], a[:, :, :], per_token(red[:, :]), ALU.add))
    link(v.tensor_scalar(b[:, :, :], b[:, :, :], float(TOPK) + 0.5, None, ALU.is_lt))
    link(v.tensor_tensor(eq[:, :, :], eq[:, :, :], b[:, :, :], ALU.mult))
    link(v.tensor_tensor(sel[:, :, :], sel[:, :, :], eq[:, :, :], ALU.add))
    link(v.tensor_tensor(sel[:, :, :], sel[:, :, :], lg[:, :, :], ALU.mult))
    link(v.tensor_reduce(red[:, :], sel[:, :, :], AXX, ALU.add))
    link(v.reciprocal(red[:, :], red[:, :]))
    link(v.tensor_tensor(sel[:, :, :], sel[:, :, :], per_token(red[:, :]), ALU.mult))
    assert link.n == ROUTING_STEPS


ROUTING_STEPS = 5 + NB + 3 + 8 + 8



def units(nc, c, name, weights, xT, plan, func, gate, scores_dram=None, bias=None, row=None, state=None,
          into_x=True, loads=()):
    U = len(plan)
    assert U % 2 == 0
    scored = [u for u, (_, _, e) in enumerate(plan) if e is not None]
    last_use = {plan[u][2]: u for u in scored}
    with Phase(nc, name) as ph:
        RING = 4
        sc = ph.sb("sc", [P, RING, GT]) if scored else None
        sg = ph.sb("sg", [P, 2, GT])
        up = ph.sb("up", [P, 2, GT]) if scored and any(p[1] and p[2] is not None for p in plan) else None
        act_ = ph.sb("act", [P, 2, GT])
        yt = ph.sb("yt", [P, 2, D])
        psG, psU, psO = ph.ps("psG", [P, 2, 512]), ph.ps("psU", [P, 2, 512]), ph.ps("psO", [P, 2, 512])
        s_gu, s_sg, s_act, s_down, s_up, s_y, s_x = ph.semaphores("hidden func act down up y x")
        s_sc = [ph.sem(f"sc{r}") for r in range(RING)] if scored else []
        block = ph.block()

        def groups(eng, body):
            body(0)
            with eng.Fori(1, NG) as n:
                body(n)

        def ready(eng, sem, n, u, back):
            if isinstance(n, int):
                if n * U + u - back + 1 > 0:
                    eng.wait_ge(sem, n * U + u - back + 1)
            else:
                eng.wait_ge(sem, n * U + (u - back + 1))

        def wide(ap, n):
            return ap[:, n * GT:(n + 1) * GT] if isinstance(n, int) else ap[:, bass.ds(n * GT, GT)]

        @block.sync
        def _(sp):
            for load in loads:
                load(sp)
            if not scored:
                return

            def scores_in(n):
                for e in range(E):
                    if e >= RING:
                        ready(sp, s_act, n, last_use[e - RING], 0)
                    else:
                        ready(sp, s_act, n, last_use[e - RING + E] - U, 0)
                    sp.dma_start(sc[:, e % RING], wide(scores_dram[e:e + 1], n).rearrange("a t -> (a t)").partition_broadcast(P)) \
                      .then_inc(s_sc[e % RING], 16)
            groups(sp, scores_in)

        @block.tensor
        def _(pe):
            c.wait(pe, weights)

            def group(n):
                for u in range(U + 1):
                    if u < U:
                        at, has_up, _ = plan[u]
                        ready(pe, s_act, n, u, 2)
                        w = c.arena[:, at:at + 2 * KC * P].rearrange("p (m k i) -> p m k i", m=2, k=KC)
                        for m, ps in ((0, psG), (1, psU))[:1 + has_up]:
                            for k in range(KC):
                                mm = nc.tensor.matmul(ps[:, u % 2], w[:, m, k], wide(xT[:, k], n), start=(k == 0), stop=(k == KC - 1))
                        mm.then_inc(s_gu, 1)
                    if u:
                        at, has_up, _ = plan[u - 1]
                        down = c.arena[:, at + (1 + has_up) * D:at + (2 + has_up) * D]
                        ready(pe, s_act, n, u, 1)
                        if u == 1 and not (isinstance(n, int) and n == 0):
                            pe.wait_ge(s_x, n * TPG)
                        for j in range(TPG):
                            mm = nc.tensor.matmul(psO[:, j // 2, j % 2 * D:(j % 2 + 1) * D], act_[:, (u - 1) % 2, j * P:(j + 1) * P],
                                                  down, start=(u == 1 and j % 2 == 0), stop=(u == U), skip_group_check=True)
                        mm.then_inc(s_down, 1)
            groups(pe, group)

        @block.scalar
        def _(act):
            c.wait(act, weights)

            def group(n):
                for u in range(U):
                    ready(act, s_gu, n, u, 0)
                    ready(act, s_act, n, u, 2)
                    b = {} if bias is None else {"bias": bias[0][:, u:u + 1]}
                    nc.scalar.activation(sg[:, u % 2], psG[:, u % 2], func, **b).then_inc(s_sg, 1)
            groups(act, group)

        @block.vector
        def _(dve):
            c.wait(dve, weights)
            per = 2 if into_x else 1
            n_up = sum(1 for _, has_up, e in plan if has_up and e is not None)

            def group(n):
                ups = 0
                for u, (_, has_up, e) in enumerate(plan):
                    hidden, score = act_[:, u % 2], None
                    if e is not None:
                        score = sc[:, e % RING]
                        dve.wait_ge(s_sc[e % RING], n * (16 * E // RING) + 16 * (e // RING + 1))
                    ready(dve, s_down, n, u, 2)
                    if has_up and e is not None:
                        ready(dve, s_gu, n, u, 0)
                        nc.vector.tensor_tensor(up[:, u % 2], psU[:, u % 2], score, ALU.mult).then_inc(s_up, 1)
                        ups += 1
                        dve.wait_ge(s_up, n * n_up + ups)
                    ready(dve, s_sg, n, u, 0)
                    if has_up and bias is not None:
                        ins = nc.vector.scalar_tensor_tensor(hidden, psU[:, u % 2], bias[1][:, u:u + 1], sg[:, u % 2], ALU.add, ALU.mult)
                    elif has_up and e is None:
                        ins = nc.vector.tensor_tensor(hidden, psU[:, u % 2], sg[:, u % 2], ALU.mult)
                    elif has_up:
                        ins = nc.vector.tensor_tensor(hidden, up[:, u % 2], sg[:, u % 2], ALU.mult)
                    else:
                        ins = nc.vector.tensor_tensor(hidden, sg[:, u % 2], score, ALU.mult)
                    ins.then_inc(s_act, 1)
                ready(dve, s_down, n, U - 1, 0)
                for j in range(TPG):
                    s = Step(n * TPG + j, j % 2, None)
                    o = psO[:, j // 2, j % 2 * D:(j % 2 + 1) * D]
                    if state is None:
                        nc.vector.scalar_tensor_tensor(seq(c.X, s), o, c.gates[:, gate:gate + 1], seq(c.X, s),
                                                       ALU.mult, ALU.add).then_inc(s_x, 1)
                    else:
                        link = Chain(dve, s_y, n * (per * TPG) + per * j)
                        y = yt[:, j % 2]
                        if into_x:
                            link(nc.vector.tensor_tensor(y, o, seq(state, s), ALU.add))
                            link(nc.vector.tensor_tensor(y, y, row, ALU.add))
                            nc.vector.scalar_tensor_tensor(seq(c.X, s), y, c.gates[:, gate:gate + 1], seq(c.X, s),
                                                           ALU.mult, ALU.add).then_inc(s_x, 1)
                        else:
                            link(nc.vector.tensor_tensor(y, o, row, ALU.add))
                            nc.vector.tensor_tensor(seq(state, s), y, seq(state, s), ALU.add).then_inc(s_x, 1)
                    if into_x:
                        dve.wait_ge(s_x, n * TPG + (j + 1))
                        nc.vector.bn_stats(seq(c.stats, s)[:, 0:6], seq(c.X, s))
            groups(dve, group)



def single_attention(nc, c, Y, gate, loads=()):
    W = c.arena[:, MLP1_AT:MLP1_AT + MLP1].rearrange("p (m k n) -> p m k n", m=2, k=KC)
    b1, gamma_c, beta_c = (c.vec1x[:, i * KC:(i + 1) * KC] for i in range(3))
    gamma, beta, b2 = (c.vec1x[:, COLS1X + i * D:COLS1X + (i + 1) * D] for i in range(3))
    with Phase(nc, "L1x_attend") as ph:
        hn = ph.sb("hn", [P, 2, D])
        hT = ph.sb("hT", [P, 2, KC, P])
        pr, pT = ph.sb("pr", [P, 2, P]), ph.sb("pT", [P, 2, P])
        mx, sm, rs = ph.sb("mx", [P, 2]), ph.sb("sm", [P, 2]), ph.sb("rs", [P, 2])
        psT, psS, psP, psV = (ph.ps(n, [P, 2, 512]) for n in ("psT", "psS", "psP", "psV"))
        s_fin, s_ln, s_kept, s_T, s_hT, s_S, s_mx, s_sub, s_exp, s_pt, s_pT, s_v, s_rs, s_y = ph.semaphores(
            "fin ln kept T hT S mx sub exp pt pT v rs y")
        block = ph.block()

        @block.sync
        def _(sp):
            for load in loads:
                load(sp)

        @block.gpsimd
        def _(pool):
            def keep(s):
                pool.wait_ge(s_ln, s.n + 1)
                nc.gpsimd.tensor_copy(seq(Y, s), hn[:, s.p]).then_inc(s_kept, 1)
            run_pipeline(pool, [(keep, 1)])

        @block.tensor
        def _(pe):
            c.wait(pe, "ctx")

            def turn_in(s):
                pe.wait_ge(s_ln, s.n + 1)
                after(pe, s_hT, s.n - 1, s, 2)
                for k in range(KC):
                    mm = nc.tensor.transpose(psT[:, s.p, k * P:(k + 1) * P], hn[:, s.p, k * P:(k + 1) * P], c.ident)
                mm.then_inc(s_T, 1)

            def scores(s):
                pe.wait_ge(s_hT, s.n + 1)
                after(pe, s_sub, s.n - 1, s, 2)
                for k in range(KC):
                    mm = nc.tensor.matmul(psS[:, s.p, 0:P], hT[:, s.p, k], seq_chunk(c.ctxT, s, k), start=(k == 0), stop=(k == KC - 1))
                mm.then_inc(s_S, 1)

            def turn(s):
                pe.wait_ge(s_exp, s.n + 1)
                after(pe, s_pT, s.n - 1, s, 2)
                nc.tensor.transpose(psP[:, s.p, 0:P], pr[:, s.p], c.ident).then_inc(s_pt, 1)

            def values(s):
                pe.wait_ge(s_pT, s.n + 1)
                after(pe, s_y, s.n - 1, s, 2)
                nc.tensor.matmul(psV[:, s.p, 0:D], pT[:, s.p], seq(c.ctx, s), start=True, stop=True).then_inc(s_v, 1)
            run_pipeline(pe, [(values, -2), (turn, -1), (scores, 0), (turn_in, 1)])

        @block.scalar
        def _(act):
            def rows(s):
                act.wait_ge(s_T, s.n + 1)
                after(act, s_S, s.n - 1, s, 2)
                nc.scalar.activation(hT[:, s.p].rearrange("p k t -> p (k t)"), psT[:, s.p, 0:D], ACT.Copy).then_inc(s_hT, 1)

            def exps(s):
                act.wait_ge(s_sub, s.n + 1)
                after(act, s_rs, s.n - 1, s, 2)
                nc.scalar.activation(pr[:, s.p], pr[:, s.p], ACT.Exp, scale=1.0 / 16, accum_out=sm[:, s.p:s.p + 1]).then_inc(s_exp, 1)

            def turned(s):
                act.wait_ge(s_pt, s.n + 1)
                after(act, s_v, s.n - 1, s, 2)
                nc.scalar.activation(pT[:, s.p], psP[:, s.p, 0:P], ACT.Copy).then_inc(s_pT, 1)
            run_pipeline(act, [(turned, -1), (rows, 1), (exps, 0)])

        @block.vector
        def _(dve):
            finish_stats(nc, Chain(dve, s_fin), c, 2, 1e-5)

            def rows(s):
                after(dve, s_T, s.n - 1, s, 2)
                after(dve, s_kept, s.n - 1, s, 2)
                normalize(nc, c, hn[:, s.p], seq(c.X, s), s).then_inc(s_ln, 1)

            def tops(s):
                dve.wait_ge(s_S, s.n + 1)
                after(dve, s_sub, s.n - 1, s, 2)
                nc.vector.tensor_reduce(mx[:, s.p:s.p + 1], psS[:, s.p, 0:P], AXX, ALU.max).then_inc(s_mx, 1)

            def below(s):
                dve.wait_ge(s_mx, s.n + 1)
                after(dve, s_pt, s.n - 1, s, 2)
                nc.vector.tensor_scalar(pr[:, s.p], psS[:, s.p, 0:P], mx[:, s.p:s.p + 1], None, ALU.subtract).then_inc(s_sub, 1)

            def sums(s):
                dve.wait_ge(s_exp, s.n + 1)
                after(dve, s_y, s.n - 1, s, 2)
                nc.vector.reciprocal(rs[:, s.p:s.p + 1], sm[:, s.p:s.p + 1]).then_inc(s_rs, 1)

            def add(s):
                dve.wait_ge(s_v, s.n + 1)
                dve.wait_ge(s_rs, s.n + 1)
                dve.wait_ge(s_kept, s.n + 1)
                nc.vector.scalar_tensor_tensor(seq(Y, s), psV[:, s.p, 0:D], rs[:, s.p:s.p + 1], seq(Y, s), ALU.mult, ALU.add).then_inc(s_y, 1)

            def stats(s):
                dve.wait_ge(s_y, s.n + 1)
                nc.vector.bn_stats(seq(c.stats, s)[:, 0:6], seq(Y, s))
            run_pipeline(dve, [(rows, 1), (add, -2), (sums, -1), (tops, 0), (stats, -2), (below, 0)])

    with Phase(nc, "L1x_mlp") as ph:
        xn, xg = ph.sb("xn", [P, 2, D]), ph.sb("xg", [P, 2, D])
        bb = ph.sb("bb", [P, D])
        x1T, h1T = ph.sb("x1T", [P, 2, KC, P]), ph.sb("h1T", [P, 2, KC, P])
        psT, psH, psO = (ph.ps(n, [P, 2, 512]) for n in ("psT", "psH", "psO"))
        s_fin, s_bb, s_ln, s_g, s_xb, s_T, s_x1T, s_H, s_h1, s_o, s_y = ph.semaphores("fin bb ln g xb T x1T H h1 o y")
        block = ph.block()

        @block.gpsimd
        def _(pool):
            c.wait(pool, "L1x")
            nc.gpsimd.tensor_tensor(bb[:, :], beta, b2, ALU.add).then_inc(s_bb, 1)
            pool.wait_ge(s_bb, 1)

            def affine(s):
                pool.wait_ge(s_ln, s.n + 1)
                after(pool, s_xb, s.n - 1, s, 2)
                nc.gpsimd.tensor_tensor(xg[:, s.p], xn[:, s.p], gamma, ALU.mult).then_inc(s_g, 1)
                pool.wait_ge(s_g, s.n + 1)
                nc.gpsimd.tensor_tensor(seq(Y, s), xg[:, s.p], bb[:, :], ALU.add).then_inc(s_xb, 1)
            run_pipeline(pool, [(affine, 1)])

        @block.tensor
        def _(pe):
            c.wait(pe, "L1x")

            def turn_in(s):
                pe.wait_ge(s_ln, s.n + 1)
                after(pe, s_x1T, s.n - 1, s, 2)
                for k in range(KC):
                    mm = nc.tensor.transpose(psT[:, s.p, k * P:(k + 1) * P], xn[:, s.p, k * P:(k + 1) * P], c.ident)
                mm.then_inc(s_T, 1)

            def hidden(s):
                pe.wait_ge(s_x1T, s.n + 1)
                after(pe, s_h1, (s.n - 1) * 2, s, 2)
                for o in range(KC):
                    for k in range(KC):
                        mm = nc.tensor.matmul(psH[:, s.p, o * P:(o + 1) * P], W[:, 0, k, o * P:(o + 1) * P], x1T[:, s.p, k],
                                              start=(k == 0), stop=(k == KC - 1))
                mm.then_inc(s_H, 1)

            def output(s):
                pe.wait_ge(s_h1, s.n * 2 + 2)
                after(pe, s_y, s.n - 1, s, 2)
                for k in range(KC):
                    mm = nc.tensor.matmul(psO[:, s.p, 0:D], h1T[:, s.p, k], W[:, 1, k], start=(k == 0), stop=(k == KC - 1))
                mm.then_inc(s_o, 1)
            run_pipeline(pe, [(output, -1), (hidden, 0), (turn_in, 1)])

        @block.scalar
        def _(act):
            c.wait(act, "L1x")

            def rows(s):
                act.wait_ge(s_T, s.n + 1)
                after(act, s_H, s.n - 1, s, 2)
                for k in range(KC):
                    ins = nc.scalar.activation(x1T[:, s.p, k], psT[:, s.p, k * P:(k + 1) * P], ACT.Identity,
                                               scale=gamma_c[:, k:k + 1], bias=beta_c[:, k:k + 1])
                ins.then_inc(s_x1T, 1)

            def hidden(s):
                act.wait_ge(s_H, s.n + 1)
                after(act, s_o, s.n - 1, s, 2)
                for k in range(KC):
                    nc.scalar.activation(h1T[:, s.p, k], psH[:, s.p, k * P:(k + 1) * P], ACT.Relu, bias=b1[:, k:k + 1]).then_inc(s_h1, 1)
            run_pipeline(act, [(hidden, 0), (rows, 1)])

        @block.vector
        def _(dve):
            c.wait(dve, "L1x")
            finish_stats(nc, Chain(dve, s_fin), c, 2, 1e-6)

            def rows(s):
                after(dve, s_g, s.n - 1, s, 2)
                after(dve, s_T, s.n - 1, s, 2)
                normalize(nc, c, xn[:, s.p], seq(Y, s), s).then_inc(s_ln, 1)

            def add(s):
                dve.wait_ge(s_o, s.n + 1)
                dve.wait_ge(s_xb, s.n + 1)
                nc.vector.tensor_tensor(seq(Y, s), psO[:, s.p, 0:D], seq(Y, s), ALU.add).then_inc(s_y, 1)
                dve.wait_ge(s_y, s.n + 1)
                nc.vector.bn_stats(seq(c.stats, s)[:, 0:6], seq(Y, s))
            run_pipeline(dve, [(rows, 1), (add, -1)])

    with Phase(nc, "L1x_last") as ph:
        xn = ph.sb("xn", [P, 2, D])
        x2, x3 = ph.sb("x2", [P, 2, D]), ph.sb("x3", [P, 2, D])
        s_fin, s_ln, s_g, s_b, s_x = ph.semaphores("fin ln g b x")
        block = ph.block()

        @block.gpsimd
        def _(pool):
            def affine(s):
                pool.wait_ge(s_ln, s.n + 1)
                after(pool, s_b, s.n - 1, s, 2)
                nc.gpsimd.tensor_tensor(x2[:, s.p], xn[:, s.p], gamma, ALU.mult).then_inc(s_g, 1)
                pool.wait_ge(s_g, s.n + 1)
                after(pool, s_x, s.n - 1, s, 2)
                nc.gpsimd.tensor_tensor(x3[:, s.p], x2[:, s.p], beta, ALU.add).then_inc(s_b, 1)
            run_pipeline(pool, [(affine, 1)])

        @block.vector
        def _(dve):
            finish_stats(nc, Chain(dve, s_fin), c, 2, 1e-6)

            def rows(s):
                after(dve, s_g, s.n - 1, s, 2)
                normalize(nc, c, xn[:, s.p], seq(Y, s), s).then_inc(s_ln, 1)

            def add(s):
                dve.wait_ge(s_b, s.n + 1)
                nc.vector.scalar_tensor_tensor(seq(c.X, s), x3[:, s.p], c.gates[:, gate:gate + 1], seq(c.X, s),
                                               ALU.mult, ALU.add).then_inc(s_x, 1)
                dve.wait_ge(s_x, s.n + 1)
                nc.vector.bn_stats(seq(c.stats, s)[:, 0:6], seq(c.X, s))
            run_pipeline(dve, [(rows, 1), (add, -1)])



def window_attention(nc, c, Y, layer, loads=()):
    name = f"L1f{layer}"
    base = layer * L1F
    wqkv = c.arena[:, base:base + WQKV].rearrange("p (k n) -> p k n", k=KC)
    wo = c.arena[:, base + WQKV:base + WQKV + WO1].rearrange("p (k n) -> p k n", k=INNER // P)
    scales = c.vec1f[:, layer, COLS1F + D:COLS1F + D + 2 * LD].rearrange("p (w d) -> p w d", w=2)
    HALF = LD // 2
    with Phase(nc, name + "_attend") as ph:
        hn = ph.sb("hn", [P, 2, D])
        hT = ph.sb("hT", [P, 2, KC, P])
        sq = ph.sb("sq", [P, 2 * INNER])
        ss, rn, tt = ph.sb("ss", [P, 2, 2 * LH]), ph.sb("rn", [P, 2, 2 * LH]), ph.sb("tt", [P, 2 * LH])
        root_c = ph.sb("root_c", [P, 2, 2 * LH])
        qn = ph.sb("qn", [P, 2, LH, LD])
        rot, cosd = ph.sb("rot", [P, 2, LH, LD]), ph.sb("cosd", [P, 2, LH, LD])
        qr = ph.sb("qr", [P, 2, LH, LD])
        cosT, sinT = ph.sb("cosT", [P, 2, LD]), ph.sb("sinT", [P, 2, LD])
        qT, kT = ph.sb("qT", [P, 2, 4, P]), ph.sb("kT", [P, 2, 4, P])
        vx = ph.sb("vx", [P, 2, LH, LD + 1])
        pr = ph.sb("pr", [P, 2, 2, 512])
        mx = ph.sb("mx", [P, 2, 2, 4])
        pT = ph.sb("pT", [P, 2, 512])
        rs = ph.sb("rs", [P, 2, 4])
        on, oT = ph.sb("on", [P, INNER]), ph.sb("oT", [P, 4, P])
        psQ = ph.ps("psQ", [P, 2, 512])
        psP = ph.ps("psP", [P, 2, 512])
        psS = ph.ps("psS", [P, 2, 512])
        psB = ph.ps("psB", [P, 2, 512])
        (s_fin, s_one, s_tab, s_ln, s_y, s_T, s_hT, s_qk, s_v, s_sq, s_ss, s_rn, s_qn, s_cos, s_rot, s_qr,
         s_qkT, s_qT, s_kT, s_vx, s_S, s_mx, s_exp, s_pt, s_ptA, s_ptV, s_pv, s_rs, s_on, s_ot, s_oT,
         s_out, s_x) = ph.semaphores(
            "fin ones tab ln y T hT qk v sq ss rn qn cos rot qr qkT qT kT vx S mx exp pt ptA ptV pv rs on ot oT out x")
        SCALE = 8.0

        def halves(t):
            return t[:, :, :, :].rearrange("p w h (i d) -> p w i h d", i=2)

        block = ph.block()

        @block.sync
        def _(sp):
            for load in loads:
                load(sp)

        @block.gpsimd
        def _(pool):
            nc.gpsimd.memset(vx[:, :, :, LD:LD + 1], 1.0).then_inc(s_one, 1)
            nc.gpsimd.memset(hT[:, :, 1, 0:1], 0.0).then_inc(s_one, 1)
            for i, value in enumerate((-0.5, 1.5)):
                nc.gpsimd.memset(root_c[:, i], value).then_inc(s_one, 1)
            pool.wait_ge(s_one, 4)

            def rows(s):
                if layer == 0:
                    pool.wait_ge(s_ln, s.n + 1)
                    nc.gpsimd.tensor_copy(seq(Y, s), hn[:, s.p]).then_inc(s_y, 1)
                else:
                    after(pool, s_T, s.n - 1, s, 2)
                    nc.gpsimd.tensor_copy(hn[:, s.p], seq(Y, s)).then_inc(s_y, 1)

            def roots(s):
                pool.wait_ge(s_ss, s.n * 3 + 3)
                after(pool, s_qn, s.n * 2 - 2, s, 2)
                newton_rsqrt(nc.gpsimd, Chain(pool, s_rn, s.n * NEWTON_STEPS), rn[:, s.p], ss[:, s.p], tt[:, :],
                             root_c[:, 0], root_c[:, 1])

            def rotate(s):
                pool.wait_ge(s_qn, s.n * 2 + 2)
                pool.wait_ge(s_tab, TABLE_STEPS)
                after(pool, s_qr, s.n, s, 1)
                for i, o in ((0, 1), (1, 0)):
                    nc.gpsimd.tensor_tensor(halves(rot)[:, :, i], halves(qn)[:, :, o],
                                            sinT[:, :, i * HALF:(i + 1) * HALF].unsqueeze(2).broadcast_to([P, 2, LH, HALF]),
                                            ALU.mult).then_inc(s_rot, 1)
            run_pipeline(pool, [(rows, 0 if layer == 0 else 1), (roots, 0), (rotate, 0)])

        @block.tensor
        def _(pe):
            c.wait(pe, name)
            pe.wait_ge(s_one, 2)

            def turn_in(s):
                pe.wait_ge(s_ln if layer == 0 else s_y, s.n + 1)
                after(pe, s_on, s.n * 2 - 4, s, 3)
                for k in range(KC):
                    mm = nc.tensor.transpose(psB[:, 1, k * P:(k + 1) * P], hn[:, s.p, k * P:(k + 1) * P], c.ident)
                mm.then_inc(s_T, 1)

            def product(out, s, j, done):
                for k in range(KC):
                    mm = nc.tensor.matmul(out, hT[:, s.p, k], wqkv[:, k, j * INNER:(j + 1) * INNER],
                                          start=(k == 0), stop=(k == KC - 1))
                mm.then_inc(done, 1)

            def queries_keys(s):
                pe.wait_ge(s_hT, s.n + 1)
                for j in range(2):
                    after(pe, s_qn, s.n * 2 - 1 + j, s, 1)
                    product(psQ[:, j], s, j, s_qk)

            def values_in(s):
                after(pe, s_exp, s.n * 2 - 3, s, 2)
                product(psS[:, 0], s, 2, s_v)

            def turn(s):
                pe.wait_ge(s_qr, s.n + 1)
                after(pe, s_ptA, s.n, s, 1)
                after(pe, s_ptV, s.n, s, 1)
                for w in range(2):
                    for k in range(4):
                        mm = nc.tensor.transpose(psP[:, w, k * P:(k + 1) * P],
                                                 qr[:, w].rearrange("p h d -> p (h d)")[:, k * P:(k + 1) * P], c.ident)
                    mm.then_inc(s_qkT, 1)

            def scores(s):
                pe.wait_ge(s_qT, s.n + 1)
                pe.wait_ge(s_kT, s.n + 1)
                for r in range(2):
                    if r == 0:
                        pe.wait_ge(s_vx, s.n + (1 if last(s) else 2))
                    else:
                        after(pe, s_oT, s.n, s, 1)
                    nc.tensor.matmul(psS[:, r], c.ident16[:, :], c.causal[:, :, :].rearrange("p a k -> p (a k)"),
                                     start=True, stop=False, skip_group_check=True)
                    rows = slice(64 * r, 64 * r + 64)
                    for k in range(4):
                        mm = nc.tensor.matmul(psS[:, r, k * P:(k + 1) * P], qT[rows, s.p, k], kT[rows, s.p, k],
                                              start=False, stop=True, skip_group_check=True)
                    mm.then_inc(s_S, 1)

            def values(s):
                for r in range(2):
                    pe.wait_ge(s_exp, s.n * 2 + r + 1)
                    for k in range(4):
                        mm = nc.tensor.transpose(psP[:, r, k * P:(k + 1) * P], pr[:, s.p, r, k * P:(k + 1) * P], c.ident)
                    mm.then_inc(s_pt, 1)
                for r in range(2):
                    pe.wait_ge(s_ptV if r else s_ptA, s.n + 1)
                    if r == 0:
                        after(pe, s_x, s.n, s, 1)
                    for k in range(4):
                        mm = nc.tensor.matmul(psB[:, r, k * 65:k * 65 + 65], pT[:, r, k * P:(k + 1) * P], vx[:, s.p, 2 * k + r],
                                              start=True, stop=True)
                    mm.then_inc(s_pv, 1)

            def turn_out(s):
                pe.wait_ge(s_on, s.n * 2 + 2)
                for k in range(4):
                    mm = nc.tensor.transpose(psS[:, 1, k * P:(k + 1) * P], on[:, k * P:(k + 1) * P], c.ident)
                mm.then_inc(s_ot, 1)

            def output(s):
                pe.wait_ge(s_oT, s.n + 1)
                for k in range(4):
                    mm = nc.tensor.matmul(psB[:, 0, 0:D], oT[:, k], wo[:, k], start=(k == 0), stop=(k == 3))
                mm.then_inc(s_out, 1)
            run_pipeline(pe, [(queries_keys, 0), (values, -2), (turn, -1), (values_in, 0), (turn_out, -2), (turn_in, 1),
                              (scores, -1), (output, -2)])

        @block.scalar
        def _(act):
            act.wait_ge(s_one, 2)

            def rows(s):
                act.wait_ge(s_T, s.n + 1)
                after(act, s_v, s.n - 1, s, 2)
                nc.scalar.activation(hT[:, s.p, 0], psB[:, 1, 0:P], ACT.Copy)
                nc.scalar.activation(hT[:, s.p, 1, 1:P], psB[:, 1, P:2 * P - 1], ACT.Copy).then_inc(s_hT, 1)

            def squares(s):
                for w in range(2):
                    act.wait_ge(s_qk, s.n * 2 + w + 1)
                    after(act, s_ss, s.n * 3, s, 1)
                    nc.scalar.activation(sq[:, w * INNER:(w + 1) * INNER], psQ[:, w], ACT.Square).then_inc(s_sq, 1)

            def values_in(s):
                act.wait_ge(s_v, s.n + 1)
                after(act, s_pv, s.n * 2 - 2, s, 2)
                nc.scalar.activation(vx[:, s.p, :, 0:LD], psS[:, 0].rearrange("p (h d) -> p h d", h=LH), ACT.Copy).then_inc(s_vx, 1)

            def turn(s):
                for w, (to, done) in enumerate(((qT, s_qT), (kT, s_kT))):
                    act.wait_ge(s_qkT, s.n * 2 + w + 1)
                    after(act, s_S, s.n * 2 - 2, s, 2)
                    nc.scalar.activation(to[:, s.p].rearrange("p k t -> p (k t)"), psP[:, w], ACT.Copy).then_inc(done, 1)

            def softmax(s):
                after(act, s_pt, s.n * 2 - 2, s, 2)
                for r in range(2):
                    act.wait_ge(s_mx, s.n * 2 + r + 1)
                    for k in range(4):
                        ins = nc.scalar.activation(pr[:, s.p, r, k * P:(k + 1) * P], psS[:, r, k * P:(k + 1) * P], ACT.Exp,
                                                   bias=mx[:, s.p, r, k:k + 1])
                    ins.then_inc(s_exp, 1)

            def values(s):
                act.wait_ge(s_pt, s.n * 2 + 1)
                after(act, s_pv, s.n * 2 - 1, s, 1)
                nc.scalar.activation(pT[:, 0], psP[:, 0], ACT.Copy).then_inc(s_ptA, 1)

            def output(s):
                act.wait_ge(s_ot, s.n + 1)
                after(act, s_out, s.n, s, 1)
                nc.scalar.activation(oT[:, :, :].rearrange("p k t -> p (k t)"), psS[:, 1], ACT.Copy).then_inc(s_oT, 1)
            run_pipeline(act, [(squares, 0), (values, -2), (turn, -1), (values_in, 0), (output, -2), (rows, 1), (softmax, -1)])

        @block.vector
        def _(dve):
            c.wait(dve, name)
            v = nc.vector
            link = Chain(dve, s_tab)
            rope = c.rope.rearrange("p (t w d) -> p t w d", t=2, w=2)
            link(v.tensor_tensor(cosT[:, :, :], rope[:, 0], scales, ALU.mult), wait=False)
            for i, o in ((0, 1), (1, 0)):
                link(v.tensor_tensor(sinT[:, :, i * HALF:(i + 1) * HALF], rope[:, 1, :, i * HALF:(i + 1) * HALF],
                                     scales[:, :, o * HALF:(o + 1) * HALF], ALU.mult), wait=(i == 1))
            link(v.tensor_scalar(cosT[:, 0], cosT[:, 0], SCALE, None, ALU.mult), wait=False)
            link(v.tensor_scalar(sinT[:, 0], sinT[:, 0], SCALE, None, ALU.mult))
            if layer == 0:
                finish_stats(nc, Chain(dve, s_fin), c, 2, 1e-5)

            def rows(s):
                after(dve, s_T, s.n - 1, s, 2)
                after(dve, s_y, s.n - 1, s, 2)
                normalize(nc, c, hn[:, s.p], seq(c.X, s), s).then_inc(s_ln, 1)

            def squares(s):
                dve.wait_ge(s_sq, s.n * 2 + 2)
                after(dve, s_rn, (s.n - 1) * NEWTON_STEPS, s, 2)
                nc.vector.tensor_reduce(ss[:, s.p], sq[:, :].rearrange("p (h d) -> p h d", d=LD), AXX, ALU.add).then_inc(s_ss, 1)
                dve.wait_ge(s_ss, s.n * 3 + 1)
                nc.vector.tensor_scalar(ss[:, s.p], ss[:, s.p], 1e-24, None, ALU.max).then_inc(s_ss, 1)
                dve.wait_ge(s_ss, s.n * 3 + 2)
                after(dve, s_qn, s.n * 2 - 2, s, 2)
                guess_rsqrt(nc.vector, rn[:, s.p], ss[:, s.p]).then_inc(s_ss, 1)

            def norms(s):
                dve.wait_ge(s_rn, (s.n + 1) * NEWTON_STEPS)
                after(dve, s_rot, s.n * 2, s, 1)
                after(dve, s_cos, s.n, s, 1)
                for w in range(2):
                    nc.vector.tensor_tensor(qn[:, w], psQ[:, w].rearrange("p (h d) -> p h d", h=LH),
                                            rn[:, s.p, w * LH:(w + 1) * LH].unsqueeze(2).broadcast_to([P, LH, LD]), ALU.mult).then_inc(s_qn, 1)

            def cosines(s):
                dve.wait_ge(s_qn, s.n * 2 + 2)
                after(dve, s_qr, s.n, s, 1)
                nc.vector.tensor_tensor(cosd[:, :, :, :], qn[:, :, :, :], cosT[:, :, :].unsqueeze(2).broadcast_to([P, 2, LH, LD]), ALU.mult).then_inc(s_cos, 1)

            def rotated(s):
                dve.wait_ge(s_rot, s.n * 2 + 2)
                dve.wait_ge(s_cos, s.n + 1)
                after(dve, s_qkT, s.n * 2, s, 1)
                nc.vector.tensor_tensor(qr[:, :, :, :], cosd[:, :, :, :], rot[:, :, :, :], ALU.add).then_inc(s_qr, 1)

            def tops(s):
                after(dve, s_exp, s.n * 2 - 2, s, 2)
                for r in range(2):
                    dve.wait_ge(s_S, s.n * 2 + r + 1)
                    nc.vector.tensor_reduce(mx[:, s.p, r], psS[:, r].rearrange("p (h k) -> p h k", h=4), AXX, ALU.max,
                                            negate=True).then_inc(s_mx, 1)

            def turned(s):
                dve.wait_ge(s_pt, s.n * 2 + 2)
                after(dve, s_pv, s.n * 2, s, 1)
                nc.vector.tensor_copy(pT[:, 1], psP[:, 1]).then_inc(s_ptV, 1)

            def values(s):
                after(dve, s_on, s.n * 2, s, 1)
                for r in range(2):
                    dve.wait_ge(s_pv, s.n * 2 + r + 1)
                    o = psB[:, r, 0:260].rearrange("p (h d) -> p h d", h=4)
                    nc.vector.reciprocal(rs[:, r], o[:, :, LD]).then_inc(s_rs, 1)
                after(dve, s_ot, s.n, s, 1)
                for r in range(2):
                    o = psB[:, r, 0:260].rearrange("p (h d) -> p h d", h=4)
                    dve.wait_ge(s_rs, s.n * 2 + r + 1)
                    nc.vector.tensor_tensor(on[:, :].rearrange("p (h r d) -> p r h d", r=2, d=LD)[:, r], o[:, :, 0:LD],
                                            rs[:, r].unsqueeze(2).broadcast_to([P, 4, LD]), ALU.mult).then_inc(s_on, 1)

            def output(s):
                dve.wait_ge(s_out, s.n + 1)
                if layer == 0:
                    dve.wait_ge(s_y, s.n + 1)
                nc.vector.tensor_tensor(seq(Y, s), psB[:, 0, 0:D], seq(Y, s), ALU.add).then_inc(s_x, 1)

            def stats(s):
                dve.wait_ge(s_x, s.n + 1)
                for i in range(2):
                    nc.vector.bn_stats(seq(c.stats, s)[:, 6 * i:6 * i + 6], seq(Y, s)[:, i * P:(i + 1) * P])
            run_pipeline(dve, [(turned, -2), (squares, 0), (values, -2)] + [(rows, 1)] * (layer == 0) +
                         [(norms, 0), (tops, -1), (cosines, 0), (output, -2), (rotated, 0), (stats, -2)])


TABLE_STEPS = 5



def turn_by_phase(nc, c):
    W = c.slot[:, 0:HEADS_W].rearrange("p (m k n) -> p m k n", m=4, k=KC)
    with Phase(nc, "L3x_turn") as ph:
        ang = ph.sb("ang", [P, 8, H16])
        rows = ph.sb("rows", [P, 2, D])
        t = [ph.sb(f"t{i}", [P, KC, H16, DH // 2]) for i in range(2)]
        psT = ph.ps("psT", [P, 4, P])
        s_in, s_r, s_sin, s_T = ph.semaphores("in r sin T")
        block = ph.block()

        @block.sync
        def _(sp):
            sp.dma_start(ang[:, 0, :], c.dram["phase"].partition_broadcast(P)).then_inc(s_in, 16)
            sp.dma_start(rows[:, :, :].rearrange("p m d -> p (m d)"), c.dram["bias_L3x"].partition_broadcast(P)).then_inc(s_in, 16)

        @block.scalar
        def _(act):
            act.wait_ge(s_r, 10)
            nc.scalar.activation(ang[:, 4, :], ang[:, 2, :], ACT.Sin)
            nc.scalar.activation(ang[:, 5, :], ang[:, 3, :], ACT.Sin).then_inc(s_sin, 1)

        @block.vector
        def _(dve):
            v = nc.vector
            c.wait(dve, "L3x")
            dve.wait_ge(s_in, 32)
            link = Chain(dve, s_r)
            rounder = float(3 << 22)
            two_pi = 2 * np.pi
            p1 = 6.28125
            p2 = round((two_pi - p1) * 2 ** 21) / 2 ** 21
            p3 = two_pi - p1 - p2
            a = [ang[:, i, :] for i in range(8)]
            link(v.tensor_scalar(a[1], a[0], 1 / two_pi, rounder, ALU.mult, ALU.add))
            link(v.tensor_scalar(a[1], a[1], -rounder, None, ALU.add))
            link(v.scalar_tensor_tensor(a[2], a[1], -p1, a[0], ALU.mult, ALU.add))
            link(v.scalar_tensor_tensor(a[2], a[1], -p2, a[2], ALU.mult, ALU.add))
            link(v.scalar_tensor_tensor(a[2], a[1], -p3, a[2], ALU.mult, ALU.add))
            link(v.tensor_scalar(a[2], a[2], 3.1415925, -3.1415925, ALU.min, ALU.max))
            link(v.tensor_scalar(a[6], a[2], -1.0, None, ALU.mult))
            link(v.tensor_tensor(a[6], a[6], a[2], ALU.max))
            link(v.tensor_scalar(a[3], a[6], -1.0, np.pi / 2, ALU.mult, ALU.add))
            link(v.tensor_copy(a[7], a[3]))
            dve.wait_ge(s_sin, 1)
            sin, cos = a[4], a[5]
            for m in range(3):
                w = (W[:, m] if m < 2 else rows[:, :, :]).rearrange("p k (h i d) -> p k h i d", h=H16, i=2)
                for k in range(KC):
                    re, im = w[:, k, :, 0], w[:, k, :, 1]
                    cb, sb = (x.unsqueeze(2).broadcast_to([P, H16, DH // 2]) for x in (cos, sin))
                    link(v.tensor_tensor(t[0][:, 0], re, sb, ALU.mult), wait=False)
                    link(v.tensor_tensor(t[0][:, 1], im, sb, ALU.mult), wait=False)
                    link(v.tensor_tensor(t[1][:, 0], re, cb, ALU.mult), wait=False)
                    link(v.tensor_tensor(t[1][:, 1], im, cb, ALU.mult))
                    link(v.tensor_tensor(re, t[1][:, 0], t[0][:, 1], ALU.subtract), wait=False)
                    link(v.tensor_tensor(im, t[1][:, 1], t[0][:, 0], ALU.add))
            dve.wait_ge(s_T, 1)
            v.tensor_copy(c.slot[:, HEADS_W:HEADS_W + 4], psT[:, :, 0])

        @block.tensor
        def _(pe):
            pe.wait_ge(s_r, 10 + 36)
            for m in range(2):
                for k in range(KC):
                    mm = nc.tensor.transpose(psT[:, 2 * m + k], rows[:, m, k * P:(k + 1) * P], c.ident)
            mm.then_inc(s_T, 1)


def fourier_filter(nc, c, gate, out):
    with Phase(nc, "L3f") as ph:
        base = 3 * KC * D
        dft = c.arena[:, 0:base].rearrange("p (m k n) -> p m k n", m=3, k=KC)
        w = c.arena[:, base:base + 2 * KC * D].rearrange("p (m k n) -> p m k n", m=2, k=KC)
        bias = c.arena[:, base + 2 * KC * D:base + 2 * KC * D + D]
        aT = ph.sb("aT", [P, 2, KC, D])
        M = ph.sb("M", [P, KC, D])
        hn, hT = ph.sb("hn", [P, 2, D]), ph.sb("hT", [P, 2, KC, P])
        yo = ph.sb("yo", [P, 2, D])
        psA, psT, psY = ph.ps("psA", [P, 4, 512]), ph.ps("psT", [P, 2, 512]), ph.ps("psY", [P, 2, 512])
        s_fin, s_A, s_a, s_M, s_m, s_ln, s_T, s_hT, s_y, s_yo, s_x, s_out = ph.semaphores(
            "fin A a M m ln T hT y yo x stored")
        block = ph.block()

        @block.sync
        def _(sp):
            for b in range(0, NB, 4):
                sp.wait_ge(s_x, b + 4)
                sp.dma_start(out[b:b + 4].rearrange("b p d -> p b d"), c.X[:, b:b + 4, :]).then_inc(s_out, 16)
            sp.wait_ge(s_out, 16 * NB // 4)

        @block.tensor
        def _(pe):
            c.wait(pe, "L3f")
            for part, pairs in enumerate((((0, 0), (1, 1)), ((1, 0), (0, 2)))):
                for o in range(KC):
                    n = 0
                    for m, f in pairs:
                        for k in range(KC):
                            mm = nc.tensor.matmul(psA[:, 2 * part + o, 0:D], w[:, m, k, o * P:(o + 1) * P], dft[:, f, k],
                                                  start=(n == 0), stop=(n == 3))
                            n += 1
            mm.then_inc(s_A, 1)
            pe.wait_ge(s_a, 4)
            for o in range(KC):
                n = 0
                for part, f in ((0, 0), (1, 2)):
                    for k in range(KC):
                        mm = nc.tensor.matmul(psY[:, o, 0:D], aT[:, part, k, o * P:(o + 1) * P], dft[:, f, k],
                                              start=(n == 0), stop=(n == 3))
                        n += 1
            mm.then_inc(s_M, 1)
            pe.wait_ge(s_m, 2)

            def turn(s):
                pe.wait_ge(s_ln, s.n + 1)
                after(pe, s_hT, s.n - 1, s, 2)
                for k in range(KC):
                    mm = nc.tensor.transpose(psT[:, s.p, k * P:(k + 1) * P], hn[:, s.p, k * P:(k + 1) * P], c.ident)
                mm.then_inc(s_T, 1)

            def filtered(s):
                pe.wait_ge(s_hT, s.n + 1)
                after(pe, s_yo, s.n - 1, s, 2)
                for k in range(KC):
                    mm = nc.tensor.matmul(psY[:, s.p, 0:D], hT[:, s.p, k], M[:, k], start=(k == 0), stop=(k == KC - 1))
                mm.then_inc(s_y, 1)
            run_pipeline(pe, [(turn, 1), (filtered, 0)])

        @block.scalar
        def _(act):
            act.wait_ge(s_A, 1)
            for i in range(4):
                nc.scalar.activation(aT[:, i // 2, i % 2], psA[:, i, 0:D], ACT.Copy, scale=1.0 / D).then_inc(s_a, 1)
            act.wait_ge(s_M, 1)
            for o in range(KC):
                nc.scalar.activation(M[:, o], psY[:, o, 0:D], ACT.Copy).then_inc(s_m, 1)

            def turned(s):
                act.wait_ge(s_T, s.n + 1)
                after(act, s_y, s.n - 1, s, 2)
                nc.scalar.activation(hT[:, s.p].rearrange("p k t -> p (k t)"), psT[:, s.p, 0:D], ACT.Copy).then_inc(s_hT, 1)
            run_pipeline(act, [(turned, 1)])

        @block.vector
        def _(dve):
            c.wait(dve, "L3f")
            finish_stats(nc, Chain(dve, s_fin), c, 2, 1e-5)

            def rows(s):
                after(dve, s_T, s.n - 1, s, 2)
                normalize(nc, c, hn[:, s.p], seq(c.X, s), s).then_inc(s_ln, 1)

            def add(s):
                dve.wait_ge(s_y, s.n + 1)
                after(dve, s_x, s.n - 1, s, 2)
                nc.vector.tensor_tensor(yo[:, s.p], psY[:, s.p, 0:D], bias, ALU.add).then_inc(s_yo, 1)
                dve.wait_ge(s_yo, s.n + 1)
                nc.vector.scalar_tensor_tensor(seq(c.X, s), yo[:, s.p], c.gates[:, gate:gate + 1], seq(c.X, s),
                                               ALU.mult, ALU.add).then_inc(s_x, 1)
            run_pipeline(dve, [(rows, 1), (add, -1)])



def prepare(nc, c, d):
    with Phase(nc, "start") as ph:
        block = ph.block()

        @block.sync
        def _(sp):
            c.dma(sp, "const", c.consts[:, :], d["consts"])
            c.dma(sp, "const", c.gates[:, :], d["gates"].partition_broadcast(P))
            c.dma(sp, "const", c.gatew[:, :].rearrange("p l k e -> p (l k e)"), d["gatew"])
            c.dma(sp, "const", c.X[:, :, :], d["x"].rearrange("b p d -> p b d"))
            for n in ("L0x", "L0f", "L1x"):
                c.load(sp, n)

        @block.scalar
        def _(act):
            c.wait(act, "const")
            nc.scalar.activation(c.gates[:, :], c.gates[:, :], ACT.Tanh).then_inc(c.s_gate, 1)

        @block.vector
        def _(dve):
            c.wait(dve, "const")
            for b in range(NB):
                nc.vector.bn_stats(c.stats[:, b, 0:6], c.X[:, b, :])
            nc.vector.tensor_copy(c.ident16[:, :], c.ident)
            nc.vector.tensor_copy(c.causal[:, :], c.consts[:, C_CAUSAL:C_CAUSAL + P].unsqueeze(1).broadcast_to([P, 4, P]))


def window_layers(nc, c, Y, gate):
    for layer in range(2):
        name = f"L1f{layer}"
        window_attention(nc, c, Y, layer)
        cols = c.vec1f[:, layer, 0:COLS1F]
        start = layer * L1F + WQKV + WO1
        with nc.sbuf_tensor(f"xT_{name}", [P, KC, NB * S], F32) as xT:
            tokens_in(nc, c, name + "_in", xT, Y, affine=(cols[:, 0:2], cols[:, 2:4], name), shift=True)
            units(nc, c, name + "_units", name, xT, [(start + u * UNIT_GLU, True, None) for u in range(UNITS1)], ACT.Gelu, gate,
                  bias=(cols[:, 4:4 + UNITS1], cols[:, 4 + UNITS1:]), row=c.vec1f[:, layer, COLS1F:COLS1F + D],
                  state=Y, into_x=(layer == 1))


def expert_layer(nc, c, name, gate, plan, which, loads=()):
    scores = nc.dram_tensor(f"scores_{name}", (E, NB * S), F32).ap()
    with nc.sbuf_tensor(f"xT_{name}", [P, KC, NB * S], F32) as xT:
        tokens_in(nc, c, name + "_in", xT, c.X, gate_w=c.gatew[:, which], scores_dram=scores, loads=loads)
        units(nc, c, name + "_units", name, xT, plan, ACT.Silu, gate, scores_dram=scores)


def flamingo_stack(nc, dram, out):
    with ExitStack() as ctx:
        c = Core(nc, ctx, dram)
        prepare(nc, c, dram)
        def loads(*names):
            return [lambda sp, n=n: c.load(sp, n) for n in names]
        heads_attention(nc, c, "L0x", 0, mask=dram["mask"])
        with nc.sbuf_tensor("Y", [P, NB, D], F32) as Y:
            with nc.sbuf_tensor("ctxT", [P, NB, KC, P], F32) as c.ctxT, nc.sbuf_tensor("ctx", [P, NB, D], F32) as c.ctx:
                expert_layer(nc, c, "L0f", 1, [(e * UNIT_GLU, True, e) for e in range(E)], 0, loads("L2x", "ctx"))
                single_attention(nc, c, Y, 2, loads("L1f0", "L1f1"))
            window_layers(nc, c, Y, 3)
        heads_attention(nc, c, "L2x", 4, loads=loads("L2f"))
        shared = [(i * UNIT_GLU, True, None) for i in range(2)]
        routed = [(2 * UNIT_GLU + i * UNIT_ONE, False, i // 2) for i in range(2 * E)]
        expert_layer(nc, c, "L2f", 5, shared + routed, 1, loads("L3x"))
        turn_by_phase(nc, c)
        heads_attention(nc, c, "L3x", 6, loads=loads("L3f"))
        fourier_filter(nc, c, 7, out)



def chunks(w):
    w = np.asarray(w)
    k = w.shape[0] // P
    return w.reshape(k, P, -1).transpose(1, 0, 2).reshape(P, -1)


def columns(v):
    return np.asarray(v).reshape(-1, P).T


def glu_unit(gate, up, down):
    m = P - gate.shape[1]
    return np.concatenate([chunks(np.pad(gate, ((0, 0), (0, m)))), chunks(np.pad(up, ((0, 0), (0, m)))),
                           np.pad(down, ((0, m), (0, 0)))], axis=1)


def constants():
    parity = (np.arange(P)[:, None] // DH % 2 == np.repeat(np.arange(2), P)[None, :])
    shift = np.eye(P, k=1)
    causal = np.where(np.arange(P)[None, :] > np.arange(P)[:, None], -1e30, 0.0)
    half = np.arange(0, LD, 2, dtype=np.float32)
    inv_freq = np.float32(1) / np.float32(10000) ** (half / np.float32(LD))
    t = np.arange(S, dtype=np.float32)
    freqs = t[:, None] * inv_freq[None, :]
    base = (half + np.float32(0.4 * LD)) / np.float32(1.4 * LD)
    scale = base[None, :] ** ((t - S // 2) / np.float32(64))[:, None]
    cos, sin = np.cos(freqs), np.sin(freqs)

    def both(a):
        return np.concatenate([a, a], axis=1)

    def signed(a):
        return np.concatenate([-a, a], axis=1)
    return np.concatenate([np.eye(P), parity, shift, causal, both(cos * scale), both(cos / scale),
                           signed(sin * scale), signed(sin / scale)], axis=1).astype(np.float32)


def layout(i):
    f = {k: np.asarray(v) for k, v in i.items()}
    zero = np.zeros(D, np.float32)

    def heads(q, k, v, o, bq, bk, bv):
        return np.concatenate([chunks(q), chunks(k), chunks(v), chunks(o), columns(bq), columns(bk), columns(bv)], axis=1)
    d = {
        "consts": constants(),
        "x": f["x"],
        "ctxT": f["ctx_1024"].transpose(0, 2, 1).reshape(NB, KC, P, S).transpose(0, 2, 1, 3),
        "ctx": f["ctx_1024"],
        "mask": f["mask_Bx1xSxS2_ik1"][:, 0],
        "gates": np.stack([f["g_xattn"], f["g_ffn"]], axis=1).reshape(8),
        "gatew": np.concatenate([chunks(f["L0_ffn_gate_w"].T), chunks(f["L2_ffn_gate_w"].T)], axis=1),
        "w_L0x": heads(f["L0_xattn_W_q"].T, f["L0_xattn_W_k"].T, f["L0_xattn_W_v"].T, f["L0_xattn_W_o"].T,
                       f["L0_xattn_b_q"], f["L0_xattn_b_k"], f["L0_xattn_b_v"]),
        "row_L0x": f["L0_xattn_b_o"],
        "w_L2x": heads(f["L2_xattn_W_q"], f["L2_xattn_W_kv"][:, :D], f["L2_xattn_W_kv"][:, D:], f["L2_xattn_W_proj"],
                       zero, zero, zero),
        "row_L2x": f["L2_xattn_b_proj"],
        "w_L3x": heads(f["L3_xattn_Wq"].T, f["L3_xattn_Wk"].T, f["L3_xattn_Wv"].T, f["L3_xattn_Wo"].T,
                       f["L3_xattn_bq"], f["L3_xattn_bk"], f["L3_xattn_bv"]),
        "row_L3x": f["L3_xattn_bo"],
        "phase": f["L3_xattn_phase"].reshape(-1),
        "bias_L3x": np.concatenate([f["L3_xattn_bq"], f["L3_xattn_bk"]]),
        "w_L0f": np.concatenate([glu_unit(f["L0_ffn_w1"][e], f["L0_ffn_w3"][e], f["L0_ffn_w2"][e]) for e in range(E)], axis=1),
        "w_L1x": np.concatenate([chunks(f["L1_xattn_W1"]), chunks(f["L1_xattn_W2"])], axis=1),
        "col_L1x": np.concatenate([columns(f["L1_xattn_b1"]), columns(f["L1_xattn_gamma"]), columns(f["L1_xattn_beta"])], axis=1),
        "row_L1x": np.concatenate([f["L1_xattn_gamma"], f["L1_xattn_beta"], f["L1_xattn_b2"]]),
    }
    for n in range(2):
        w1, b1, w2 = f["L1_ffn_w1"][n], f["L1_ffn_b1"][n], f["L1_ffn_w2"][n]
        cuts = [(a, min(a + P, HID)) for a in range(0, HID, P)]
        pad = UNITS1 * P - HID
        d[f"w_L1f{n}"] = np.concatenate(
            [chunks(f["L1_ffn_wqkv"][n]), chunks(f["L1_ffn_wo"][n])]
            + [glu_unit(w1[:, HID + a:HID + b], w1[:, a:b], w2[a:b]) for a, b in cuts], axis=1)
        d[f"col_L1f{n}"] = np.concatenate([columns(f["L1_ffn_ln_g"][n]), columns(f["L1_ffn_ln_b"][n]),
                                           columns(np.pad(b1[HID:], (0, pad))), columns(np.pad(b1[:HID], (0, pad)))], axis=1)
        d[f"row_L1f{n}"] = np.concatenate([f["L1_ffn_b2"][n], f["L1_ffn_q_scale"][n], f["L1_ffn_k_scale"][n]])
    gu, down = f["L2_ffn_shared_gu"].T, f["L2_ffn_shared_down"].T
    units = [glu_unit(gu[:, a:a + P], gu[:, D + a:D + a + P], down[a:a + P]) for a in range(0, D, P)]
    for e in range(E):
        up, down = f["L2_ffn_w1"][e].T, f["L2_ffn_w2"][e].T
        units += [np.concatenate([chunks(up[:, a:a + P]), down[a:a + P]], axis=1) for a in range(0, D, P)]
    d["w_L2f"] = np.concatenate(units, axis=1)
    angle = 2 * np.pi * (np.outer(np.arange(D), np.arange(D)) % D) / D
    cos, sin = np.cos(angle).astype(np.float32), np.sin(angle).astype(np.float32)
    d["dft"] = np.concatenate([chunks(cos), chunks(sin), chunks(-sin)], axis=1)
    d["w_L3f"] = np.concatenate([chunks(f["L3_ffn_w_freq_real"]), chunks(f["L3_ffn_w_freq_imag"])], axis=1)
    d["row_L3f"] = f["L3_ffn_bias"]
    return {k: np.ascontiguousarray(v) for k, v in d.items()}


def kernel(**inputs):
    import concourse.bacc as bacc
    from concourse.bass_utils import run_bass_kernel_spmd

    nc = bacc.Bacc("TRN2", target_bir_lowering=False, num_devices=1)
    arrays = layout(inputs)
    dram = {k: nc.dram_tensor(f"in_{k}", v.shape, mybir.dt.from_np(v.dtype), kind="ExternalInput").ap()
            for k, v in arrays.items()}
    out = nc.dram_tensor("out_x", (NB, S, D), F32, kind="ExternalOutput").ap()
    flamingo_stack(nc, dram, out)
    r = run_bass_kernel_spmd(nc, [{f"in_{k}": v for k, v in arrays.items()}], core_ids=[0])
    return r.results[0]["out_x"]
```
